# Optimizing a Trainium2 kernel written in Bass

```python
import numpy as np
import jax
import jax.numpy as jnp

def _softmax(x, axis=-1):
    return jax.nn.softmax(x, axis=axis)

def _gelu(x):
    return jax.nn.gelu(x, approximate=True)

def _silu(x):
    return jax.nn.silu(x)

def _sigmoid(x):
    return jax.nn.sigmoid(x)

def _layernorm(x, axis=-1, eps=1e-05):
    m = jnp.mean(x, axis=axis, keepdims=True)
    v = jnp.var(x, axis=axis, keepdims=True)
    return (x - m) / jnp.sqrt(v + eps)

def _scatter_add(tgt, idx, src, axis=0):
    return tgt.at[idx].add(src)

def _segment_sum(src, seg, n):
    return jax.ops.segment_sum(src, seg, n)
kernel_name = 'mk_xattn_ffn_d2_seqx_r4_a006cb'

def setup_inputs(seed: int=0):
    np.random.seed(seed)
    _w = jnp.asarray

    def _rec_inputs():
        import jax
        import jax.numpy as jnp
        _rk = jax.random.key(seed)
        x = 7.22e-05 + 1 * jax.random.normal(jax.random.fold_in(_rk, 1), (4, 512, 512), jnp.float32)
        _lenS = 512 - jax.random.randint(jax.random.fold_in(_rk, 7), (4,), 0, max(1, 512 // 4) + 1, jnp.int32)
        _lenS2 = 512 - jax.random.randint(jax.random.fold_in(_rk, 8), (4,), 0, max(1, 512 // 4) + 1, jnp.int32)
        _ctx_1024P = jax.random.normal(jax.random.fold_in(_rk, 11), (4, 16, 256), jnp.float32)
        _ctx_1024c = jax.random.dirichlet(jax.random.fold_in(_rk, 511), 0.3 * jnp.ones((16,), jnp.float32), (4, 512))
        _ctx_1024t = jnp.einsum('bsk,bkd->bsd', _ctx_1024c, _ctx_1024P)
        _ctx_1024t = _ctx_1024t * jax.lax.rsqrt(jnp.mean(jnp.square(_ctx_1024t)) + 1e-12) * 0.953939
        ctx_1024 = 2.81802e-05 + 1.00001 * (_ctx_1024t + 0.3 * jax.random.normal(jax.random.fold_in(_rk, 611), (4, 512, 256), jnp.float32))
        fside_BxSx2_0 = jax.random.uniform(jax.random.fold_in(_rk, 12), (4, 512, 2), jnp.float32, 0.0, 0.999707)
        return (x, ctx_1024, fside_BxSx2_0)
    x, ctx_1024, fside_BxSx2_0 = _rec_inputs()

    def _L0_xattn_setup():
        import jax, jax.numpy as jnp
        import numpy as np
        key = jax.random.key(seed)
        ks = jax.random.split(key, 6)
        B, L, N, C, D = (8, 128, 512, 256, 128)
        return {'teacher_logits': jax.random.normal(ks[0], (B, L, N), dtype=jnp.float32), 'teacher_features': jax.random.normal(ks[1], (B, N, C), dtype=jnp.float32), 'Wq': jax.random.normal(ks[2], (D, C), dtype=jnp.float32) * (1.0 / np.sqrt(C)), 'bq': jnp.zeros((D,), dtype=jnp.float32), 'Wk': jax.random.normal(ks[3], (D, C), dtype=jnp.float32) * (1.0 / np.sqrt(C)), 'bk': jnp.zeros((D,), dtype=jnp.float32)}
    _L0_xattn_all = _L0_xattn_setup()
    _L0_xattn_in = {k: v for k, v in _L0_xattn_all.items() if k in ('Wq', 'bq', 'Wk', 'bk')}
    del _L0_xattn_all

    def _L0_ffn_setup():
        import jax, jax.numpy as jnp
        import numpy as np
        B, T, D = (1, 256, 512)
        F_DIM = 352
        E = 8
        TOPK = 2
        key = jax.random.key(seed)
        ks = jax.random.split(key, 5)
        x = jax.random.normal(ks[0], (B, T, D), dtype=jnp.float32)
        gate_w = jax.random.normal(ks[1], (E, D), dtype=jnp.float32) * 0.02
        gate_proj = jax.random.normal(ks[2], (E, F_DIM, D), dtype=jnp.float32) * 0.02
        up_proj = jax.random.normal(ks[3], (E, F_DIM, D), dtype=jnp.float32) * 0.02
        down_proj = jax.random.normal(ks[4], (E, D, F_DIM), dtype=jnp.float32) * 0.02
        return {'x': x, 'gate_w': gate_w, 'gate_proj': gate_proj, 'up_proj': up_proj, 'down_proj': down_proj}
    _L0_ffn_all = _L0_ffn_setup()
    _L0_ffn_in = {k: v for k, v in _L0_ffn_all.items() if k in ('gate_w', 'gate_proj', 'up_proj', 'down_proj')}
    del _L0_ffn_all

    def _L1_xattn_setup():
        import jax, jax.numpy as jnp
        import numpy as np
        DIM = 512
        CTX_DIM = 256
        N_HEADS = 32
        HEAD_DIM = DIM // N_HEADS
        POS_DIM = 2
        B, N, CTXN = (2, 512, 512)
        ROPE_BASE = 10000.0

        def apply_axial_rope(x, pos):
            b, n, h, d = x.shape
            p = pos.shape[-1]
            dpa = d // p
            half = dpa // 2
            freqs = ROPE_BASE ** (-jnp.arange(half, dtype=x.dtype) / half)
            ang = pos[..., :, None] * freqs
            cos = jnp.cos(ang)[:, :, None, :, :]
            sin = jnp.sin(ang)[:, :, None, :, :]
            xr = x.reshape(b, n, h, p, half, 2)
            x1, x2 = (xr[..., 0], xr[..., 1])
            out = jnp.stack([x1 * cos - x2 * sin, x1 * sin + x2 * cos], axis=-1)
            return out.reshape(b, n, h, d)
        key = jax.random.key(seed)
        ks = jax.random.split(key, 8)
        x = jax.random.normal(ks[0], (B, N, DIM), jnp.float32)
        ctx = jax.random.normal(ks[1], (B, CTXN, CTX_DIM), jnp.float32)
        pos_map = jax.random.uniform(ks[2], (B, N, POS_DIM), jnp.float32)
        ctx_pos_map = jax.random.uniform(ks[3], (B, CTXN, POS_DIM), jnp.float32)
        Wq = jax.random.normal(ks[4], (DIM, DIM), jnp.float32) / np.sqrt(DIM)
        Wkv = jax.random.normal(ks[5], (CTX_DIM, 2 * DIM), jnp.float32) / np.sqrt(CTX_DIM)
        Wout = jax.random.normal(ks[6], (DIM, DIM), jnp.float32) / np.sqrt(DIM)
        bout = jnp.zeros((DIM,), jnp.float32)
        return {'x': x, 'ctx': ctx, 'pos_map': pos_map, 'ctx_pos_map': ctx_pos_map, 'Wq': Wq, 'Wkv': Wkv, 'Wout': Wout, 'bout': bout}
    _L1_xattn_all = _L1_xattn_setup()
    _L1_xattn_in = {k: v for k, v in _L1_xattn_all.items() if k in ('Wq', 'Wkv', 'Wout', 'bout')}
    del _L1_xattn_all

    def _L1_ffn_setup():
        import jax, jax.numpy as jnp
        import numpy as np
        B, S, D = (4, 512, 512)
        DFF = 1408
        E, K, R = (8, 2, 16)
        SCALING = 32.0 / 16.0
        key = jax.random.key(seed)
        ks = jax.random.split(key, 12)
        s = lambda k, shape, scale: jax.random.normal(k, shape, dtype=jnp.float32) * scale
        return {'x': s(ks[0], (B, S, D), 1.0), 'Wg': s(ks[1], (DFF, D), 0.02), 'Wu': s(ks[2], (DFF, D), 0.02), 'Wd': s(ks[3], (D, DFF), 0.02), 'Wr': s(ks[4], (E, D), 0.02), 'Ag': s(ks[5], (E, R, D), 0.02), 'Bg': s(ks[6], (E, DFF, R), 0.02), 'Au': s(ks[7], (E, R, D), 0.02), 'Bu': s(ks[8], (E, DFF, R), 0.02), 'Ad': s(ks[9], (E, R, DFF), 0.02), 'Bd': s(ks[10], (E, D, R), 0.02)}
    _L1_ffn_all = _L1_ffn_setup()
    _L1_ffn_in = {k: v for k, v in _L1_ffn_all.items() if k in ('Wg', 'Wu', 'Wd', 'Wr', 'Ag', 'Bg', 'Au', 'Bu', 'Ad', 'Bd')}
    del _L1_ffn_all
    return {'x': x, 'ctx_1024': ctx_1024, 'fside_BxSx2_0': fside_BxSx2_0, 'L0_xattn_Wq': _L0_xattn_in['Wq'], 'L0_xattn_bq': _L0_xattn_in['bq'], 'L0_xattn_Wk': _L0_xattn_in['Wk'], 'L0_xattn_bk': _L0_xattn_in['bk'], 'L0_ffn_gate_w': _L0_ffn_in['gate_w'], 'L0_ffn_gate_proj': _L0_ffn_in['gate_proj'], 'L0_ffn_up_proj': _L0_ffn_in['up_proj'], 'L0_ffn_down_proj': _L0_ffn_in['down_proj'], 'L1_xattn_Wq': _L1_xattn_in['Wq'], 'L1_xattn_Wkv': _L1_xattn_in['Wkv'], 'L1_xattn_Wout': _L1_xattn_in['Wout'], 'L1_xattn_bout': _L1_xattn_in['bout'], 'L1_ffn_Wg': _L1_ffn_in['Wg'], 'L1_ffn_Wu': _L1_ffn_in['Wu'], 'L1_ffn_Wd': _L1_ffn_in['Wd'], 'L1_ffn_Wr': _L1_ffn_in['Wr'], 'L1_ffn_Ag': _L1_ffn_in['Ag'], 'L1_ffn_Bg': _L1_ffn_in['Bg'], 'L1_ffn_Au': _L1_ffn_in['Au'], 'L1_ffn_Bu': _L1_ffn_in['Bu'], 'L1_ffn_Ad': _L1_ffn_in['Ad'], 'L1_ffn_Bd': _L1_ffn_in['Bd']}

def reference(x, ctx_1024, fside_BxSx2_0, L0_xattn_Wq, L0_xattn_bq, L0_xattn_Wk, L0_xattn_bk, L0_ffn_gate_w, L0_ffn_gate_proj, L0_ffn_up_proj, L0_ffn_down_proj, L1_xattn_Wq, L1_xattn_Wkv, L1_xattn_Wout, L1_xattn_bout, L1_ffn_Wg, L1_ffn_Wu, L1_ffn_Wd, L1_ffn_Wr, L1_ffn_Ag, L1_ffn_Bg, L1_ffn_Au, L1_ffn_Bu, L1_ffn_Ad, L1_ffn_Bd):
    import jax
    import jax.numpy as jnp

    def _L0_xattn_ref(teacher_logits, teacher_features, Wq, bq, Wk, bk):
        import jax, jax.numpy as jnp
        import numpy as np
        query = jnp.einsum('bnc,dc->bnd', teacher_features, Wq) + bq
        key = jnp.einsum('bnc,dc->bnd', teacher_features, Wk) + bk
        energy = jnp.einsum('bnd,bmd->bnm', query, key)
        attention = jax.nn.softmax(energy, axis=-1)
        x_m = jnp.einsum('bln,bmn->blm', teacher_logits, attention)
        return x_m

    def _L0_ffn_ref(x, gate_w, gate_proj, up_proj, down_proj):
        import jax, jax.numpy as jnp
        import numpy as np
        B, T, D = (1, 256, 512)
        F_DIM = 352
        E = 8
        TOPK = 2
        b, t, d = x.shape
        x_flat = x.reshape(-1, d)
        n = x_flat.shape[0]
        router_logits = x_flat @ gate_w.T
        top_w, sel = jax.lax.top_k(router_logits, TOPK)
        top_w = jax.nn.softmax(top_w, axis=-1)
        tok_ids = jnp.arange(n)[:, None]
        tw = jnp.zeros((n, E), dtype=x.dtype).at[tok_ids, sel].add(top_w)
        g = jnp.einsum('nd,efd->enf', x_flat, gate_proj)
        u = jnp.einsum('nd,efd->enf', x_flat, up_proj)
        h = jax.nn.silu(g) * u
        eo = jnp.einsum('enf,edf->end', h, down_proj)
        out = jnp.einsum('end,ne->nd', eo, tw)
        return out.reshape(b, t, d)

    def _L1_xattn_ref(x, ctx, pos_map, ctx_pos_map, Wq, Wkv, Wout, bout):
        import jax, jax.numpy as jnp
        import numpy as np
        DIM = 512
        CTX_DIM = 256
        N_HEADS = 32
        HEAD_DIM = DIM // N_HEADS
        POS_DIM = 2
        B, N, CTXN = (2, 512, 512)
        ROPE_BASE = 10000.0

        def apply_axial_rope(x, pos):
            b, n, h, d = x.shape
            p = pos.shape[-1]
            dpa = d // p
            half = dpa // 2
            freqs = ROPE_BASE ** (-jnp.arange(half, dtype=x.dtype) / half)
            ang = pos[..., :, None] * freqs
            cos = jnp.cos(ang)[:, :, None, :, :]
            sin = jnp.sin(ang)[:, :, None, :, :]
            xr = x.reshape(b, n, h, p, half, 2)
            x1, x2 = (xr[..., 0], xr[..., 1])
            out = jnp.stack([x1 * cos - x2 * sin, x1 * sin + x2 * cos], axis=-1)
            return out.reshape(b, n, h, d)
        b, n, _ = x.shape
        ctx_n = ctx.shape[1]
        q = (x @ Wq).reshape(b, n, N_HEADS, HEAD_DIM)
        k, v = jnp.split(ctx @ Wkv, 2, axis=-1)
        k = k.reshape(b, ctx_n, N_HEADS, HEAD_DIM)
        v = v.reshape(b, ctx_n, N_HEADS, HEAD_DIM)
        q = apply_axial_rope(q, pos_map)
        k = apply_axial_rope(k, ctx_pos_map)
        scale = 1.0 / np.sqrt(HEAD_DIM).astype(np.float32)
        logits = jnp.einsum('bqhd,bkhd->bhqk', q, k) * scale
        w = jax.nn.softmax(logits, axis=-1)
        attn = jnp.einsum('bhqk,bkhd->bqhd', w, v)
        attn = attn.reshape(b, n, N_HEADS * HEAD_DIM)
        return attn @ Wout + bout

    def _L1_ffn_ref(x, Wg, Wu, Wd, Wr, Ag, Bg, Au, Bu, Ad, Bd):
        import jax, jax.numpy as jnp
        import numpy as np
        B, S, D = (4, 512, 512)
        DFF = 1408
        E, K, R = (8, 2, 16)
        SCALING = 32.0 / 16.0
        b, s, d = x.shape
        xf = x.reshape(-1, d)
        gate_base = xf @ Wg.T
        up_base = xf @ Wu.T
        base_out = jax.nn.silu(gate_base) * up_base @ Wd.T
        router_logits = xf @ Wr.T
        probs = jax.nn.softmax(router_logits.astype(jnp.float32), axis=-1)
        topw, topi = jax.lax.top_k(probs, K)
        topw = topw.astype(x.dtype)
        expert_w = jnp.sum(jax.nn.one_hot(topi, E, dtype=x.dtype) * topw[..., None], axis=1)

        def expert_step(acc, params):
            Ag_e, Bg_e, Au_e, Bu_e, Ad_e, Bd_e, we = params
            g_lora = xf @ Ag_e.T @ Bg_e.T * SCALING
            u_lora = xf @ Au_e.T @ Bu_e.T * SCALING
            h = jax.nn.silu(gate_base + g_lora) * (up_base + u_lora)
            d_delta = h @ Ad_e.T @ Bd_e.T * SCALING
            return (acc + d_delta * we[:, None], None)
        acc0 = jnp.zeros_like(base_out)
        acc, _ = jax.lax.scan(expert_step, acc0, (Ag, Bg, Au, Bu, Ad, Bd, expert_w.T))
        return (base_out + acc).reshape(b, s, d)
    x = x + _L0_xattn_ref(_layernorm(x, axis=-1), ctx_1024, L0_xattn_Wq, L0_xattn_bq, L0_xattn_Wk, L0_xattn_bk)
    x = x + _L0_ffn_ref(_layernorm(x, axis=-1), L0_ffn_gate_w, L0_ffn_gate_proj, L0_ffn_up_proj, L0_ffn_down_proj)
    x = x + _L1_xattn_ref(_layernorm(x, axis=-1), ctx_1024, fside_BxSx2_0, fside_BxSx2_0, L1_xattn_Wq, L1_xattn_Wkv, L1_xattn_Wout, L1_xattn_bout)
    x = x + _L1_ffn_ref(_layernorm(x, axis=-1), L1_ffn_Wg, L1_ffn_Wu, L1_ffn_Wd, L1_ffn_Wr, L1_ffn_Ag, L1_ffn_Bg, L1_ffn_Au, L1_ffn_Bu, L1_ffn_Ad, L1_ffn_Bd)
    return x

_drawn_inputs = setup_inputs


def setup_inputs(seed=0):
    import zlib

    import numpy as np

    out = dict(_drawn_inputs(seed))
    spreads = {'L0_xattn_bq': (0.0, 0.1), 'L0_xattn_bk': (0.0, 2.0), 'L1_xattn_bout': (0.0, 0.1)}
    factors = {'L0_ffn_gate_w': 3.064,
     'L0_ffn_gate_proj': 2.669,
     'L1_ffn_Wr': 8.0,
     'L1_ffn_Ag': 8.0,
     'L1_ffn_Bg': 8.0,
     'L1_ffn_Au': 8.0,
     'L1_ffn_Bu': 8.0,
     'L1_ffn_Ad': 8.0,
     'L1_ffn_Bd': 8.0,
     'L1_ffn_Wd': 52.439}
    for name, (base, spread) in spreads.items():
        noise = np.random.default_rng([zlib.crc32(name.encode()), seed]).standard_normal(out[name].shape)
        drawn = base * np.exp(spread * noise) if base else spread * noise
        out[name] = jnp.asarray(drawn.astype(out[name].dtype))
    for name, factor in factors.items():
        out[name] = (out[name] * factor).astype(out[name].dtype)
    return out
```

```python
import numpy as np

import concourse.bass as bass
from concourse import mybir

FP32 = mybir.dt.float32
FP32R = mybir.dt.float32r
ALU = mybir.AluOpType
ACT = mybir.ActivationFunctionType
AXIS_X = mybir.AxisListType.X

P = 128
B, S, D = 4, 512, 512
TOKENS = B * S
TILES = TOKENS // P
TPB = S // P
DK = D // P
CTX = 256
CK = CTX // P
QK0 = 128
EPS = 1e-5
DMA = 16

E0, F0 = 8, 352
FW0 = [128, 128, 96]
E1, R1, DFF = 8, 16, 1408
SCALING1 = 2.0

HEADS, HD = 32, 16
ROPE_BASE = 10000.0
HI, LO = 0, 1


def ds(start, size):
    return bass.ds(start, size)


def fp32(ap):
    return ap.bitcast(FP32)


def product(nc, out, pairs):
    passes = [(l[a], r[b]) for l, r in pairs for a, b in ((HI, HI), (HI, LO), (LO, HI))]
    last = None
    for i, (l, r) in enumerate(passes):
        last = nc.tensor.matmul(out, l, r, start=(i == 0), stop=(i == len(passes) - 1))
    return last


def add_product(nc, out, l, r):
    last = None
    for a, b in ((HI, HI), (HI, LO), (LO, HI)):
        last = nc.tensor.matmul(out, l[a], r[b], start=False, stop=True, skip_group_check=True)
    return last


class Norm:

    def __init__(self, nc, ctx, tag, xn=None):
        sb = lambda name, shape: ctx.enter_context(nc.sbuf_tensor(f"{tag}_{name}", shape, FP32))
        self.stats = sb("stats", [P, TPB, 6])
        self.moments = sb("moments", [P, TPB, 2])
        self.var = sb("var", [P, TPB])
        self.std = sb("std", [P, TPB])
        self.rstd = sb("rstd", [P, TPB])
        self.xn = sb("xn", [P, TPB, D]) if xn is None else xn
        sem = lambda name: ctx.enter_context(nc.semaphore(f"{tag}_{name}"))
        self.var_ready = sem("var_ready")
        self.std_ready = sem("std_ready")
        self.xn_ready = sem("xn_ready")


def norm_vector(nc, dve, n, it, x_tile):
    for t in range(TPB):
        nc.vector.bn_stats(n.stats[:, t, :], x_tile(t))
    nc.vector.drain()
    for t in range(TPB):
        nc.vector.bn_aggr(n.moments[:, t, :], n.stats[:, t, :])
    nc.vector.drain()
    nc.vector.tensor_scalar_add(n.var[:], n.moments[:, :, 1], EPS).then_inc(n.var_ready, 1)
    dve.wait_ge(n.std_ready, it + 1)
    nc.vector.reciprocal(n.rstd[:], n.std[:])
    nc.vector.drain()
    for t in range(TPB):
        nc.vector.tensor_scalar(n.xn[:, t, :], x_tile(t), n.moments[:, t, 0:1], n.rstd[:, t:t + 1],
                                ALU.subtract, ALU.mult).then_inc(n.xn_ready, 1)


def norm_scalar(nc, act, n, it):
    act.wait_ge(n.var_ready, it + 1)
    nc.scalar.activation(n.std[:], n.var[:], ACT.Sqrt).then_inc(n.std_ready, 1)


class Split:

    def __init__(self, nc, ctx, tag):
        sem = lambda name: ctx.enter_context(nc.semaphore(f"{tag}_{name}"))
        self.filled = sem("filled")
        self.hi_done = sem("hi_done")
        self.split = sem("split")


def split_hi(nc, act, s, job, hi, psum):
    act.wait_ge(s.filled, job + 1)
    nc.scalar.activation(hi, psum, ACT.Copy).then_inc(s.hi_done, 1)


def split_lo(nc, dve, s, job, lo, psum, hi):
    dve.wait_ge(s.hi_done, job + 1)
    nc.vector.tensor_tensor(lo, psum, fp32(hi), ALU.subtract).then_inc(s.split, 1)


def transposes(nc, s, bank, ins, ident):
    last = None
    at = 0
    for a in ins:
        rows, cols = a.shape[0], a.shape[1]
        last = nc.tensor.transpose(bank[0:cols, at:at + rows], a, ident[0:rows, 0:rows])
        at += rows
    last.then_inc(s.filled, 1)


def phase_attention0(nc, io, x, ident):
    from contextlib import ExitStack
    x_dram = io["x"].rearrange("b (t p) d -> p (b t) d", p=P)
    ctx_dram = io["ctx_1024"].rearrange("b (t p) c -> p (b t) c", p=P)
    with ExitStack() as ctx:
        def sb(name, shape, dt=FP32):
            return ctx.enter_context(nc.sbuf_tensor(f"a0_{name}", shape, dt))

        def ps(name, shape):
            return ctx.enter_context(nc.psum_tensor(f"a0_{name}", shape, FP32))

        def sem(name):
            return ctx.enter_context(nc.semaphore(f"a0_{name}"))

        wq_raw = sb("wq_raw", [P, CTX])
        wk_raw = sb("wk_raw", [P, CTX])
        bias = sb("bias", [P, 2])
        wT = sb("wT", [P, 2, 2, CK, P], FP32R)
        ctx_raw = sb("ctx_raw", [P, TPB, CTX])
        ctxT = sb("ctxT", [P, 2, CK, S], FP32R)
        xnT = sb("xnT", [P, 2, DK, S], FP32R)
        qkT = sb("qkT", [P, 2, 2, S], FP32R)
        att = sb("att", [P, TPB, S])
        attT = sb("attT", [P, 2, DK, S], FP32R)
        rowmax = sb("rowmax", [P, TPB])
        negmax = sb("negmax", [P, TPB])
        rowsum = sb("rowsum", [P, TPB])
        rinv = sb("rinv", [P, TPB])
        n = Norm(nc, ctx, "a0n")
        tp = [ps(f"tp{i}", [P, S]) for i in range(2)]
        mm = [ps(f"mm{i}", [P, S]) for i in range(2)]
        en = [ps(f"en{i}", [P, S]) for i in range(TPB)]
        t_ = Split(nc, ctx, "a0t")
        qk_ = Split(nc, ctx, "a0qk")
        w_in, x_in, ctx_in = sem("w_in"), sem("x_in"), sem("ctx_in")
        energy_ready, negmax_ready, exp_ready, att_ready = (
            sem("energy_ready"), sem("negmax_ready"), sem("exp_ready"), sem("att_ready"))
        mix_ready, x_added = sem("mix_ready"), sem("x_added")
        ident_ready = sem("ident_ready")
        W_JOBS, JOBS = 1, CK + 2 * TPB
        block = ctx.enter_context(nc.Block())

        @block.gpsimd
        def _(pool):
            nc.gpsimd.memset(ident[:], 0.0).then_inc(ident_ready, 1)
            pool.wait_ge(ident_ready, 1)
            nc.gpsimd.affine_select(out=ident[:], in_=ident[:], compare_op=ALU.not_equal, fill=1.0, base=0,
                                    pattern=[[-1, P]], channel_multiplier=1).then_inc(ident_ready, 1)

        @block.sync
        def _(sp):
            sp.dma_start(wq_raw[:], io["L0_xattn_Wq"]).then_inc(w_in, DMA)
            sp.dma_start(wk_raw[:], io["L0_xattn_Wk"]).then_inc(w_in, DMA)
            sp.dma_start(bias[:, 0:1], io["L0_xattn_bq"].rearrange("(p a) -> p a", a=1)).then_inc(w_in, DMA)
            sp.dma_start(bias[:, 1:2], io["L0_xattn_bk"].rearrange("(p a) -> p a", a=1)).then_inc(w_in, DMA)
            with sp.Fori(0, B) as b:
                sp.wait_ge(x_in, DMA * b)
                sp.dma_start(x[:, ds(b * TPB, TPB), :], x_dram[:, ds(b * TPB, TPB), :]).then_inc(x_in, DMA)
                sp.wait_ge(t_.filled, b * JOBS)
                sp.dma_start(ctx_raw[:], ctx_dram[:, ds(b * TPB, TPB), :]).then_inc(ctx_in, DMA)

        @block.tensor
        def _(pe):
            pe.wait_ge(ident_ready, 2)
            pe.wait_ge(w_in, 4 * DMA)
            transposes(nc, t_, tp[0], [w[:, k * P:(k + 1) * P] for w in (wq_raw, wk_raw) for k in range(CK)], ident)
            with pe.Fori(0, B) as b:
                job = W_JOBS + b * JOBS
                pe.wait_ge(ctx_in, DMA * (b + 1))
                for k in range(CK):
                    pe.wait_ge(t_.split, job + k)
                    transposes(nc, t_, tp[(W_JOBS + k) % 2], [ctx_raw[:, t, k * P:(k + 1) * P] for t in range(TPB)], ident)
                for t in range(TPB):
                    pe.wait_ge(n.xn_ready, b * TPB + t + 1)
                    pe.wait_ge(t_.split, job + CK + t)
                    transposes(nc, t_, tp[(W_JOBS + CK + t) % 2], [n.xn[:, t, k * P:(k + 1) * P] for k in range(DK)], ident)
                pe.wait_ge(t_.split, job + CK + 1)
                pe.wait_ge(x_added, b * TPB)
                for i in range(2):
                    product(nc, mm[i][:], [([wT[:, h, i, k, :] for h in (HI, LO)],
                                            [ctxT[:, h, k, :] for h in (HI, LO)]) for k in range(CK)]
                            ).then_inc(qk_.filled, 1)
                pe.wait_ge(qk_.split, 2 * b + 2)
                for m in range(TPB):
                    product(nc, en[m][:], [([qkT[:, h, 0, m * P:(m + 1) * P] for h in (HI, LO)],
                                            [qkT[:, h, 1, :] for h in (HI, LO)])]).then_inc(energy_ready, 1)
                for m in range(TPB):
                    pe.wait_ge(att_ready, b * TPB + m + 1)
                    pe.wait_ge(t_.split, job + CK + TPB + m)
                    transposes(nc, t_, tp[(W_JOBS + CK + TPB + m) % 2], [att[:, m, k * P:(k + 1) * P] for k in range(DK)], ident)
                pe.wait_ge(t_.split, job + JOBS + 1)
                for t in range(TPB):
                    if t >= 2:
                        pe.wait_ge(x_added, b * TPB + t - 1)
                    product(nc, mm[t % 2][:], [([xnT[:, h, k, t * P:(t + 1) * P] for h in (HI, LO)],
                                                [attT[:, h, k, :] for h in (HI, LO)]) for k in range(DK)]
                            ).then_inc(mix_ready, 1)

        @block.scalar
        def _(act):
            split_hi(nc, act, t_, 0, wT[:, HI].rearrange("p a k c -> p (a k c)"), tp[0][:])
            with act.Fori(0, B) as b:
                job = W_JOBS + b * JOBS
                for k in range(CK):
                    split_hi(nc, act, t_, job + k, ctxT[:, HI, k, :], tp[(W_JOBS + k) % 2][:])
                norm_scalar(nc, act, n, b)
                for t in range(TPB):
                    split_hi(nc, act, t_, job + CK + t, xnT[:, HI, :, t * P:(t + 1) * P],
                             tp[(W_JOBS + CK + t) % 2][:].rearrange("p (k c) -> p k c", k=DK))
                for i in range(2):
                    act.wait_ge(qk_.filled, 2 * b + i + 1)
                    nc.scalar.activation(qkT[:, HI, i, :], mm[i][:], ACT.Identity,
                                         bias=bias[:, i:i + 1]).then_inc(qk_.hi_done, 1)
                for m in range(TPB):
                    act.wait_ge(negmax_ready, b * TPB + m + 1)
                    nc.scalar.activation(att[:, m, :], en[m][:], ACT.Exp, bias=negmax[:, m:m + 1],
                                         accum_out=rowsum[:, m:m + 1]).then_inc(exp_ready, 1)
                for m in range(TPB):
                    split_hi(nc, act, t_, job + CK + TPB + m, attT[:, HI, :, m * P:(m + 1) * P],
                             tp[(W_JOBS + CK + TPB + m) % 2][:].rearrange("p (k c) -> p k c", k=DK))

        @block.vector
        def _(dve):
            dve.sem_inc(t_.split, 1)
            split_lo(nc, dve, t_, 0, wT[:, LO].rearrange("p a k c -> p (a k c)"), tp[0][:],
                     wT[:, HI].rearrange("p a k c -> p (a k c)"))
            with dve.Fori(0, B) as b:
                job = W_JOBS + b * JOBS
                for k in range(CK):
                    split_lo(nc, dve, t_, job + k, ctxT[:, LO, k, :], tp[(W_JOBS + k) % 2][:], ctxT[:, HI, k, :])
                dve.wait_ge(x_in, DMA * (b + 1))
                norm_vector(nc, dve, n, b, lambda t: x[:, ds(b * TPB + t, 1), :])
                for t in range(TPB):
                    split_lo(nc, dve, t_, job + CK + t, xnT[:, LO, :, t * P:(t + 1) * P],
                             tp[(W_JOBS + CK + t) % 2][:].rearrange("p (k c) -> p k c", k=DK),
                             xnT[:, HI, :, t * P:(t + 1) * P])
                for i in range(2):
                    dve.wait_ge(qk_.hi_done, 2 * b + i + 1)
                    nc.vector.scalar_tensor_tensor(out=qkT[:, LO, i, :], in0=mm[i][:], scalar=bias[:, i:i + 1],
                                                   in1=fp32(qkT[:, HI, i, :]), op0=ALU.add,
                                                   op1=ALU.subtract).then_inc(qk_.split, 1)
                for m in range(TPB):
                    dve.wait_ge(energy_ready, b * TPB + m + 1)
                    nc.vector.reduce_max(rowmax[:, m:m + 1], en[m][:], AXIS_X)
                    nc.vector.drain()
                    nc.vector.tensor_scalar(negmax[:, m:m + 1], rowmax[:, m:m + 1], -1.0, None,
                                            ALU.mult).then_inc(negmax_ready, 1)
                for m in range(TPB):
                    dve.wait_ge(exp_ready, b * TPB + m + 1)
                    nc.vector.reciprocal(rinv[:, m:m + 1], rowsum[:, m:m + 1])
                    nc.vector.drain()
                    nc.vector.tensor_scalar(att[:, m, :], att[:, m, :], rinv[:, m:m + 1], None,
                                            ALU.mult).then_inc(att_ready, 1)
                    if m >= 1:
                        lo_att(nc, dve, t_, job, m - 1, attT, tp)
                lo_att(nc, dve, t_, job, TPB - 1, attT, tp)
                for t in range(TPB):
                    dve.wait_ge(mix_ready, b * TPB + t + 1)
                    nc.vector.tensor_tensor(x[:, ds(b * TPB + t, 1), :], mm[t % 2][:].rearrange("p (a c) -> p a c", a=1), x[:, ds(b * TPB + t, 1), :],
                                            ALU.add).then_inc(x_added, 1)


def lo_att(nc, dve, s, job, m, attT, tp):
    split_lo(nc, dve, s, job + CK + TPB + m, attT[:, LO, :, m * P:(m + 1) * P],
             tp[(1 + CK + TPB + m) % 2][:].rearrange("p (k c) -> p k c", k=DK), attT[:, HI, :, m * P:(m + 1) * P])


def top_two(nc, dve, logits, rev, t):
    def wide(a):
        return a[:].unsqueeze(2).to_broadcast(list(logits.shape))

    for source, top, hot in ((logits, t.top1, t.hot1), (t.rest, t.top2, t.hot2)):
        nc.vector.reduce_max(top[:], source[:], AXIS_X)
        nc.vector.drain()
        nc.vector.tensor_tensor(t.score[:], source[:], wide(top), ALU.is_equal)
        nc.vector.drain()
        nc.vector.tensor_tensor(t.score[:], t.score[:], rev[:], ALU.mult)
        nc.vector.drain()
        nc.vector.reduce_max(t.best[:], t.score[:], AXIS_X)
        nc.vector.drain()
        nc.vector.tensor_tensor(hot[:], t.score[:], wide(t.best), ALU.is_equal)
        nc.vector.drain()
        if source is logits:
            nc.vector.scalar_tensor_tensor(out=t.rest[:], in0=hot[:], scalar=-3e38, in1=logits[:],
                                           op0=ALU.mult, op1=ALU.add)
            nc.vector.drain()


class TopTwo:
    def __init__(self, nc, ctx, tag, tiles, experts):
        def sb(name, shape):
            return ctx.enter_context(nc.sbuf_tensor(f"{tag}_{name}", shape, FP32))
        self.score, self.rest, self.hot1, self.hot2 = (
            sb(name, [P, tiles, experts]) for name in ("score", "rest", "hot1", "hot2"))
        self.top1, self.top2, self.best, self.gap, self.e, self.w1, self.w2, self.den = (
            sb(name, [P, tiles]) for name in ("top1", "top2", "best", "gap", "e", "w1", "w2", "den"))


def phase_moe0(nc, io, x, ident):
    from contextlib import ExitStack
    gate_dram, up_dram, down_dram = io["L0_ffn_gate_proj"], io["L0_ffn_up_proj"], io["L0_ffn_down_proj"]
    NF = len(FW0)
    NB = B
    STEPS = NF * NB
    PREP = 3
    JOBS = NF * PREP
    with ExitStack() as ctx:
        def sb(name, shape, dt=FP32):
            return ctx.enter_context(nc.sbuf_tensor(f"m_{name}", shape, dt))

        def ps(name, shape):
            return ctx.enter_context(nc.psum_tensor(f"m_{name}", shape, FP32))

        def sem(name):
            return ctx.enter_context(nc.semaphore(f"m_{name}"))

        xnT = sb("xnT", [P, 2, DK, TOKENS], FP32R)
        gw_raw = sb("gw_raw", [E0, D])
        gwT = sb("gwT", [P, 2, DK, E0], FP32R)
        rl = sb("rl", [P, S])
        logits = sb("logits", [P, TILES, E0])
        rev = sb("rev", [P, TILES, E0])
        weight = sb("weight", [P, TILES, E0])
        gate_raw = [sb(f"gate_raw{j}", [P, D]) for j in range(NF)]
        up_raw = [sb(f"up_raw{j}", [P, D]) for j in range(NF)]
        down_raw = [sb(f"down_raw{j}", [P, DK, P]) for j in range(NF)]
        gateT = [sb(f"gateT{j}", [P, 2, DK, P], FP32R) for j in range(NF)]
        upT = [sb(f"upT{j}", [P, 2, DK, P], FP32R) for j in range(NF)]
        downT = [sb(f"downT{j}", [P, 2, D], FP32R) for j in range(NF)]
        silu = [sb(f"silu{i}", [P, S]) for i in range(2)]
        hid = [sb(f"hid{i}", [P, S]) for i in range(2)]
        hidS = [sb(f"hidS{i}", [P, 2, S], FP32R) for i in range(2)]
        n = Norm(nc, ctx, "mn")
        t = TopTwo(nc, ctx, "mt", TILES, E0)
        g_ps = [ps(f"g{i}", [P, S]) for i in range(2)]
        u_ps = [ps(f"u{i}", [P, S]) for i in range(2)]
        y_ps = [ps(f"y{i}", [P, D]) for i in range(3)]
        prep_ps = ps("prep", [P, D])
        prep_ = Split(nc, ctx, "mp")
        xt_ = Split(nc, ctx, "mx")
        gw_in = sem("gw_in")
        raw_in = [sem(f"raw_in{j}") for j in range(NF)]
        router_ready, router_copied, logits_ready, logits_done = (
            sem("router_ready"), sem("router_copied"), sem("logits_ready"), sem("logits_done"))
        gap_ready, gap_exp, rl_clear = sem("gap_ready"), sem("gap_exp"), sem("rl_clear")
        gate_ready, up_ready, silu_done, hid_done, hid_hi, hid_split = (
            sem("gate_ready"), sem("up_ready"), sem("silu_done"), sem("hid_done"), sem("hid_hi"), sem("hid_split"))
        y_ready, y_added = sem("y_ready"), sem("y_added")
        block = ctx.enter_context(nc.Block())

        def prep_views(j, part):
            f = FW0[j]
            if part < 2:
                raw, to = ((gate_raw, gateT), (up_raw, upT))[part]
                return ([raw[j][0:f, k * P:(k + 1) * P] for k in range(DK)],
                        prep_ps[:, 0:DK * f].rearrange("p (k c) -> p k c", k=DK),
                        [to[j][:, h, :, 0:f] for h in (HI, LO)])
            return ([down_raw[j][:, k, 0:f] for k in range(DK)], prep_ps[0:f, :],
                    [downT[j][0:f, h, :] for h in (HI, LO)])

        def prep_job(e, j, c):
            return 2 * PREP + e * JOBS + j * PREP + c, (j + 2) % NF

        @block.sync
        def _(sp):
            def load(e, j):
                f0, f = sum(FW0[:j]), FW0[j]
                sp.dma_start(gate_raw[j][0:f, :], gate_dram[ds(e, 1), f0:f0 + f, :].rearrange("e f d -> (e f) d")).then_inc(raw_in[j], DMA)
                sp.dma_start(up_raw[j][0:f, :], up_dram[ds(e, 1), f0:f0 + f, :].rearrange("e f d -> (e f) d")).then_inc(raw_in[j], DMA)
                sp.dma_start(down_raw[j][:, :, 0:f], down_dram[ds(e, 1), :, f0:f0 + f]
                             .rearrange("e (k p) f -> p (e k) f", p=P)).then_inc(raw_in[j], DMA)

            sp.dma_start(gw_raw[:], io["L0_ffn_gate_w"]).then_inc(gw_in, DMA)
            for j in range(NF):
                load(0, j)
            with sp.Fori(1, E0) as e:
                for j in range(NF):
                    sp.wait_ge(prep_.filled, (e - 1) * JOBS + (j + 1) * PREP)
                    load(e, j)

        @block.tensor
        def _(pe):
            def prep(job, j, part):
                pe.wait_ge(prep_.split, job)
                transposes(nc, prep_, prep_ps, prep_views(j, part)[0], ident)

            pe.wait_ge(gw_in, DMA)
            transposes(nc, xt_, y_ps[0], [gw_raw[:, k * P:(k + 1) * P] for k in range(DK)], ident)
            for j in range(2):
                pe.wait_ge(raw_in[j], 3 * DMA)
                for part in range(PREP):
                    prep(j * PREP + part, j, part)
            with pe.Fori(0, NB) as b:
                for k in range(TPB):
                    pe.wait_ge(n.xn_ready, b * TPB + k + 1)
                    pe.wait_ge(xt_.split, b * TPB + k + 1)
                    transposes(nc, xt_, y_ps[(k + 1) % 2], [n.xn[:, k, i * P:(i + 1) * P] for i in range(DK)], ident)
                pe.wait_ge(xt_.split, b * TPB + TPB + 2)
                pe.wait_ge(router_copied, b)
                product(nc, g_ps[0][0:E0, :], [([gwT[:, h, k, :] for h in (HI, LO)],
                                               [xnT[:, h, k, ds(b * S, S)] for h in (HI, LO)]) for k in range(DK)]
                        ).then_inc(router_ready, 1)
                pe.wait_ge(router_copied, b + 1)
                pe.wait_ge(logits_done, b)
                last = None
                for k in range(TPB):
                    last = nc.tensor.transpose(g_ps[1][:, k * P:(k + 1) * P], rl[:, k * P:(k + 1) * P], ident[:])
                last.then_inc(logits_ready, 1)

            pe.wait_ge(logits_done, NB)

            def down(step, j, c):
                pe.wait_ge(hid_split, step + 1)
                f = FW0[j]
                for i in range(TPB):
                    pe.wait_ge(y_added, step * TPB + i)
                    at = ((j * NB + c) * TPB + i) % 3
                    product(nc, y_ps[at][:], [([hidS[c % 2][0:f, h, i * P:(i + 1) * P] for h in (HI, LO)],
                                               [downT[j][0:f, h, :] for h in (HI, LO)])]).then_inc(y_ready, 1)

            def expert(e, last):
                for j in range(NF):
                    f = FW0[j]
                    pe.wait_ge(prep_.split, e * JOBS + (j + 1) * PREP)
                    for c in range(NB):
                        step = e * STEPS + j * NB + c
                        pe.wait_ge(hid_done, step)
                        for to, w, ready in ((g_ps, gateT, gate_ready), (u_ps, upT, up_ready)):
                            product(nc, to[c % 2][0:f, :], [([w[j][:, h, k, 0:f] for h in (HI, LO)],
                                                            [xnT[:, h, k, c * S:(c + 1) * S] for h in (HI, LO)])
                                                           for k in range(DK)]).then_inc(ready, 1)
                        if (j, c) != (0, 0):
                            down(step - 1, *((j, c - 1) if c else (j - 1, NB - 1)))
                        if c < PREP and not (last and j > 0):
                            job, slot = prep_job(e, j, c)
                            if c == 0:
                                pe.wait_ge(raw_in[slot], (e + 1 + (j > 0)) * 3 * DMA)
                            prep(job, slot, c)
                down(e * STEPS + STEPS - 1, NF - 1, NB - 1)

            with pe.Fori(0, E0 - 1) as e:
                expert(e, False)
            expert(E0 - 1, True)

        @block.scalar
        def _(act):
            def prep(job, j, part):
                _, psum, (hi, lo) = prep_views(j, part)
                split_hi(nc, act, prep_, job, hi, psum)

            split_hi(nc, act, xt_, 0, gwT[:, HI].rearrange("p k e -> p (k e)"), y_ps[0][:, 0:DK * E0])
            for j in range(2):
                for part in range(PREP):
                    prep(j * PREP + part, j, part)
            act.wait_ge(rl_clear, 1)
            with act.Fori(0, NB) as b:
                norm_scalar(nc, act, n, b)
                for k in range(TPB):
                    split_hi(nc, act, xt_, 1 + b * TPB + k, xnT[:, HI, :, ds((b * TPB + k) * P, P)],
                             y_ps[(k + 1) % 2][:].rearrange("p (k c) -> p k c", k=DK))
                act.wait_ge(router_ready, b + 1)
                nc.scalar.activation(rl[0:E0, :], g_ps[0][0:E0, :], ACT.Copy).then_inc(router_copied, 1)
            act.wait_ge(gap_ready, 1)
            nc.scalar.activation(t.e[:], t.gap[:], ACT.Exp).then_inc(gap_exp, 1)

            def expert(e, last):
                for j in range(NF):
                    f = FW0[j]
                    for c in range(NB):
                        step = e * STEPS + j * NB + c
                        act.wait_ge(gate_ready, step + 1)
                        act.wait_ge(hid_done, step)
                        nc.scalar.activation(silu[c % 2][0:f, :], g_ps[c % 2][0:f, :], ACT.Silu).then_inc(silu_done, 1)
                        act.wait_ge(hid_done, step + 2)
                        nc.scalar.activation(hidS[c % 2][0:f, HI, :], hid[c % 2][0:f, :], ACT.Copy).then_inc(hid_hi, 1)
                        if c < PREP and not (last and j > 0):
                            job, slot = prep_job(e, j, c)
                            prep(job, slot, c)

            with act.Fori(0, E0 - 1) as e:
                expert(e, False)
            expert(E0 - 1, True)

        @block.vector
        def _(dve):
            def prep(job, j, part):
                _, psum, (hi, lo) = prep_views(j, part)
                split_lo(nc, dve, prep_, job, lo, psum, hi)

            nc.vector.memset(rl[:], 0.0).then_inc(rl_clear, 1)
            dve.sem_inc(xt_.split, 1)
            dve.sem_inc(hid_done, 1)
            dve.sem_inc(y_added, 2)
            for i in range(E0):
                nc.vector.memset(rev[:, :, i:i + 1], float(E0 - i))
            split_lo(nc, dve, xt_, 0, gwT[:, LO].rearrange("p k e -> p (k e)"), y_ps[0][:, 0:DK * E0],
                     gwT[:, HI].rearrange("p k e -> p (k e)"))
            for j in range(2):
                for part in range(PREP):
                    prep(j * PREP + part, j, part)
            with dve.Fori(0, NB) as b:
                norm_vector(nc, dve, n, b, lambda k: x[:, ds(b * TPB + k, 1), :])
                for k in range(TPB):
                    split_lo(nc, dve, xt_, 1 + b * TPB + k, xnT[:, LO, :, ds((b * TPB + k) * P, P)],
                             y_ps[(k + 1) % 2][:].rearrange("p (k c) -> p k c", k=DK),
                             xnT[:, HI, :, ds((b * TPB + k) * P, P)])
                dve.wait_ge(logits_ready, b + 1)
                nc.vector.tensor_copy(logits[:, ds(b * TPB, TPB), :],
                                      g_ps[1][:].rearrange("p (k e) -> p k e", k=TPB)[:, :, 0:E0]).then_inc(logits_done, 1)
            nc.vector.drain()
            top_two(nc, dve, logits, rev, t)
            nc.vector.tensor_tensor(t.gap[:], t.top2[:], t.top1[:], ALU.subtract).then_inc(gap_ready, 1)
            dve.wait_ge(gap_exp, 1)
            nc.vector.tensor_scalar_add(t.den[:], t.e[:], 1.0)
            nc.vector.drain()
            nc.vector.reciprocal(t.w1[:], t.den[:])
            nc.vector.drain()
            nc.vector.tensor_tensor(t.w2[:], t.e[:], t.w1[:], ALU.mult)
            nc.vector.drain()
            wide = lambda a: a[:].unsqueeze(2).to_broadcast([P, TILES, E0])
            nc.vector.tensor_tensor(t.hot1[:], t.hot1[:], wide(t.w1), ALU.mult)
            nc.vector.tensor_tensor(t.hot2[:], t.hot2[:], wide(t.w2), ALU.mult)
            nc.vector.drain()
            nc.vector.tensor_tensor(weight[:], t.hot1[:], t.hot2[:], ALU.add)
            nc.vector.drain()

            def add(e, step, j, c, i):
                dve.wait_ge(y_ready, step * TPB + i + 1)
                at = ((j * NB + c) * TPB + i) % 3
                tile = c * TPB + i
                nc.vector.scalar_tensor_tensor(
                    out=x[:, tile, :], in0=y_ps[at][:], scalar=weight[:, tile, ds(e, 1)], in1=x[:, tile, :],
                    op0=ALU.mult, op1=ALU.add).then_inc(y_added, 1)

            def expert(e, last):
                for j in range(NF):
                    f = FW0[j]
                    for c in range(NB):
                        step = e * STEPS + j * NB + c
                        before = (step - 1, *((j, c - 1) if c else (j - 1, NB - 1)))
                        first = (j, c) == (0, 0)
                        dve.wait_ge(silu_done, step + 1)
                        dve.wait_ge(up_ready, step + 1)
                        nc.vector.tensor_tensor(hid[c % 2][0:f, :], u_ps[c % 2][0:f, :], silu[c % 2][0:f, :],
                                                ALU.mult).then_inc(hid_done, 1)
                        if not first:
                            add(e, *before, 0)
                        dve.wait_ge(hid_hi, step + 1)
                        nc.vector.tensor_tensor(hidS[c % 2][0:f, LO, :], hid[c % 2][0:f, :],
                                                fp32(hidS[c % 2][0:f, HI, :]), ALU.subtract).then_inc(hid_split, 1)
                        if not first:
                            for i in range(1, TPB):
                                add(e, *before, i)
                        if c < PREP and not (last and j > 0):
                            job, slot = prep_job(e, j, c)
                            prep(job, slot, c)
                for i in range(TPB):
                    add(e, e * STEPS + STEPS - 1, NF - 1, NB - 1, i)

            with dve.Fori(0, E0 - 1) as e:
                expert(e, False)
            expert(E0 - 1, True)


GROUP = 4
GROUPS = B * HEADS // GROUP
QROWS, KROWS = 3 * HD + 2, 3 * HD
PAD = 32


def scratch(nc):
    def dram(name, shape, dt):
        return nc.dram_tensor(name, shape, dt, kind="Internal").ap()
    return {"q": dram("q_stack", [B * HEADS, QROWS, S], FP32),
            "k": dram("k_stack", [B * HEADS, KROWS, S], FP32),
            "v": dram("v_pad", [GROUPS, S, GROUP * PAD], FP32)}


def phase_qkv1(nc, io, x, ident):
    from contextlib import ExitStack
    io["scratch"] = scr = scratch(nc)
    ctx_dram = io["ctx_1024"].rearrange("b (t p) c -> p (b t) c", p=P)
    pos_dram = io["fside_BxSx2_0"].rearrange("b (t p) a -> p (b t) a", p=P)
    TWO_PI = 2.0 * np.pi
    c1 = float(np.float32(np.floor(TWO_PI * 2 ** 8) / 2 ** 8))
    c2 = float(np.floor((TWO_PI - c1) * 2 ** 20) / 2 ** 20)
    c3 = float(np.float32(TWO_PI - c1 - c2))
    ROUND = 1.5 * 2 ** 23
    PI_F = float(np.nextafter(np.float32(np.pi), np.float32(0)))
    AX, HALF = 2, HD // 4
    FREQS = [float(np.float32(ROPE_BASE) ** np.float32(-j / HALF)) for j in range(HALF)]
    HT = HEADS * HD // P
    with ExitStack() as ctx:
        def sb(name, shape, dt=FP32):
            return ctx.enter_context(nc.sbuf_tensor(f"q_{name}", shape, dt))

        def ps(name, shape):
            return ctx.enter_context(nc.psum_tensor(f"q_{name}", shape, FP32))

        def sem(name):
            return ctx.enter_context(nc.semaphore(f"q_{name}"))

        wq_raw = sb("wq_raw", [P, DK, D])
        wkv_raw = sb("wkv_raw", [P, CK, 2 * D])
        wq = sb("wq", [P, 2, DK, D], FP32R)
        wkv = sb("wkv", [P, 2, CK, 2 * D], FP32R)
        pos = sb("pos", [P, TILES, AX])
        ang, turns, red, mag, sine, cosine, nsine = (
            sb(name, [P, TILES, AX * HALF]) for name in ("ang", "turns", "red", "mag", "sine", "cosine", "nsine"))
        cos2 = sb("cos2", [P, TILES, HD])
        ctx_raw = sb("ctx_raw", [P, TPB, CTX])
        ctxT = sb("ctxT", [P, 2, CK, S], FP32R)
        xnT = sb("xnT", [P, 2, DK, S], FP32R)
        by_cos = [sb(f"by_cos{i}", [P, HEADS, HD]) for i in range(2)]
        by_sin = [sb(f"by_sin{i}", [P, HEADS, HD]) for i in range(2)]
        rot = [sb(f"rot{i}", [P, HEADS * HD]) for i in range(2)]
        qkT = [sb(f"qkT{i}", [P, 2, HT, S], FP32R) for i in range(2)]
        vpad = [sb(f"vpad{i}", [P, HEADS, PAD]) for i in range(2)]
        zeros = sb("zeros", [P, 2, S])
        n = Norm(nc, ctx, "qn")
        tp = [ps(f"tp{i}", [P, S]) for i in range(2)]
        qk_ps = [ps("qp", [P, D]), ps("kp", [P, D])]
        v_ps = [ps(f"vp{i}", [P, D]) for i in range(2)]
        t_ = Split(nc, ctx, "qt")
        w_in, pos_in, ctx_in = sem("w_in"), sem("pos_in"), sem("ctx_in")
        w_hi, w_split, red_ready, trig_ready = sem("w_hi"), sem("w_split"), sem("red_ready"), sem("trig_ready")
        qk_ready, rope_done, rot_done, v_ready, v_copied = (
            sem("qk_ready"), sem("rope_done"), sem("rot_done"), sem("v_ready"), sem("v_copied"))
        pads_set, out_q, out_v, out_zero = sem("pads_set"), sem("out_q"), sem("out_v"), sem("out_zero")
        JOBS = CK + TPB + 2 * TPB
        block = ctx.enter_context(nc.Block())

        def rot_job(b, t, i):
            return b * JOBS + CK + TPB + 2 * t + i

        @block.sync
        def _(sp):
            sp.dma_start(wq_raw[:], io["L1_xattn_Wq"].rearrange("(k p) n -> p k n", p=P)).then_inc(w_in, DMA)
            sp.dma_start(wkv_raw[:], io["L1_xattn_Wkv"].rearrange("(k p) n -> p k n", p=P)).then_inc(w_in, DMA)
            sp.dma_start(pos[:], pos_dram).then_inc(pos_in, DMA)
            with sp.Fori(0, B) as b:
                sp.wait_ge(t_.filled, b * JOBS)
                sp.dma_start(ctx_raw[:], ctx_dram[:, ds(b * TPB, TPB), :]).then_inc(ctx_in, DMA)
                for t in range(TPB):
                    sp.wait_ge(v_copied, b * TPB + t + 1)
                    sp.dma_start(scr["v"][ds(b * (HEADS // GROUP), HEADS // GROUP), t * P:(t + 1) * P, :].rearrange("g p c -> p g c"),
                                 vpad[t % 2][:].rearrange("p (g h) c -> p g (h c)", h=GROUP)).then_inc(out_v, DMA)
                sp.wait_ge(t_.split, (b + 1) * JOBS + 1)
                for i, (name, rows) in enumerate((("q", (HI, HI, LO)), ("k", (HI, LO, HI)))):
                    for block_row, part in enumerate(rows):
                        to = scr[name][ds(b * HEADS, HEADS), block_row * HD:(block_row + 1) * HD, :]
                        for ht in range(HT):
                            sp.dma_start(to[ht * (P // HD):(ht + 1) * (P // HD)],
                                         fp32(qkT[i][:, part, ht, :])).then_inc(out_q, DMA)
            sp.wait_ge(out_v, TILES * DMA)
            sp.wait_ge(out_q, B * 6 * HT * DMA)
            sp.wait_ge(out_zero, DMA)

        @block.tensor
        def _(pe):
            with pe.Fori(0, B) as b:
                pe.wait_ge(ctx_in, DMA * (b + 1))
                for k in range(CK):
                    pe.wait_ge(t_.split, b * JOBS + k)
                    transposes(nc, t_, tp[k % 2], [ctx_raw[:, t, k * P:(k + 1) * P] for t in range(TPB)], ident)
                for t in range(TPB):
                    pe.wait_ge(n.xn_ready, b * TPB + t + 1)
                    pe.wait_ge(t_.split, b * JOBS + CK + t)
                    transposes(nc, t_, tp[(CK + t) % 2], [n.xn[:, t, k * P:(k + 1) * P] for k in range(DK)], ident)
                pe.wait_ge(w_split, 2)

                def turn(t):
                    for i in range(2):
                        pe.wait_ge(rot_done, 2 * (b * TPB + t) + i + 1)
                        pe.wait_ge(t_.split, rot_job(b, t, i))
                        transposes(nc, t_, tp[i], [rot[i][:, k * P:(k + 1) * P] for k in range(HT)], ident)

                for t in range(TPB):
                    tile = b * TPB + t
                    cols = slice(t * P, (t + 1) * P)
                    if t == 0:
                        pe.wait_ge(t_.split, b * JOBS + CK + TPB + 1)
                    pe.wait_ge(rope_done, 2 * tile)
                    product(nc, qk_ps[0][:], [([xnT[:, h, k, cols] for h in (HI, LO)],
                                               [wq[:, h, k, :] for h in (HI, LO)]) for k in range(DK)]).then_inc(qk_ready, 1)
                    product(nc, qk_ps[1][:], [([ctxT[:, h, k, cols] for h in (HI, LO)],
                                               [wkv[:, h, k, 0:D] for h in (HI, LO)]) for k in range(CK)]).then_inc(qk_ready, 1)
                    pe.wait_ge(v_copied, tile)
                    product(nc, v_ps[t % 2][:], [([ctxT[:, h, k, cols] for h in (HI, LO)],
                                                  [wkv[:, h, k, D:2 * D] for h in (HI, LO)]) for k in range(CK)]).then_inc(v_ready, 1)
                    if t:
                        turn(t - 1)
                turn(TPB - 1)

        @block.scalar
        def _(act):
            act.wait_ge(w_in, 2 * DMA)
            nc.scalar.activation(wq[:, HI], wq_raw[:], ACT.Copy).then_inc(w_hi, 1)
            nc.scalar.activation(wkv[:, HI], wkv_raw[:], ACT.Copy).then_inc(w_hi, 1)
            act.wait_ge(red_ready, 1)
            nc.scalar.activation(sine[:], red[:], ACT.Sin).then_inc(trig_ready, 1)
            nc.scalar.activation(cosine[:], mag[:], ACT.Sin).then_inc(trig_ready, 1)
            act.wait_ge(pads_set, 5)
            with act.Fori(0, B) as b:
                for k in range(CK):
                    split_hi(nc, act, t_, b * JOBS + k, ctxT[:, HI, k, :], tp[k % 2][:])
                norm_scalar(nc, act, n, b)
                for t in range(TPB):
                    split_hi(nc, act, t_, b * JOBS + CK + t, xnT[:, HI, :, t * P:(t + 1) * P],
                             tp[(CK + t) % 2][:].rearrange("p (k c) -> p k c", k=DK))
                act.wait_ge(out_q, b * 6 * HT * DMA)

                def turn(t):
                    for i in range(2):
                        split_hi(nc, act, t_, rot_job(b, t, i), qkT[i][:, HI, :, t * P:(t + 1) * P],
                                 tp[i][:].rearrange("p (k c) -> p k c", k=HT))

                for t in range(TPB):
                    tile = b * TPB + t
                    act.wait_ge(v_ready, tile + 1)
                    act.wait_ge(out_v, tile * DMA)
                    nc.scalar.activation(vpad[t % 2][:, :, 0:HD], v_ps[t % 2][:].rearrange("p (h c) -> p h c", h=HEADS),
                                         ACT.Copy).then_inc(v_copied, 1)
                    if t:
                        turn(t - 1)
                turn(TPB - 1)

        @block.gpsimd
        def _(pool):
            for i in range(2):
                nc.gpsimd.memset(vpad[i][:], 0.0).then_inc(pads_set, 1)
            nc.gpsimd.memset(zeros[:], 0.0).then_inc(pads_set, 1)
            pool.wait_ge(pads_set, 3)
            for i in range(2):
                nc.gpsimd.memset(vpad[i][:, :, HD:HD + 1], 1.0).then_inc(pads_set, 1)
            pool.dma_start(scr["q"][:, 3 * HD:QROWS, :], zeros[:]).then_inc(out_zero, DMA)
            with pool.Fori(0, B) as b:
                for t in range(TPB):
                    for i in range(2):
                        pool.wait_ge(rope_done, 2 * (b * TPB + t) + i + 1)
                        pool.wait_ge(t_.filled, rot_job(b, t - 1, i) + 1 if t else b * JOBS)
                        nc.gpsimd.tensor_tensor(rot[i][:], by_cos[i][:].rearrange("p h c -> p (h c)"),
                                                by_sin[i][:].rearrange("p h c -> p (h c)"), ALU.add).then_inc(rot_done, 1)

        @block.vector
        def _(dve):
            dve.sem_inc(t_.split, 1)
            dve.wait_ge(pos_in, DMA)
            ang4 = ang[:].rearrange("p t (a j) -> p t a j", a=AX)
            for j in range(HALF):
                nc.vector.tensor_scalar(ang4[:, :, :, j], pos[:], FREQS[j], None, ALU.mult)
            nc.vector.drain()
            nc.vector.tensor_scalar(turns[:], ang[:], float(1.0 / TWO_PI), ROUND, ALU.mult, ALU.add)
            nc.vector.drain()
            nc.vector.tensor_scalar(turns[:], turns[:], -ROUND, None, ALU.add)
            nc.vector.drain()
            source = ang
            for part in (c1, c2, c3):
                nc.vector.scalar_tensor_tensor(out=red[:], in0=turns[:], scalar=-part, in1=source[:], op0=ALU.mult, op1=ALU.add)
                nc.vector.drain()
                source = red
            nc.vector.tensor_scalar(red[:], red[:], PI_F, -PI_F, ALU.min, ALU.max)
            nc.vector.drain()
            nc.vector.tensor_scalar(mag[:], red[:], -1.0, None, ALU.mult)
            nc.vector.drain()
            nc.vector.tensor_tensor(mag[:], mag[:], red[:], ALU.max)
            nc.vector.drain()
            nc.vector.tensor_scalar(mag[:], mag[:], -1.0, float(np.pi / 2), ALU.mult, ALU.add).then_inc(red_ready, 1)
            dve.wait_ge(trig_ready, 2)
            nc.vector.tensor_scalar(nsine[:], sine[:], -1.0, None, ALU.mult)
            for r in range(2):
                nc.vector.tensor_copy(cos2[:].rearrange("p t (f r) -> p t f r", r=2)[:, :, :, r], cosine[:])
            for i, (w, raw) in enumerate(((wq, wq_raw), (wkv, wkv_raw))):
                dve.wait_ge(w_hi, i + 1)
                nc.vector.tensor_tensor(w[:, LO], raw[:], fp32(w[:, HI]), ALU.subtract).then_inc(w_split, 1)
            with dve.Fori(0, B) as b:
                for k in range(CK):
                    split_lo(nc, dve, t_, b * JOBS + k, ctxT[:, LO, k, :], tp[k % 2][:], ctxT[:, HI, k, :])
                norm_vector(nc, dve, n, b, lambda t: x[:, ds(b * TPB + t, 1), :])
                for t in range(TPB):
                    split_lo(nc, dve, t_, b * JOBS + CK + t, xnT[:, LO, :, t * P:(t + 1) * P],
                             tp[(CK + t) % 2][:].rearrange("p (k c) -> p k c", k=DK), xnT[:, HI, :, t * P:(t + 1) * P])

                def turn(t):
                    for i in range(2):
                        split_lo(nc, dve, t_, rot_job(b, t, i), qkT[i][:, LO, :, t * P:(t + 1) * P],
                                 tp[i][:].rearrange("p (k c) -> p k c", k=HT), qkT[i][:, HI, :, t * P:(t + 1) * P])

                for t in range(TPB):
                    tile = b * TPB + t
                    for i in range(2):
                        dve.wait_ge(qk_ready, 2 * tile + i + 1)
                        dve.wait_ge(rot_done, 2 * tile)
                        src = qk_ps[i][:].rearrange("p (h c) -> p h c", h=HEADS)
                        nc.vector.tensor_tensor(by_cos[i][:], src, cos2[:, ds(tile, 1), :].to_broadcast([P, HEADS, HD]), ALU.mult)
                        pairs = qk_ps[i][:].rearrange("p (h f r) -> p h f r", h=HEADS, r=2)
                        swapped = by_sin[i][:].rearrange("p h (f r) -> p h f r", r=2)
                        for r, table in ((0, nsine), (1, sine)):
                            last = nc.vector.tensor_tensor(swapped[:, :, :, r], pairs[:, :, :, 1 - r],
                                                           table[:, ds(tile, 1), :].to_broadcast([P, HEADS, HD // 2]), ALU.mult)
                        last.then_inc(rope_done, 1)
                    if t:
                        turn(t - 1)
                turn(TPB - 1)


RING = 4


def phase_rope_attention1(nc, io, x, ident, attn):
    from contextlib import ExitStack
    scr = io["scratch"]
    KT = S // P
    SCALE = 1.0 / float(np.sqrt(HD))
    with ExitStack() as ctx:
        def sb(name, shape, dt=FP32):
            return ctx.enter_context(nc.sbuf_tensor(f"r_{name}", shape, dt))

        def ps(name, shape):
            return ctx.enter_context(nc.psum_tensor(f"r_{name}", shape, FP32))

        def sem(name):
            return ctx.enter_context(nc.semaphore(f"r_{name}"))

        kM = [sb(f"kM{s}", [P, GROUP, S], FP32R) for s in range(RING)]
        qS = [sb(f"qS{s}", [P, GROUP // 2, S], FP32R) for s in range(RING)]
        v = [sb(f"v{s}", [P, KT, GROUP * PAD]) for s in range(RING)]
        probs = [sb(f"probs{k}", [P, GROUP, S]) for k in range(KT)]
        top = [sb(f"top{i}", [P, KT, GROUP]) for i in range(2)]
        shift = [sb(f"shift{i}", [P, KT, GROUP, 2], FP32R) for i in range(2)]
        shiftT = [sb(f"shiftT{i}", [2 * GROUP, S], FP32R) for i in range(2)]
        outT = sb("outT", [P, S])
        rinv = sb("rinv", [P, KT * GROUP])
        bout = sb("bout", [P, D])
        st_ps = [ps(f"st{i}", [P, 2, S]) for i in range(2)]
        max_ps = [ps(f"max{i}", [P, S]) for i in range(2)]
        out_ps = ps("out", [P, S])
        tp = ps("tp", [P, S])
        set_, ones_set = sem("set"), sem("ones_set")
        kqv_in = [sem(f"kqv_in{s}") for s in range(RING)]
        shift_in = [sem(f"shift_in{s}") for s in range(RING)]
        bout_in = sem("bout_in")
        max_ready, max_read, shift_made = sem("max_ready"), sem("max_read"), sem("shift_made")
        shift_turned, shift_copied = sem("shift_turned"), sem("shift_copied")
        scores_ready, exp_done = sem("scores_ready"), sem("exp_done")
        out_ready, out_copied, out_turned, out_done = sem("out_ready"), sem("out_copied"), sem("out_turned"), sem("out_done")
        LOADS, SHIFTS = 5, 4
        block = ctx.enter_context(nc.Block())

        def steps(engine, step):
            rings = GROUPS // RING
            for s in range(RING):
                step(s, 0, s, s == 0, RING)
            with engine.Fori(1, rings - 1) as i:
                for s in range(RING):
                    step(i * RING + s, i, s, False, RING)
            for s in range(RING):
                step((rings - 1) * RING + s, rings - 1, s, False, RING - 1 - s)

        @block.gpsimd
        def _(pool):
            for s in range(RING):
                nc.gpsimd.memset(fp32(kM[s][:]), 0.0).then_inc(set_, 1)
                nc.gpsimd.memset(fp32(qS[s][:]), 0.0).then_inc(set_, 1)
            pool.wait_ge(set_, 2 * RING)
            for s in range(RING):
                for h in range(GROUP):
                    lo_row = 64 * (h % 2) + 32
                    nc.gpsimd.memset(fp32(kM[s][lo_row:lo_row + 32, h, :]), 1.0).then_inc(ones_set, 1)
            pool.wait_ge(ones_set, RING * GROUP)
            pool.wait_ge(bout_in, DMA)
            with pool.Fori(0, TILES) as tile:
                nc.gpsimd.tensor_tensor(x[:, ds(tile, 1), :], x[:, ds(tile, 1), :],
                                        bout[:].rearrange("p (a c) -> p a c", a=1), ALU.add)

        @block.sync
        def _(sp):
            def load(g, s):
                for half in range(2):
                    rows = 64 * half
                    heads = slice(half, GROUP, 2)
                    sp.dma_start(fp32(kM[s][rows:rows + KROWS, heads, :]),
                                 scr["k"][ds(g * GROUP, GROUP), :, :][heads].rearrange("h r n -> r h n")).then_inc(kqv_in[s], DMA)
                    sp.dma_start(fp32(qS[s][rows:rows + QROWS, :, :]),
                                 scr["q"][ds(g * GROUP, GROUP), :, :][heads].rearrange("h r n -> r h n")).then_inc(kqv_in[s], DMA)
                sp.dma_start(v[s][:], scr["v"][ds(g, 1), :, :].rearrange("g (k p) c -> p (g k) c", p=P)).then_inc(kqv_in[s], DMA)

            def shifts(g, s):
                sp.wait_ge(shift_copied, g + 1)
                for h in range(GROUP):
                    row = 64 * (h % 2) + 3 * HD
                    sp.dma_start(fp32(qS[s][row:row + 2, h // 2, :]), fp32(shiftT[s % 2][2 * h:2 * h + 2, :])).then_inc(shift_in[s], DMA)

            sp.dma_start(bout[:], io["L1_xattn_bout"].rearrange("(a n) -> a n", a=1).to_broadcast([P, D])).then_inc(bout_in, DMA)
            sp.wait_ge(ones_set, RING * GROUP)
            for s in range(RING - 1):
                load(s, s)
            shifts(0, 0)

            def step(g, i, s, first, left):
                if left >= RING - 1:
                    sp.wait_ge(out_ready, g)
                    load(g + RING - 1, (s + RING - 1) % RING)
                if left >= 1:
                    shifts(g + 1, (s + 1) % RING)

            steps(sp, step)

        @block.tensor
        def _(pe):
            def scores(g, i, s, k):
                if k == 0:
                    pe.wait_ge(shift_in[s], (i + 1) * SHIFTS * DMA)
                for pair in range(2):
                    pe.wait_ge(exp_done, (g * KT + k) * 2 + pair)
                    last = None
                    for j in range(2):
                        last = nc.tensor.matmul(st_ps[pair][:, j, :], kM[s][:, 2 * pair + j, k * P:(k + 1) * P],
                                                qS[s][:, pair, :], start=True, stop=True)
                    last.then_inc(scores_ready, 1)

            def maxima(g, i, s, q):
                if q == 0:
                    pe.wait_ge(kqv_in[s], (i + 1) * LOADS * DMA)
                for h in range(GROUP):
                    pe.wait_ge(max_read, (g * KT + q) * GROUP + h)
                    nc.tensor.matmul(max_ps[h % 2][:], qS[s][:, h // 2, q * P:(q + 1) * P], kM[s][:, h, :],
                                     start=True, stop=True).then_inc(max_ready, 1)

            def turn_shifts(g, s):
                pe.wait_ge(shift_made, g + 1)
                if not (isinstance(g, int) and g < 3):
                    pe.wait_ge(out_done, g - 2)
                last = None
                for q in range(KT):
                    last = nc.tensor.transpose(tp[0:2 * GROUP, q * P:(q + 1) * P],
                                               fp32(shift[s % 2][:, q].rearrange("p h a -> p (h a)")), ident[:])
                last.then_inc(shift_turned, 1)

            def values(g, s, k):
                pe.wait_ge(exp_done, (g * KT + k) * 2 + 3)
                if k == 0:
                    pe.wait_ge(out_copied, g)
                last = None
                for h in range(GROUP):
                    last = nc.tensor.matmul(out_ps[h * PAD:(h + 1) * PAD, :], v[s][:, k, h * PAD:(h + 1) * PAD],
                                            probs[k][:, h, :], start=(k == 0), stop=(k == KT - 1))
                if k == KT - 1:
                    last.then_inc(out_ready, 1)

            def turn_out(g, shifts_copied):
                pe.wait_ge(out_copied, g + 1)
                pe.wait_ge(out_done, g)
                pe.wait_ge(shift_copied, shifts_copied)
                last = None
                for q in range(KT):
                    last = nc.tensor.transpose(tp[:, q * P:(q + 1) * P], outT[:, q * P:(q + 1) * P], ident[:])
                last.then_inc(out_turned, 1)

            for g in range(2):
                for q in range(KT):
                    maxima(g, 0, g, q)
            turn_shifts(0, 0)

            def step(g, i, s, first, left):
                for k in range(KT):
                    scores(g, i, s, k)
                    if k == 0:
                        if not first:
                            values(g - 1, (s - 1) % RING, KT - 1)
                        if left >= 1:
                            turn_shifts(g + 1, (s + 1) % RING)
                    else:
                        values(g, s, k - 1)
                        if k == 1 and not first:
                            turn_out(g - 1, g + 2 if left >= 1 else g + 1)
                    if left >= 2:
                        maxima(g + 2, i + (s + 2) // RING, (s + 2) % RING, k)

            steps(pe, step)
            values(GROUPS - 1, RING - 1, KT - 1)
            turn_out(GROUPS - 1, GROUPS)

        @block.scalar
        def _(act):
            def copy_shifts(g, s):
                act.wait_ge(shift_turned, g + 1)
                nc.scalar.activation(shiftT[s % 2][:], tp[0:2 * GROUP, :], ACT.Copy).then_inc(shift_copied, 1)

            def copy_out(g):
                act.wait_ge(out_ready, g + 1)
                nc.scalar.activation(outT[:], out_ps[:], ACT.Copy).then_inc(out_copied, 1)

            copy_shifts(0, 0)

            def step(g, i, s, first, left):
                for k in range(KT):
                    for pair in range(2):
                        act.wait_ge(scores_ready, (g * KT + k) * 2 + pair + 1)
                        nc.scalar.activation(probs[k][:, 2 * pair:2 * pair + 2, :], st_ps[pair][:], ACT.Exp,
                                             scale=SCALE).then_inc(exp_done, 1)
                    if k == 0:
                        if not first:
                            copy_out(g - 1)
                        if left >= 1:
                            copy_shifts(g + 1, (s + 1) % RING)

            steps(act, step)
            copy_out(GROUPS - 1)

        @block.vector
        def _(dve):
            def read_maxima(g, s, q):
                for h in range(GROUP):
                    dve.wait_ge(max_ready, (g * KT + q) * GROUP + h + 1)
                    nc.vector.reduce_max(top[s % 2][:, q, h:h + 1], max_ps[h % 2][:], AXIS_X).then_inc(max_read, 1)

            def make_shifts(s):
                nc.vector.drain()
                nc.vector.tensor_scalar(shift[s % 2][:, :, :, 0], top[s % 2][:], -1.0, None, ALU.mult)
                nc.vector.drain()
                nc.vector.scalar_tensor_tensor(out=shift[s % 2][:, :, :, 1], in0=top[s % 2][:], scalar=-1.0,
                                               in1=fp32(shift[s % 2][:, :, :, 0]), op0=ALU.mult,
                                               op1=ALU.subtract).then_inc(shift_made, 1)

            def normalise(g):
                dve.wait_ge(out_turned, g + 1)
                turned = tp[:].rearrange("p (a c) -> p a c", c=PAD)
                nc.vector.reciprocal(rinv[:], turned[:, :, HD])
                nc.vector.drain()
                nc.vector.tensor_tensor(attn[:, ds(g, 1), :, :].rearrange("p g a c -> p (g a) c"), turned[:, :, 0:HD],
                                        rinv[:].unsqueeze(2).to_broadcast([P, KT * GROUP, HD]), ALU.mult).then_inc(out_done, 1)

            dve.sem_inc(max_read, 1)
            dve.sem_inc(exp_done, 1)
            for g in range(2):
                for q in range(KT):
                    read_maxima(g, g, q)
                make_shifts(g)

            def step(g, i, s, first, left):
                for q in range(KT):
                    if left >= 2:
                        read_maxima(g + 2, s, q)
                    if q == 1 and not first:
                        normalise(g - 1)
                if left >= 2:
                    make_shifts((s + 2) % RING)

            steps(dve, step)
            normalise(GROUPS - 1)


def phase_out1(nc, io, x, ident, attn):
    from contextlib import ExitStack
    with ExitStack() as ctx:
        def sb(name, shape, dt=FP32):
            return ctx.enter_context(nc.sbuf_tensor(f"o_{name}", shape, dt))

        def ps(name, shape):
            return ctx.enter_context(nc.psum_tensor(f"o_{name}", shape, FP32))

        def sem(name):
            return ctx.enter_context(nc.semaphore(f"o_{name}"))

        w_raw = sb("w_raw", [P, DK, D])
        w = sb("w", [P, 2, DK, D], FP32R)
        rows = [sb(f"rows{i}", [P, D]) for i in range(2)]
        aT = [sb(f"aT{i}", [P, 2, DK, P], FP32R) for i in range(2)]
        tp = [ps(f"tp{i}", [P, D]) for i in range(2)]
        y_ps = [ps(f"y{i}", [P, D]) for i in range(2)]
        t_ = Split(nc, ctx, "ot")
        w_in, w_hi, w_split, rows_ready, y_ready, y_added = (
            sem("w_in"), sem("w_hi"), sem("w_split"), sem("rows_ready"), sem("y_ready"), sem("y_added"))
        block = ctx.enter_context(nc.Block())

        @block.sync
        def _(sp):
            sp.dma_start(w_raw[:], io["L1_xattn_Wout"].rearrange("(k p) n -> p k n", p=P)).then_inc(w_in, DMA)

        @block.tensor
        def _(pe):
            def out_product(tile, t):
                pe.wait_ge(t_.split, tile + 2)
                pe.wait_ge(y_added, tile)
                product(nc, y_ps[t % 2][:], [([aT[t % 2][:, h, k, :] for h in (HI, LO)],
                                              [w[:, h, k, :] for h in (HI, LO)]) for k in range(DK)]).then_inc(y_ready, 1)

            with pe.Fori(0, B) as b:
                for t in range(TPB):
                    tile = b * TPB + t
                    pe.wait_ge(rows_ready, tile + 1)
                    pe.wait_ge(t_.split, tile)
                    transposes(nc, t_, tp[t % 2], [rows[t % 2][:, k * P:(k + 1) * P] for k in range(DK)], ident)
                    if t == 0:
                        pe.wait_ge(w_split, 1)
                    if t:
                        out_product(tile - 1, t - 1)
                out_product(b * TPB + TPB - 1, TPB - 1)

        @block.scalar
        def _(act):
            act.wait_ge(w_in, DMA)
            nc.scalar.activation(w[:, HI], w_raw[:], ACT.Copy).then_inc(w_hi, 1)
            with act.Fori(0, B) as b:
                for t in range(TPB):
                    tile = b * TPB + t
                    act.wait_ge(t_.filled, tile - 1 if t else b * TPB)
                    nc.scalar.activation(rows[t % 2][:].rearrange("p (g c) -> p g c", g=HEADS // GROUP),
                                         attn[:, ds(b * (HEADS // GROUP), HEADS // GROUP), t * GROUP:(t + 1) * GROUP, :]
                                         .rearrange("p g a c -> p g (a c)"), ACT.Copy).then_inc(rows_ready, 1)
                    split_hi(nc, act, t_, tile, aT[t % 2][:, HI], tp[t % 2][:].rearrange("p (k c) -> p k c", k=DK))

        @block.vector
        def _(dve):
            dve.sem_inc(t_.split, 1)
            dve.sem_inc(y_added, 1)
            dve.wait_ge(w_hi, 1)
            nc.vector.tensor_tensor(w[:, LO], w_raw[:], fp32(w[:, HI]), ALU.subtract).then_inc(w_split, 1)

            def add(tile, t):
                dve.wait_ge(y_ready, tile + 1)
                nc.vector.tensor_tensor(x[:, ds(tile, 1), :], y_ps[t % 2][:].rearrange("p (a c) -> p a c", a=1),
                                        x[:, ds(tile, 1), :], ALU.add).then_inc(y_added, 1)

            with dve.Fori(0, B) as b:
                for t in range(TPB):
                    tile = b * TPB + t
                    split_lo(nc, dve, t_, tile, aT[t % 2][:, LO], tp[t % 2][:].rearrange("p (k c) -> p k c", k=DK), aT[t % 2][:, HI])
                    if t:
                        add(tile - 1, t - 1)
                add(b * TPB + TPB - 1, TPB - 1)


def phase_rope1(nc, io, x, ident):
    phase_qkv1(nc, io, x, ident)
    with nc.sbuf_tensor("attn", [P, GROUPS, TPB * GROUP, HD], FP32) as attn:
        phase_rope_attention1(nc, io, x, ident, attn)
        phase_out1(nc, io, x, ident, attn)


def phase_ffn1(nc, io, x, ident):
    from contextlib import ExitStack
    ER = E1 * R1
    NF = DFF // P
    HALVES = 2
    CH = B // HALVES
    HT, HTOK = CH * TPB, CH * S
    STEPS = NF * CH
    PREP = 4
    USES = TPB + 2
    gate_dram, up_dram, down_dram = io["L1_ffn_Wg"], io["L1_ffn_Wu"], io["L1_ffn_Wd"]
    out_dram = io["out"].rearrange("b (t p) d -> p (b t) d", p=P)
    with ExitStack() as ctx:
        def sb(name, shape, dt=FP32):
            return ctx.enter_context(nc.sbuf_tensor(f"f_{name}", shape, dt))

        def ps(name, shape):
            return ctx.enter_context(nc.psum_tensor(f"f_{name}", shape, FP32))

        def sem(name):
            return ctx.enter_context(nc.semaphore(f"f_{name}"))

        xnT = sb("xnT", [P, 2, DK, HTOK], FP32R)
        agT, auT = sb("agT", [P, 2, DK, ER], FP32R), sb("auT", [P, 2, DK, ER], FP32R)
        wrT = sb("wrT", [P, 2, DK, E1], FP32R)
        bdT = sb("bdT", [ER, 2, D], FP32R)
        wr_raw = sb("wr_raw", [E1, D])
        gate_raw, up_raw, down_raw = sb("gate_raw", [P, D]), sb("up_raw", [P, D]), sb("down_raw", [P, DK, P])
        lora_raw = sb("lora_raw", [P, 3, P])
        gateT = [sb(f"gateT{s}", [P, 2, DK, P], FP32R) for s in range(2)]
        upT = [sb(f"upT{s}", [P, 2, DK, P], FP32R) for s in range(2)]
        downT = [sb(f"downT{s}", [P, 2, D], FP32R) for s in range(2)]
        loraT = [sb(f"loraT{s}", [P, 2, 3, P], FP32R) for s in range(2)]
        rl = sb("rl", [P, S])
        logits = sb("logits", [P, HT, E1])
        shifted = sb("shifted", [P, HT, E1])
        rev = sb("rev", [P, HT, E1])
        hots = sb("hots", [P, HT, 4, E1])
        am = sb("am", [P, 2, 2, 2, HTOK], FP32R)
        down_acc = sb("down_acc", [P, 2, HTOK])
        hidS = [sb(f"hidS{c}", [P, 3, 2, S], FP32R) for c in range(2)]
        work = sb("work", [P, 10, S])

        def hid(c, var):
            return work[:, 4 + 3 * c + var, :]

        mk = work[:, 4, :]
        maskT = work[:, 5:9, :].rearrange("p (k c) n -> p k (c n)", k=2)
        n = Norm(nc, ctx, "fn", xn=work[:, 0:4, :])
        t = TopTwo(nc, ctx, "ft", HT, E1)
        g_ps = [ps(f"g{c}", [P, S]) for c in range(CH)]
        u_ps = [ps(f"u{c}", [P, S]) for c in range(CH)]
        prep_ps = ps("prep", [P, S])
        y_ps = [ps(f"y{i}", [P, S]) for i in range(3)]
        c_, xt_, prep_ = Split(nc, ctx, "fc"), Split(nc, ctx, "fx"), Split(nc, ctx, "fp")
        am_ = Split(nc, ctx, "fa")
        const_in, raw_in = sem("const_in"), sem("raw_in")
        router_ready, router_copied, logits_ready, logits_done = (
            sem("router_ready"), sem("router_copied"), sem("logits_ready"), sem("logits_done"))
        gap_ready, gap_exp, rl_clear = sem("gap_ready"), sem("gap_exp"), sem("rl_clear")
        mk_made, mk_turned, mask_copied, a_ready, a_used = (
            sem("mk_made"), sem("mk_turned"), sem("mask_copied"), sem("a_ready"), sem("a_used"))
        gate_ready, up_ready = sem("gate_ready"), sem("up_ready")
        silu_done, hid_done, hid_hi, hid_split = sem("silu_done"), sem("hid_done"), sem("hid_hi"), sem("hid_split")
        y_ready, y_added = sem("y_ready"), sem("y_added")
        z_ready, z_hi, z_split, z_out, z_added, stored = (
            sem("z_ready"), sem("z_hi"), sem("z_split"), sem("z_out"), sem("z_added"), sem("stored"))
        CONST_JOBS = 4
        block = ctx.enter_context(nc.Block())

        def const_views(job):
            if job < 2:
                raw, to = ((gate_raw, agT), (up_raw, auT))[job]
                return ([raw[:, k * P:(k + 1) * P] for k in range(DK)],
                        prep_ps[:].rearrange("p (k c) -> p k c", k=DK), [to[:, h] for h in (HI, LO)])
            if job == 2:
                return ([wr_raw[:, k * P:(k + 1) * P] for k in range(DK)],
                        prep_ps[:, 0:DK * E1].rearrange("p (k c) -> p k c", k=DK), [wrT[:, h] for h in (HI, LO)])
            return ([down_raw[:, k, :] for k in range(DK)], prep_ps[:], [bdT[:, h] for h in (HI, LO)])

        def prep_views(s, part):
            if part < 2:
                raw, to = ((gate_raw, gateT), (up_raw, upT))[part]
                return ([raw[:, k * P:(k + 1) * P] for k in range(DK)],
                        prep_ps[:].rearrange("p (k c) -> p k c", k=DK), [to[s][:, h] for h in (HI, LO)])
            if part == 2:
                return ([down_raw[:, k, :] for k in range(DK)], prep_ps[:], [downT[s][:, h] for h in (HI, LO)])
            return ([lora_raw[:, k, :] for k in range(3)], prep_ps[:, 0:3 * P].rearrange("p (k c) -> p k c", k=3),
                    [loraT[s][:, h] for h in (HI, LO)])

        def tiles(engine, half, tile):
            tile(0, 0, True, False)
            tile(1, 1, False, False)
            with engine.Fori(1, (NF - 1) // 2) as i:
                for s in range(2):
                    tile(2 * i + s, s, False, False)
            tile(NF - 1, 0, False, True)

        def ring(c, use):
            return y_ps[(c * USES + use) % 3]

        @block.sync
        def _(sp):
            sp.dma_start(wr_raw[:], io["L1_ffn_Wr"]).then_inc(const_in, DMA)
            sp.dma_start(gate_raw[:], io["L1_ffn_Ag"].rearrange("e r d -> (e r) d")).then_inc(const_in, DMA)
            sp.dma_start(up_raw[:], io["L1_ffn_Au"].rearrange("e r d -> (e r) d")).then_inc(const_in, DMA)
            for k in range(DK):
                sp.dma_start(down_raw[:, k, :].rearrange("p (e r) -> p e r", e=E1),
                             io["L1_ffn_Bd"][:, k * P:(k + 1) * P, :].rearrange("e p r -> p e r")).then_inc(const_in, DMA)
            sp.wait_ge(c_.filled, CONST_JOBS)

            def load(h, f):
                sp.wait_ge(prep_.filled, (h * NF + f) * PREP)
                sp.dma_start(gate_raw[:], gate_dram[ds(f * P, P), :]).then_inc(raw_in, DMA)
                sp.dma_start(up_raw[:], up_dram[ds(f * P, P), :]).then_inc(raw_in, DMA)
                sp.dma_start(down_raw[:], down_dram[:, ds(f * P, P)].rearrange("(k p) f -> p k f", p=P)).then_inc(raw_in, DMA)
                for i, name in enumerate(("L1_ffn_Bg", "L1_ffn_Bu")):
                    sp.dma_start(lora_raw[:, i, :].rearrange("p (e r) -> p e r", e=E1),
                                 io[name][:, ds(f * P, P), :].rearrange("e f r -> f e r")).then_inc(raw_in, DMA)
                sp.dma_start(lora_raw[:, 2, :], io["L1_ffn_Ad"].rearrange("e r f -> (e r) f")[:, ds(f * P, P)]).then_inc(raw_in, DMA)

            with sp.Fori(0, HALVES) as h:
                with sp.Fori(0, NF) as f:
                    load(h, f)
                for c in range(CH):
                    sp.wait_ge(z_added, h * HT + (c + 1) * TPB)
                    sp.dma_start(out_dram[:, ds(h * HT + c * TPB, TPB), :], x[:, ds(h * HT + c * TPB, TPB), :]).then_inc(stored, DMA)
            sp.wait_ge(stored, HALVES * CH * DMA)

        LOADS = 6

        @block.tensor
        def _(pe):
            def prep(h, f, s, part):
                job = (h * NF + f) * PREP + part
                if part == 0:
                    pe.wait_ge(raw_in, (h * NF + f + 1) * LOADS * DMA)
                pe.wait_ge(prep_.split, job)
                transposes(nc, prep_, prep_ps, prep_views(s, part)[0], ident)

            pe.wait_ge(const_in, (3 + DK) * DMA)
            for job in range(CONST_JOBS):
                pe.wait_ge(c_.split, job)
                transposes(nc, c_, prep_ps, const_views(job)[0], ident)
            pe.wait_ge(c_.split, CONST_JOBS)
            with pe.Fori(0, HALVES) as h:
                for part in range(PREP):
                    prep(h, 0, 0, part)
                for c in range(CH):
                    for k in range(TPB):
                        job = (h * CH + c) * TPB + k
                        pe.wait_ge(n.xn_ready, job + 1)
                        pe.wait_ge(xt_.split, job)
                        transposes(nc, xt_, (g_ps, u_ps)[k % 2][0], [n.xn[:, k, i * P:(i + 1) * P] for i in range(DK)], ident)
                    pe.wait_ge(xt_.split, (h * CH + c + 1) * TPB + 1)
                    pe.wait_ge(router_copied, h * CH + c)
                    product(nc, g_ps[1][0:E1, :], [([wrT[:, i, k, :] for i in (HI, LO)],
                                                 [xnT[:, i, k, c * S:(c + 1) * S] for i in (HI, LO)])
                                                for k in range(DK)]).then_inc(router_ready, 1)
                    pe.wait_ge(router_copied, h * CH + c + 1)
                    pe.wait_ge(logits_done, h * CH + c)
                    last = None
                    for k in range(TPB):
                        last = nc.tensor.transpose(u_ps[1][:, k * P:(k + 1) * P], rl[:, k * P:(k + 1) * P], ident[:])
                    last.then_inc(logits_ready, 1)

                def turn_masks(base):
                    for i in range(HT):
                        pe.wait_ge(mk_made, base + i + 1)
                        pe.wait_ge(mask_copied, base + i)
                        for k in range(4):
                            last = nc.tensor.transpose(y_ps[i % 2][:, k * P:(k + 1) * P], mk[:, k * P:(k + 1) * P], ident[:])
                        last.then_inc(mk_turned, 1)

                turn_masks(h * 2 * HT)
                pe.wait_ge(logits_done, h * CH + CH)
                for c in range(CH):
                    for i, (a, to) in enumerate(((agT, g_ps[1]), (auT, u_ps[1]))):
                        pe.wait_ge(a_used, 4 * (h * CH + c) + 2 * i - 2 if c else 4 * h * CH)
                        product(nc, to[:], [([a[:, j, k, :] for j in (HI, LO)],
                                             [xnT[:, j, k, c * S:(c + 1) * S] for j in (HI, LO)])
                                            for k in range(DK)]).then_inc(a_ready, 1)
                pe.wait_ge(am_.split, (h + 1) * CH * 4)

                def ring_wait(step, use):
                    pe.wait_ge(y_added, step * USES + use)

                def down(step, s, c):
                    pe.wait_ge(hid_split, 3 * step + 3 + 1)
                    for i in range(TPB):
                        ring_wait(step, i)
                        product(nc, ring(c, i)[:], [([hidS[c][:, 0, j, i * P:(i + 1) * P] for j in (HI, LO)],
                                                     [downT[s][:, j, :] for j in (HI, LO)])]).then_inc(y_ready, 1)

                def down_lora(step, s, c):
                    for k in range(2):
                        pe.wait_ge(hid_split, 3 * step + 3 + 2 + k)
                        ring_wait(step, TPB + k)
                        product(nc, ring(c, TPB + k)[:], [([loraT[s][:, j, 2, :] for j in (HI, LO)],
                                                          [hidS[c][:, 1 + k, j, :] for j in (HI, LO)])]).then_inc(y_ready, 1)

                def lora(step, s, c, var):
                    pe.wait_ge(hid_done, 3 * step + var + 3)
                    for i, (to, ready) in enumerate(((g_ps[c], gate_ready), (u_ps[c], up_ready))):
                        add_product(nc, to[:], [loraT[s][:, j, i, :] for j in (HI, LO)],
                                    [am[:, i, var - 1, j, c * S:(c + 1) * S] for j in (HI, LO)]).then_inc(ready, 1)

                def tile(f, s, first, last):
                    pe.wait_ge(prep_.split, (h * NF + f + 1) * PREP)
                    for c in range(CH):
                        step = h * STEPS + f * CH + c
                        before = (step - 1, s if c else 1 - s, 1 - c)
                        has_before = not (first and c == 0)
                        pe.wait_ge(hid_done, 3 * step)
                        product(nc, g_ps[c][:], [([gateT[s][:, j, k, :] for j in (HI, LO)],
                                                  [xnT[:, j, k, c * S:(c + 1) * S] for j in (HI, LO)])
                                                 for k in range(DK)]).then_inc(gate_ready, 1)
                        if not last:
                            prep(h, f + 1, 1 - s, 2 * c)
                        product(nc, u_ps[c][:], [([upT[s][:, j, k, :] for j in (HI, LO)],
                                                  [xnT[:, j, k, c * S:(c + 1) * S] for j in (HI, LO)])
                                                 for k in range(DK)]).then_inc(up_ready, 1)
                        if has_before:
                            down(*before)
                        lora(step, s, c, 1)
                        if not last:
                            prep(h, f + 1, 1 - s, 2 * c + 1)
                        if has_before:
                            down_lora(*before)
                        lora(step, s, c, 2)

                tiles(pe, h, tile)
                end = (h * STEPS + STEPS - 1, 0, CH - 1)
                down(*end)
                down_lora(*end)
                pe.wait_ge(y_added, (h + 1) * STEPS * USES + 2)
                turn_masks(h * 2 * HT + HT)
                pe.wait_ge(z_split, h + 1)
                for i in range(HT):
                    pe.wait_ge(z_added, h * HT + i - 1 if i else h * HT)
                    product(nc, y_ps[i % 2][:], [([am[:, 0, 0, j, i * P:(i + 1) * P] for j in (HI, LO)],
                                                 [bdT[:, j, :] for j in (HI, LO)])]).then_inc(z_out, 1)

        @block.scalar
        def _(act):
            def prep(h, f, s, part):
                _, psum, (hi, lo) = prep_views(s, part)
                split_hi(nc, act, prep_, (h * NF + f) * PREP + part, hi, psum)

            for job in range(CONST_JOBS):
                _, psum, (hi, lo) = const_views(job)
                split_hi(nc, act, c_, job, hi, psum)
            act.wait_ge(rl_clear, 1)
            with act.Fori(0, HALVES) as h:
                for part in range(PREP):
                    prep(h, 0, 0, part)
                for c in range(CH):
                    norm_scalar(nc, act, n, h * CH + c)
                    for k in range(TPB):
                        at = (c * TPB + k) * P
                        split_hi(nc, act, xt_, (h * CH + c) * TPB + k, xnT[:, HI, :, at:at + P],
                                 (g_ps, u_ps)[k % 2][0][:].rearrange("p (k c) -> p k c", k=DK))
                    act.wait_ge(router_ready, h * CH + c + 1)
                    nc.scalar.activation(rl[0:E1, :], g_ps[1][0:E1, :], ACT.Copy).then_inc(router_copied, 1)
                act.wait_ge(gap_ready, h + 1)
                nc.scalar.activation(shifted[:], shifted[:], ACT.Exp).then_inc(gap_exp, 1)
                nc.scalar.activation(t.e[:], t.gap[:], ACT.Exp).then_inc(gap_exp, 1)

                def copy_masks(base, part):
                    for i in range(HT):
                        act.wait_ge(mk_turned, base + i + 1)
                        nc.scalar.activation(maskT[:, :, i * P:(i + 1) * P],
                                             y_ps[i % 2][:, part * 2 * P:(part + 1) * 2 * P].rearrange("p (k c) -> p k c", k=2),
                                             ACT.Copy).then_inc(mask_copied, 1)

                copy_masks(h * 2 * HT, 0)
                for c in range(CH):
                    for i in range(2):
                        for k in range(2):
                            job = 4 * (h * CH + c) + 2 * i + k
                            act.wait_ge(a_used, job + 1)
                            nc.scalar.activation(am[:, i, k, HI, c * S:(c + 1) * S], work[:, 2 * i + k, :], ACT.Copy).then_inc(am_.hi_done, 1)

                def tile(f, s, first, last):
                    for c in range(CH):
                        step = h * STEPS + f * CH + c

                        def silu(var):
                            act.wait_ge(gate_ready, 3 * step + var + 1)
                            nc.scalar.activation(hid(c, var), g_ps[c][:], ACT.Silu).then_inc(silu_done, 1)

                        def hi(var):
                            act.wait_ge(hid_done, 3 * step + var + 1 + 3)
                            nc.scalar.activation(hidS[c][:, var, HI, :], hid(c, var), ACT.Copy).then_inc(hid_hi, 1)

                        act.wait_ge(hid_split, 3 * step)
                        silu(0)
                        if not last:
                            prep(h, f + 1, 1 - s, 2 * c)
                        hi(0)
                        silu(1)
                        if not last:
                            prep(h, f + 1, 1 - s, 2 * c + 1)
                        hi(1)
                        silu(2)
                        hi(2)

                tiles(act, h, tile)
                copy_masks(h * 2 * HT + HT, 1)
                act.wait_ge(z_ready, h + 1)
                nc.scalar.activation(am[:, 0, 0, HI, :], down_acc[:, 0, :], ACT.Copy).then_inc(z_hi, 1)

        @block.gpsimd
        def _(pool):
            pool.sem_inc(hid_split, 3)
            with pool.Fori(0, HALVES) as h:
                def tile(f, s, first, last):
                    for c in range(CH):
                        step = h * STEPS + f * CH + c
                        for var in range(3):
                            pool.wait_ge(hid_hi, 3 * step + var + 1)
                            nc.gpsimd.tensor_tensor(hidS[c][:, var, LO, :], hid(c, var), fp32(hidS[c][:, var, HI, :]),
                                                    ALU.subtract).then_inc(hid_split, 1)

                tiles(pool, h, tile)

        @block.vector
        def _(dve):
            def prep(h, f, s, part):
                _, psum, (hi, lo) = prep_views(s, part)
                split_lo(nc, dve, prep_, (h * NF + f) * PREP + part, lo, psum, hi)

            nc.vector.memset(rl[:], 0.0).then_inc(rl_clear, 1)
            dve.sem_inc(xt_.split, 1)
            dve.sem_inc(mask_copied, 1)
            dve.sem_inc(hid_done, 3)
            dve.sem_inc(y_added, 2)
            for i in range(E1):
                nc.vector.memset(rev[:, :, i:i + 1], float(E1 - i))
            for job in range(CONST_JOBS):
                _, psum, (hi, lo) = const_views(job)
                split_lo(nc, dve, c_, job, lo, psum, hi)
            with dve.Fori(0, HALVES) as h:
                for part in range(PREP):
                    prep(h, 0, 0, part)
                for c in range(CH):
                    norm_vector(nc, dve, n, h * CH + c, lambda k: x[:, ds(h * HT + c * TPB + k, 1), :])
                    for k in range(TPB):
                        at = (c * TPB + k) * P
                        split_lo(nc, dve, xt_, (h * CH + c) * TPB + k, xnT[:, LO, :, at:at + P],
                                 (g_ps, u_ps)[k % 2][0][:].rearrange("p (k c) -> p k c", k=DK), xnT[:, HI, :, at:at + P])
                    dve.wait_ge(logits_ready, h * CH + c + 1)
                    nc.vector.tensor_copy(logits[:, c * TPB:(c + 1) * TPB, :],
                                          u_ps[1][:].rearrange("p (k e) -> p k e", k=TPB)[:, :, 0:E1]).then_inc(logits_done, 1)
                nc.vector.drain()
                top_two(nc, dve, logits, rev, t)
                wide = lambda a: a[:].unsqueeze(2).to_broadcast([P, HT, E1])
                nc.vector.tensor_tensor(shifted[:], logits[:], wide(t.top1), ALU.subtract)
                nc.vector.tensor_tensor(t.gap[:], t.top2[:], t.top1[:], ALU.subtract)
                nc.vector.memset(down_acc[:], 0.0)
                nc.vector.drain().then_inc(gap_ready, 1)
                dve.wait_ge(gap_exp, 2 * h + 2)
                nc.vector.reduce_sum(t.den[:], shifted[:], AXIS_X)
                nc.vector.drain()
                nc.vector.reciprocal(t.w1[:], t.den[:])
                nc.vector.drain()
                nc.vector.tensor_tensor(t.w2[:], t.e[:], t.w1[:], ALU.mult)
                nc.vector.tensor_copy(hots[:, :, 0, :], t.hot1[:])
                nc.vector.tensor_tensor(hots[:, :, 1, :], t.hot2[:], t.hot1[:], ALU.subtract)
                nc.vector.drain()
                nc.vector.tensor_tensor(hots[:, :, 2, :], t.hot1[:], wide(t.w1), ALU.mult)
                nc.vector.tensor_tensor(hots[:, :, 3, :], t.hot2[:], wide(t.w2), ALU.mult)
                nc.vector.drain()

                def make_masks(base):
                    for i in range(HT):
                        dve.wait_ge(mk_turned, base + i)
                        nc.vector.tensor_copy(mk.rearrange("p (e r) -> p e r", r=R1),
                                              hots[:, i].rearrange("p k e -> p (k e)").unsqueeze(2)
                                              .to_broadcast([P, 4 * E1, R1])).then_inc(mk_made, 1)

                make_masks(h * 2 * HT)
                dve.wait_ge(mask_copied, h * 2 * HT + HT + 1)
                for c in range(CH):
                    for i, src in enumerate((g_ps[1], u_ps[1])):
                        dve.wait_ge(a_ready, 2 * (h * CH + c) + i + 1)
                        for k in range(2):
                            job = 4 * (h * CH + c) + 2 * i + k
                            nc.vector.scalar_tensor_tensor(out=work[:, 2 * i + k, :], in0=src[:], scalar=SCALING1,
                                                           in1=maskT[:, k, c * S:(c + 1) * S], op0=ALU.mult,
                                                           op1=ALU.mult).then_inc(a_used, 1)
                    for i in range(2):
                        for k in range(2):
                            job = 4 * (h * CH + c) + 2 * i + k
                            dve.wait_ge(am_.hi_done, job + 1)
                            nc.vector.tensor_tensor(am[:, i, k, LO, c * S:(c + 1) * S], work[:, 2 * i + k, :],
                                                    fp32(am[:, i, k, HI, c * S:(c + 1) * S]), ALU.subtract).then_inc(am_.split, 1)
                    dve.wait_ge(am_.split, 4 * (h * CH + c) + 4)

                def add_down(step, c, i):
                    dve.wait_ge(y_ready, step * USES + i + 1)
                    at = ds(h * HT + c * TPB + i, 1)
                    nc.vector.tensor_tensor(x[:, at, :], ring(c, i)[:].rearrange("p (a c) -> p a c", a=1), x[:, at, :],
                                            ALU.add).then_inc(y_added, 1)

                def add_down_lora(step, c, k):
                    dve.wait_ge(y_ready, step * USES + TPB + k + 1)
                    acc = down_acc[:, k, c * S:(c + 1) * S]
                    nc.vector.tensor_tensor(acc, ring(c, TPB + k)[:], acc, ALU.add).then_inc(y_added, 1)

                def tile(f, s, first, last):
                    for c in range(CH):
                        step = h * STEPS + f * CH + c
                        before = (step - 1, 1 - c)
                        has_before = not (first and c == 0)

                        def hidden(var):
                            dve.wait_ge(silu_done, 3 * step + var + 1)
                            dve.wait_ge(up_ready, 3 * step + var + 1)
                            nc.vector.tensor_tensor(hid(c, var), hid(c, var), u_ps[c][:], ALU.mult).then_inc(hid_done, 1)

                        if not last:
                            prep(h, f + 1, 1 - s, 2 * c)
                        hidden(0)
                        if has_before:
                            for i in range(TPB):
                                add_down(*before, i)
                        hidden(1)
                        if not last:
                            prep(h, f + 1, 1 - s, 2 * c + 1)
                        if has_before:
                            for k in range(2):
                                add_down_lora(*before, k)
                        hidden(2)

                tiles(dve, h, tile)
                end = (h * STEPS + STEPS - 1, CH - 1)
                for i in range(TPB):
                    add_down(*end, i)
                for k in range(2):
                    add_down_lora(*end, k)
                dve.wait_ge(hid_split, 3 * (h + 1) * STEPS + 3)
                make_masks(h * 2 * HT + HT)
                dve.wait_ge(mask_copied, h * 2 * HT + 2 * HT + 1)
                dve.wait_ge(y_added, (h + 1) * STEPS * USES + 2)
                nc.vector.tensor_tensor(down_acc[:, 0, :], down_acc[:, 0, :], maskT[:, 0, :], ALU.mult)
                nc.vector.tensor_tensor(down_acc[:, 1, :], down_acc[:, 1, :], maskT[:, 1, :], ALU.mult)
                nc.vector.drain()
                nc.vector.tensor_tensor(down_acc[:, 0, :], down_acc[:, 0, :], down_acc[:, 1, :], ALU.add).then_inc(z_ready, 1)
                dve.wait_ge(z_hi, h + 1)
                nc.vector.tensor_tensor(am[:, 0, 0, LO, :], down_acc[:, 0, :], fp32(am[:, 0, 0, HI, :]), ALU.subtract).then_inc(z_split, 1)
                for i in range(HT):
                    dve.wait_ge(z_out, h * HT + i + 1)
                    at = h * HT + i
                    nc.vector.scalar_tensor_tensor(out=x[:, ds(at, 1), :], in0=y_ps[i % 2][:].rearrange("p (a c) -> p a c", a=1),
                                                   scalar=SCALING1, in1=x[:, ds(at, 1), :], op0=ALU.mult, op1=ALU.add).then_inc(z_added, 1)
                dve.wait_ge(z_added, (h + 1) * HT)


def program(nc, io):
    with nc.sbuf_tensor("x_tokens", [P, TILES, D], FP32) as x, nc.sbuf_tensor("identity", [P, P], FP32) as ident:
        phase_attention0(nc, io, x, ident)
        phase_moe0(nc, io, x, ident)
        phase_rope1(nc, io, x, ident)
        phase_ffn1(nc, io, x, ident)


_INS = ["x", "ctx_1024", "fside_BxSx2_0", "L0_xattn_Wq", "L0_xattn_bq", "L0_xattn_Wk", "L0_xattn_bk",
        "L0_ffn_gate_w", "L0_ffn_gate_proj", "L0_ffn_up_proj", "L0_ffn_down_proj",
        "L1_xattn_Wq", "L1_xattn_Wkv", "L1_xattn_Wout", "L1_xattn_bout",
        "L1_ffn_Wg", "L1_ffn_Wu", "L1_ffn_Wd", "L1_ffn_Wr", "L1_ffn_Ag", "L1_ffn_Bg", "L1_ffn_Au", "L1_ffn_Bu",
        "L1_ffn_Ad", "L1_ffn_Bd"]
_OUT = ((4, 512, 512), "float32")


def kernel(**inputs):
    import numpy as _np
    import concourse.bacc as _bacc
    from concourse import mybir as _mybir
    from concourse.bass_utils import run_bass_kernel_spmd as _run

    nc = _bacc.Bacc("TRN2", target_bir_lowering=False, num_devices=1)
    arrays, io = {}, {}
    for name in _INS:
        a = _np.ascontiguousarray(inputs[name])
        arrays[f"in_{name}"] = a
        io[name] = nc.dram_tensor(f"in_{name}", a.shape, _mybir.dt.from_np(a.dtype), kind="ExternalInput").ap()
    shape, dtype = _OUT
    io["out"] = nc.dram_tensor("out_0", shape, _mybir.dt.from_np(_np.dtype(dtype)), kind="ExternalOutput").ap()
    program(nc, io)
    r = _run(nc, [arrays], core_ids=[0])
    return r.results[0]["out_0"]
```

```python
import numpy as np

import concourse.bass as bass
from concourse import mybir

FP32 = mybir.dt.float32
FP32R = mybir.dt.float32r
ALU = mybir.AluOpType
ACT = mybir.ActivationFunctionType
AXIS_X = mybir.AxisListType.X

P = 128
B, S, D = 4, 512, 512
TOKENS = B * S
TILES = TOKENS // P
TPB = S // P
DK = D // P
CTX = 256
CK = CTX // P
QK0 = 128
EPS = 1e-5
DMA = 16

E0, F0 = 8, 352
FW0 = [128, 128, 96]
E1, R1, DFF = 8, 16, 1408
SCALING1 = 2.0

HEADS, HD = 32, 16
ROPE_BASE = 10000.0
HI, LO = 0, 1


def ds(start, size):
    return bass.ds(start, size)


def fp32(ap):
    return ap.bitcast(FP32)


def product(nc, out, pairs):
    passes = [(l[a], r[b]) for l, r in pairs for a, b in ((HI, HI), (HI, LO), (LO, HI))]
    last = None
    for i, (l, r) in enumerate(passes):
        last = nc.tensor.matmul(out, l, r, start=(i == 0), stop=(i == len(passes) - 1))
    return last


def add_product(nc, out, l, r, start=False):
    last = None
    for i, (a, b) in enumerate(((HI, HI), (HI, LO), (LO, HI))):
        last = nc.tensor.matmul(out, l[a], r[b], start=(start and i == 0), stop=True, skip_group_check=True)
    return last


class TokenNorm:

    def __init__(self, nc, ctx, tag, stats):
        sb = lambda name, shape: ctx.enter_context(nc.sbuf_tensor(f"{tag}_{name}", shape, FP32))
        self.stats = stats
        self.moments = sb("moments", [P, TILES, 2])
        self.var, self.std, self.rstd = (sb(name, [P, TILES]) for name in ("var", "std", "rstd"))
        sem = lambda name: ctx.enter_context(nc.semaphore(f"{tag}_{name}"))
        self.var_ready = sem("var_ready")
        self.std_ready = sem("std_ready")
        self.xn_ready = sem("xn_ready")


def tile_stats(nc, stats, x, tile):
    nc.vector.bn_stats(stats[:, ds(tile, 1), :].rearrange("p t s -> p (t s)"),
                       x[:, ds(tile, 1), :].rearrange("p t d -> p (t d)"))


def token_var(nc, n):
    for t in range(TILES):
        nc.vector.bn_aggr(n.moments[:, t, :], n.stats[:, t, :])
    nc.vector.drain()
    nc.vector.tensor_scalar_add(n.var[:], n.moments[:, :, 1], EPS).then_inc(n.var_ready, 1)


def token_rstd(nc, dve, n):
    dve.wait_ge(n.std_ready, 1)
    nc.vector.reciprocal(n.rstd[:], n.std[:])
    nc.vector.drain()


def token_std(nc, act, n):
    act.wait_ge(n.var_ready, 1)
    nc.scalar.activation(n.std[:], n.var[:], ACT.Sqrt).then_inc(n.std_ready, 1)


def normalise_tile(nc, n, x, tile, out):
    nc.vector.tensor_scalar(out.rearrange("p (t d) -> p t d", t=1), x[:, ds(tile, 1), :], n.moments[:, ds(tile, 1), 0],
                            n.rstd[:, ds(tile, 1)], ALU.subtract, ALU.mult).then_inc(n.xn_ready, 1)


class Split:

    def __init__(self, nc, ctx, tag):
        sem = lambda name: ctx.enter_context(nc.semaphore(f"{tag}_{name}"))
        self.filled = sem("filled")
        self.hi_done = sem("hi_done")
        self.split = sem("split")


def split_hi(nc, act, s, job, hi, psum):
    act.wait_ge(s.filled, job + 1)
    nc.scalar.activation(hi, psum, ACT.Copy).then_inc(s.hi_done, 1)


def split_lo(nc, dve, s, job, lo, psum, hi):
    dve.wait_ge(s.hi_done, job + 1)
    nc.vector.tensor_tensor(lo, psum, fp32(hi), ALU.subtract).then_inc(s.split, 1)


def transposes(nc, s, bank, ins, ident):
    last = None
    at = 0
    for a in ins:
        rows, cols = a.shape[0], a.shape[1]
        last = nc.tensor.transpose(bank[0:cols, at:at + rows], a, ident[0:rows, 0:rows])
        at += rows
    last.then_inc(s.filled, 1)


def phase_attention0(nc, io, x, ident, stats):
    from contextlib import ExitStack
    x_dram = io["x"].rearrange("b (t p) d -> p (b t) d", p=P)
    ctx_dram = io["ctx_1024"].rearrange("b (t p) c -> p (b t) c", p=P)
    with ExitStack() as ctx:
        def sb(name, shape, dt=FP32):
            return ctx.enter_context(nc.sbuf_tensor(f"a0_{name}", shape, dt))

        def ps(name, shape):
            return ctx.enter_context(nc.psum_tensor(f"a0_{name}", shape, FP32))

        def sem(name):
            return ctx.enter_context(nc.semaphore(f"a0_{name}"))

        wq_raw = sb("wq_raw", [P, CTX])
        wk_raw = sb("wk_raw", [P, CTX])
        bias = sb("bias", [P, 2])
        wT = sb("wT", [P, 2, 2, CK, P], FP32R)
        ctx_raw = sb("ctx_raw", [P, TPB, CTX])
        ctxT = sb("ctxT", [P, 2, CK, S], FP32R)
        xnT = sb("xnT", [P, 2, DK, S], FP32R)
        qkT = sb("qkT", [P, 2, 2, S], FP32R)
        att = sb("att", [P, TPB, S])
        attT = sb("attT", [P, 2, DK, S], FP32R)
        rowmax = sb("rowmax", [P, TPB])
        negmax = sb("negmax", [P, TPB])
        rowsum = sb("rowsum", [P, TPB])
        rinv = sb("rinv", [P, TPB])
        stats_in = sb("stats_in", [P, TPB, 6])
        moments = sb("moments", [P, TPB, 2])
        var, std, rstd, shift = (sb(name, [P, TPB]) for name in ("var", "std", "rstd", "shift"))
        xn = sb("xn", [P, TPB, D])
        tp = [ps(f"tp{i}", [P, S]) for i in range(2)]
        mm = [ps(f"mm{i}", [P, S]) for i in range(2)]
        en = [ps(f"en{i}", [P, S]) for i in range(TPB)]
        t_ = Split(nc, ctx, "a0t")
        qk_ = Split(nc, ctx, "a0qk")
        w_in, x_in, ctx_in = sem("w_in"), sem("x_in"), sem("ctx_in")
        energy_ready, negmax_ready, exp_ready, att_ready = (
            sem("energy_ready"), sem("negmax_ready"), sem("exp_ready"), sem("att_ready"))
        mix_ready, x_added = sem("mix_ready"), sem("x_added")
        var_ready, std_ready, rstd_ready, xn_ready, rinv_ready = (
            sem("var_ready"), sem("std_ready"), sem("rstd_ready"), sem("xn_ready"), sem("rinv_ready"))
        ident_ready = sem("ident_ready")
        FIRST_JOBS, JOBS = 1 + CK, 2 * TPB + CK
        block = ctx.enter_context(nc.Block())

        def bank(job_in_batch):
            return tp[(FIRST_JOBS + job_in_batch) % 2]

        def by_block(psum):
            return psum[:].rearrange("p (k c) -> p k c", k=DK)

        @block.gpsimd
        def _(pool):
            nc.gpsimd.memset(ident[:], 0.0).then_inc(ident_ready, 1)
            pool.wait_ge(ident_ready, 1)
            nc.gpsimd.affine_select(out=ident[:], in_=ident[:], compare_op=ALU.not_equal, fill=1.0, base=0,
                                    pattern=[[-1, P]], channel_multiplier=1).then_inc(ident_ready, 1)

        @block.sync
        def _(sp):
            sp.dma_start(wq_raw[:], io["L0_xattn_Wq"]).then_inc(w_in, DMA)
            sp.dma_start(wk_raw[:], io["L0_xattn_Wk"]).then_inc(w_in, DMA)
            sp.dma_start(bias[:, 0:1], io["L0_xattn_bq"].rearrange("(p a) -> p a", a=1)).then_inc(w_in, DMA)
            sp.dma_start(bias[:, 1:2], io["L0_xattn_bk"].rearrange("(p a) -> p a", a=1)).then_inc(w_in, DMA)

            def load_x(b):
                sp.dma_start(x[:, ds(b * TPB, TPB), :], x_dram[:, ds(b * TPB, TPB), :]).then_inc(x_in, DMA)

            def load_context(b):
                sp.dma_start(ctx_raw[:], ctx_dram[:, ds(b * TPB, TPB), :]).then_inc(ctx_in, DMA)

            load_context(0)
            load_x(0)
            sp.wait_ge(x_in, DMA)
            load_x(1)
            sp.wait_ge(t_.filled, FIRST_JOBS)
            load_context(1)
            with sp.Fori(2, B) as b:
                sp.wait_ge(x_in, b * DMA)
                load_x(b)
                sp.wait_ge(t_.filled, FIRST_JOBS + (b - 2) * JOBS + CK)
                load_context(b)

        @block.tensor
        def _(pe):
            def context(job, psum, b):
                pe.wait_ge(ctx_in, DMA * (b + 1))
                for k in range(CK):
                    pe.wait_ge(t_.split, job + k)
                    transposes(nc, t_, psum[k], [ctx_raw[:, t, k * P:(k + 1) * P] for t in range(TPB)], ident)

            def query_key(job, b, i):
                if i == 0:
                    pe.wait_ge(t_.split, job + 1)
                    if not isinstance(b, int):
                        pe.wait_ge(x_added, (b - 1) * TPB)
                product(nc, mm[i][:], [([wT[:, h, i, k, :] for h in (HI, LO)],
                                        [ctxT[:, h, k, :] for h in (HI, LO)]) for k in range(CK)]
                        ).then_inc(qk_.filled, 1)

            def energy(b):
                pe.wait_ge(qk_.split, 2 * b + 2)
                pe.wait_ge(exp_ready, b * TPB)
                for m in range(TPB):
                    product(nc, en[m][:], [([qkT[:, h, 0, m * P:(m + 1) * P] for h in (HI, LO)],
                                            [qkT[:, h, 1, :] for h in (HI, LO)])]).then_inc(energy_ready, 1)

            def batch(b, last):
                job = FIRST_JOBS + b * JOBS
                ahead = 0 if last else CK
                if not last:
                    context(job, [bank(k) for k in range(CK)], b + 1)
                for t in range(TPB):
                    pe.wait_ge(xn_ready, b * TPB + t + 1)
                    pe.wait_ge(t_.split, job + ahead + t)
                    transposes(nc, t_, bank(ahead + t), [xn[:, t, k * P:(k + 1) * P] for k in range(DK)], ident)
                    if t % 2 and not last:
                        query_key(job + CK, b + 1, t // 2)
                for m in range(TPB):
                    at = ahead + TPB + m
                    pe.wait_ge(att_ready, b * TPB + m + 1)
                    pe.wait_ge(t_.split, job + at)
                    transposes(nc, t_, bank(at), [att[:, m, k * P:(k + 1) * P] for k in range(DK)], ident)
                if not last:
                    energy(b + 1)
                pe.wait_ge(t_.split, job + ahead + 2 * TPB + 1)
                for t in range(TPB):
                    if t >= 2:
                        pe.wait_ge(x_added, b * TPB + t - 1)
                    product(nc, mm[t % 2][:], [([xnT[:, h, k, t * P:(t + 1) * P] for h in (HI, LO)],
                                                [attT[:, h, k, :] for h in (HI, LO)]) for k in range(DK)]
                            ).then_inc(mix_ready, 1)

            pe.wait_ge(ident_ready, 2)
            pe.wait_ge(w_in, 4 * DMA)
            transposes(nc, t_, tp[0], [w[:, k * P:(k + 1) * P] for w in (wq_raw, wk_raw) for k in range(CK)], ident)
            context(1, [tp[(1 + k) % 2] for k in range(CK)], 0)
            for i in range(2):
                query_key(FIRST_JOBS, 0, i)
            energy(0)
            with pe.Fori(0, B - 1) as b:
                batch(b, False)
            pe.wait_ge(x_added, (B - 1) * TPB)
            batch(B - 1, True)

        @block.scalar
        def _(act):
            def context(job, psum):
                for k in range(CK):
                    split_hi(nc, act, t_, job + k, ctxT[:, HI, k, :], psum[k][:])

            def query_key(b, i):
                act.wait_ge(qk_.filled, 2 * b + i + 1)
                nc.scalar.activation(qkT[:, HI, i, :], mm[i][:], ACT.Identity,
                                     bias=bias[:, i:i + 1]).then_inc(qk_.hi_done, 1)

            def softmax_and_norm(b):
                for m in range(TPB):
                    act.wait_ge(negmax_ready, b * TPB + m + 1)
                    nc.scalar.activation(att[:, m, :], en[m][:], ACT.Exp, bias=negmax[:, m:m + 1],
                                         accum_out=rowsum[:, m:m + 1]).then_inc(exp_ready, 1)
                act.wait_ge(var_ready, b + 1)
                nc.scalar.activation(std[:], var[:], ACT.Sqrt).then_inc(std_ready, 1)
                act.wait_ge(rstd_ready, b + 1)
                for t in range(TPB):
                    nc.scalar.activation(xn[:, t, :].rearrange("p (a d) -> p a d", a=1), x[:, ds(b * TPB + t, 1), :],
                                         ACT.Identity, bias=shift[:, t:t + 1], scale=rstd[:, t:t + 1]).then_inc(xn_ready, 1)
                act.wait_ge(rinv_ready, b + 1)
                for m in range(TPB):
                    nc.scalar.activation(att[:, m, :], att[:, m, :], ACT.Copy, scale=rinv[:, m:m + 1]).then_inc(att_ready, 1)

            def batch(b, last):
                job = FIRST_JOBS + b * JOBS
                ahead = 0 if last else CK
                if not last:
                    context(job, [bank(k) for k in range(CK)])
                for t in range(TPB):
                    split_hi(nc, act, t_, job + ahead + t, xnT[:, HI, :, t * P:(t + 1) * P], by_block(bank(ahead + t)))
                    if t % 2 and not last:
                        query_key(b + 1, t // 2)
                for m in range(TPB):
                    at = ahead + TPB + m
                    split_hi(nc, act, t_, job + at, attT[:, HI, :, m * P:(m + 1) * P], by_block(bank(at)))
                if not last:
                    softmax_and_norm(b + 1)

            split_hi(nc, act, t_, 0, wT[:, HI].rearrange("p a k c -> p (a k c)"), tp[0][:])
            context(1, [tp[(1 + k) % 2] for k in range(CK)])
            for i in range(2):
                query_key(0, i)
            softmax_and_norm(0)
            with act.Fori(0, B - 1) as b:
                batch(b, False)
            batch(B - 1, True)

        @block.vector
        def _(dve):
            def context(job, psum):
                for k in range(CK):
                    split_lo(nc, dve, t_, job + k, ctxT[:, LO, k, :], psum[k][:], ctxT[:, HI, k, :])

            def query_key(b, i):
                dve.wait_ge(qk_.hi_done, 2 * b + i + 1)
                nc.vector.scalar_tensor_tensor(out=qkT[:, LO, i, :], in0=mm[i][:], scalar=bias[:, i:i + 1],
                                               in1=fp32(qkT[:, HI, i, :]), op0=ALU.add,
                                               op1=ALU.subtract).then_inc(qk_.split, 1)

            def maxima(b):
                for m in range(TPB):
                    dve.wait_ge(energy_ready, b * TPB + m + 1)
                    nc.vector.reduce_max(rowmax[:, m:m + 1], en[m][:], AXIS_X)
                    nc.vector.drain()
                    nc.vector.tensor_scalar(negmax[:, m:m + 1], rowmax[:, m:m + 1], -1.0, None,
                                            ALU.mult).then_inc(negmax_ready, 1)

            def sums(b):
                dve.wait_ge(exp_ready, (b + 1) * TPB)
                nc.vector.reciprocal(rinv[:], rowsum[:]).then_inc(rinv_ready, 1)

            def variances(b):
                dve.wait_ge(x_in, DMA * (b + 1))
                for t in range(TPB):
                    nc.vector.bn_stats(stats_in[:, t, :], x[:, ds(b * TPB + t, 1), :].rearrange("p a d -> p (a d)"))
                nc.vector.drain()
                for t in range(TPB):
                    nc.vector.bn_aggr(moments[:, t, :], stats_in[:, t, :])
                nc.vector.drain()
                nc.vector.tensor_scalar_add(var[:], moments[:, :, 1], EPS).then_inc(var_ready, 1)

            def reciprocals(b):
                dve.wait_ge(std_ready, b + 1)
                nc.vector.reciprocal(rstd[:], std[:])
                nc.vector.drain()
                nc.vector.scalar_tensor_tensor(out=shift[:], in0=moments[:, :, 0], scalar=-1.0, in1=rstd[:],
                                               op0=ALU.mult, op1=ALU.mult).then_inc(rstd_ready, 1)

            def final_stats(b, t):
                dve.wait_ge(x_added, b * TPB + t + 1)
                tile_stats(nc, stats, x, b * TPB + t)

            def batch(b, last):
                job = FIRST_JOBS + b * JOBS
                ahead = 0 if last else CK
                if not last:
                    context(job, [bank(k) for k in range(CK)])
                for t in range(TPB):
                    split_lo(nc, dve, t_, job + ahead + t, xnT[:, LO, :, t * P:(t + 1) * P], by_block(bank(ahead + t)),
                             xnT[:, HI, :, t * P:(t + 1) * P])
                    if t % 2 and not last:
                        query_key(b + 1, t // 2)
                for m in range(TPB):
                    at = ahead + TPB + m
                    split_lo(nc, dve, t_, job + at, attT[:, LO, :, m * P:(m + 1) * P], by_block(bank(at)),
                             attT[:, HI, :, m * P:(m + 1) * P])
                if not last:
                    maxima(b + 1)
                    variances(b + 1)
                for t in range(TPB):
                    dve.wait_ge(mix_ready, b * TPB + t + 1)
                    tile = x[:, ds(b * TPB + t, 1), :]
                    nc.vector.tensor_tensor(tile, mm[t % 2][:].rearrange("p (a c) -> p a c", a=1), tile,
                                            ALU.add).then_inc(x_added, 1)
                    if t == 0 and not last:
                        reciprocals(b + 1)
                        sums(b + 1)
                    if t:
                        final_stats(b, t - 1)
                final_stats(b, TPB - 1)

            dve.sem_inc(t_.split, 1)
            split_lo(nc, dve, t_, 0, wT[:, LO].rearrange("p a k c -> p (a k c)"), tp[0][:],
                     wT[:, HI].rearrange("p a k c -> p (a k c)"))
            context(1, [tp[(1 + k) % 2] for k in range(CK)])
            variances(0)
            for i in range(2):
                query_key(0, i)
            maxima(0)
            reciprocals(0)
            sums(0)
            with dve.Fori(0, B - 1) as b:
                batch(b, False)
            batch(B - 1, True)


def top_two(nc, dve, logits, rev, t):
    def wide(a):
        return a[:].unsqueeze(2).to_broadcast(list(logits.shape))

    for source, top, hot in ((logits, t.top1, t.hot1), (t.rest, t.top2, t.hot2)):
        nc.vector.reduce_max(top[:], source[:], AXIS_X)
        nc.vector.drain()
        nc.vector.tensor_tensor(t.score[:], source[:], wide(top), ALU.is_equal)
        nc.vector.drain()
        nc.vector.tensor_tensor(t.score[:], t.score[:], rev[:], ALU.mult)
        nc.vector.drain()
        nc.vector.reduce_max(t.best[:], t.score[:], AXIS_X)
        nc.vector.drain()
        nc.vector.tensor_tensor(hot[:], t.score[:], wide(t.best), ALU.is_equal)
        nc.vector.drain()
        if source is logits:
            nc.vector.scalar_tensor_tensor(out=t.rest[:], in0=hot[:], scalar=-3e38, in1=logits[:],
                                           op0=ALU.mult, op1=ALU.add)
            nc.vector.drain()


class TopTwo:
    def __init__(self, nc, ctx, tag, tiles, experts):
        def sb(name, shape):
            return ctx.enter_context(nc.sbuf_tensor(f"{tag}_{name}", shape, FP32))
        self.score, self.rest, self.hot1, self.hot2 = (
            sb(name, [P, tiles, experts]) for name in ("score", "rest", "hot1", "hot2"))
        self.top1, self.top2, self.best, self.gap, self.e, self.w1, self.w2, self.den = (
            sb(name, [P, tiles]) for name in ("top1", "top2", "best", "gap", "e", "w1", "w2", "den"))


def phase_moe0(nc, io, x, ident, stats):
    from contextlib import ExitStack
    gate_dram, up_dram, down_dram = io["L0_ffn_gate_proj"], io["L0_ffn_up_proj"], io["L0_ffn_down_proj"]
    NF = len(FW0)
    NB = B
    STEPS = NF * NB
    PREP = 3
    JOBS = NF * PREP
    with ExitStack() as ctx:
        def sb(name, shape, dt=FP32):
            return ctx.enter_context(nc.sbuf_tensor(f"m_{name}", shape, dt))

        def ps(name, shape):
            return ctx.enter_context(nc.psum_tensor(f"m_{name}", shape, FP32))

        def sem(name):
            return ctx.enter_context(nc.semaphore(f"m_{name}"))

        xnT = sb("xnT", [P, 2, DK, TOKENS], FP32R)
        gw_raw = sb("gw_raw", [E0, D])
        gwT = sb("gwT", [P, 2, DK, E0], FP32R)
        rl = sb("rl", [P, S])
        logits = sb("logits", [P, TILES, E0])
        rev = sb("rev", [P, TILES, E0])
        weight = sb("weight", [P, TILES, E0])
        gate_raw = [sb(f"gate_raw{j}", [P, D]) for j in range(NF)]
        up_raw = [sb(f"up_raw{j}", [P, D]) for j in range(NF)]
        down_raw = [sb(f"down_raw{j}", [P, DK, P]) for j in range(NF)]
        gateT = [sb(f"gateT{j}", [P, 2, DK, P], FP32R) for j in range(NF)]
        upT = [sb(f"upT{j}", [P, 2, DK, P], FP32R) for j in range(NF)]
        downT = [sb(f"downT{j}", [P, 2, D], FP32R) for j in range(NF)]
        silu = [sb(f"silu{i}", [P, S]) for i in range(2)]
        hid = [sb(f"hid{i}", [P, S]) for i in range(2)]
        hidS = [sb(f"hidS{i}", [P, 2, S], FP32R) for i in range(2)]
        n = TokenNorm(nc, ctx, "mn", stats)
        xn = sb("xn", [P, TPB, D])
        t = TopTwo(nc, ctx, "mt", TILES, E0)
        g_ps = [ps(f"g{i}", [P, S]) for i in range(2)]
        u_ps = [ps(f"u{i}", [P, S]) for i in range(2)]
        y_ps = [ps(f"y{i}", [P, D]) for i in range(3)]
        prep_ps = ps("prep", [P, D])
        prep_ = Split(nc, ctx, "mp")
        xt_ = Split(nc, ctx, "mx")
        gw_in = sem("gw_in")
        raw_in = [sem(f"raw_in{j}") for j in range(NF)]
        router_ready, router_copied, logits_ready, logits_done = (
            sem("router_ready"), sem("router_copied"), sem("logits_ready"), sem("logits_done"))
        gap_ready, gap_exp, rl_clear = sem("gap_ready"), sem("gap_exp"), sem("rl_clear")
        gate_ready, up_ready, silu_done, hid_done, hid_hi, hid_split = (
            sem("gate_ready"), sem("up_ready"), sem("silu_done"), sem("hid_done"), sem("hid_hi"), sem("hid_split"))
        y_ready, y_added = sem("y_ready"), sem("y_added")
        block = ctx.enter_context(nc.Block())

        def prep_views(j, part, bank=prep_ps):
            f = FW0[j]
            if part < 2:
                raw, to = ((gate_raw, gateT), (up_raw, upT))[part]
                return ([raw[j][0:f, k * P:(k + 1) * P] for k in range(DK)],
                        bank[:, 0:DK * f].rearrange("p (k c) -> p k c", k=DK),
                        [to[j][:, h, :, 0:f] for h in (HI, LO)])
            return ([down_raw[j][:, k, 0:f] for k in range(DK)], bank[0:f, :],
                    [downT[j][0:f, h, :] for h in (HI, LO)])

        def first_bank(job):
            return (prep_ps, u_ps[0])[job % 2]

        def prep_job(e, j, c):
            return 2 * PREP + e * JOBS + j * PREP + c, (j + 2) % NF

        @block.sync
        def _(sp):
            def load(e, j):
                f0, f = sum(FW0[:j]), FW0[j]
                sp.dma_start(gate_raw[j][0:f, :], gate_dram[ds(e, 1), f0:f0 + f, :].rearrange("e f d -> (e f) d")).then_inc(raw_in[j], DMA)
                sp.dma_start(up_raw[j][0:f, :], up_dram[ds(e, 1), f0:f0 + f, :].rearrange("e f d -> (e f) d")).then_inc(raw_in[j], DMA)
                sp.dma_start(down_raw[j][:, :, 0:f], down_dram[ds(e, 1), :, f0:f0 + f]
                             .rearrange("e (k p) f -> p (e k) f", p=P)).then_inc(raw_in[j], DMA)

            sp.dma_start(gw_raw[:], io["L0_ffn_gate_w"]).then_inc(gw_in, DMA)
            for j in range(NF):
                load(0, j)
            with sp.Fori(1, E0) as e:
                for j in range(NF):
                    sp.wait_ge(prep_.filled, (e - 1) * JOBS + (j + 1) * PREP)
                    load(e, j)

        @block.tensor
        def _(pe):
            def prep(job, j, part):
                pe.wait_ge(prep_.split, job)
                transposes(nc, prep_, prep_ps, prep_views(j, part)[0], ident)

            def tile(b, k):
                pe.wait_ge(n.xn_ready, b * TPB + k + 1)
                pe.wait_ge(xt_.split, b * TPB + k + 1)
                transposes(nc, xt_, y_ps[(k + 1) % 2], [xn[:, k, i * P:(i + 1) * P] for i in range(DK)], ident)

            def router(b, k):
                if k == 0:
                    pe.wait_ge(xt_.split, b * TPB + TPB + 2)
                    pe.wait_ge(router_copied, b)
                last = add_product(nc, g_ps[0][0:E0, :], [gwT[:, h, k, :] for h in (HI, LO)],
                                   [xnT[:, h, k, ds(b * S, S)] for h in (HI, LO)], start=(k == 0))
                if k == DK - 1:
                    last.then_inc(router_ready, 1)

            def turn_logits(b):
                pe.wait_ge(router_copied, b + 1)
                pe.wait_ge(logits_done, b)
                last = None
                for k in range(TPB):
                    last = nc.tensor.transpose(g_ps[1][:, k * P:(k + 1) * P], rl[:, k * P:(k + 1) * P], ident[:])
                last.then_inc(logits_ready, 1)

            pe.wait_ge(gw_in, DMA)
            transposes(nc, xt_, y_ps[0], [gw_raw[:, k * P:(k + 1) * P] for k in range(DK)], ident)
            for k in range(TPB):
                tile(0, k)
            with pe.Fori(1, NB) as b:
                for k in range(TPB - 1):
                    tile(b, k)
                    router(b - 1, k)
                router(b - 1, DK - 1)
                tile(b, TPB - 1)
                turn_logits(b - 1)
            for k in range(DK):
                router(NB - 1, k)
            for j in range(2):
                pe.wait_ge(raw_in[j], 3 * DMA)
                for part in range(PREP):
                    job = j * PREP + part
                    if job >= 2:
                        pe.wait_ge(prep_.split, job - 1)
                    transposes(nc, prep_, first_bank(job), prep_views(j, part)[0], ident)
            turn_logits(NB - 1)
            pe.wait_ge(logits_done, NB)

            def down(step, j, c):
                pe.wait_ge(hid_split, step + 1)
                f = FW0[j]
                for i in range(TPB):
                    pe.wait_ge(y_added, step * TPB + i)
                    at = ((j * NB + c) * TPB + i) % 3
                    product(nc, y_ps[at][:], [([hidS[c % 2][0:f, h, i * P:(i + 1) * P] for h in (HI, LO)],
                                               [downT[j][0:f, h, :] for h in (HI, LO)])]).then_inc(y_ready, 1)

            def expert(e, last):
                for j in range(NF):
                    f = FW0[j]
                    pe.wait_ge(prep_.split, e * JOBS + (j + 1) * PREP)
                    for c in range(NB):
                        step = e * STEPS + j * NB + c
                        pe.wait_ge(hid_done, step)
                        for to, w, ready in ((g_ps, gateT, gate_ready), (u_ps, upT, up_ready)):
                            product(nc, to[c % 2][0:f, :], [([w[j][:, h, k, 0:f] for h in (HI, LO)],
                                                            [xnT[:, h, k, c * S:(c + 1) * S] for h in (HI, LO)])
                                                           for k in range(DK)]).then_inc(ready, 1)
                        if (j, c) != (0, 0):
                            down(step - 1, *((j, c - 1) if c else (j - 1, NB - 1)))
                        if c < PREP and not (last and j > 0):
                            job, slot = prep_job(e, j, c)
                            if c == 0:
                                pe.wait_ge(raw_in[slot], (e + 1 + (j > 0)) * 3 * DMA)
                            prep(job, slot, c)
                down(e * STEPS + STEPS - 1, NF - 1, NB - 1)

            with pe.Fori(0, E0 - 1) as e:
                expert(e, False)
            expert(E0 - 1, True)

        @block.scalar
        def _(act):
            def prep(job, j, part, bank=prep_ps):
                _, psum, (hi, lo) = prep_views(j, part, bank)
                split_hi(nc, act, prep_, job, hi, psum)

            def tile(b, k):
                split_hi(nc, act, xt_, 1 + b * TPB + k, xnT[:, HI, :, ds((b * TPB + k) * P, P)],
                         y_ps[(k + 1) % 2][:].rearrange("p (k c) -> p k c", k=DK))

            def copy_router(b):
                act.wait_ge(router_ready, b + 1)
                nc.scalar.activation(rl[0:E0, :], g_ps[0][0:E0, :], ACT.Copy).then_inc(router_copied, 1)

            token_std(nc, act, n)
            split_hi(nc, act, xt_, 0, gwT[:, HI].rearrange("p k e -> p (k e)"), y_ps[0][:, 0:DK * E0])
            act.wait_ge(rl_clear, 1)
            for k in range(TPB):
                tile(0, k)
            with act.Fori(1, NB) as b:
                for k in range(TPB - 1):
                    tile(b, k)
                copy_router(b - 1)
                tile(b, TPB - 1)
            copy_router(NB - 1)
            for j in range(2):
                for part in range(PREP):
                    prep(j * PREP + part, j, part, first_bank(j * PREP + part))
            act.wait_ge(gap_ready, 1)
            nc.scalar.activation(t.e[:], t.gap[:], ACT.Exp).then_inc(gap_exp, 1)

            def expert(e, last):
                for j in range(NF):
                    f = FW0[j]
                    for c in range(NB):
                        step = e * STEPS + j * NB + c
                        act.wait_ge(gate_ready, step + 1)
                        act.wait_ge(hid_done, step)
                        nc.scalar.activation(silu[c % 2][0:f, :], g_ps[c % 2][0:f, :], ACT.Silu).then_inc(silu_done, 1)
                        act.wait_ge(hid_done, step + 2)
                        nc.scalar.activation(hidS[c % 2][0:f, HI, :], hid[c % 2][0:f, :], ACT.Copy).then_inc(hid_hi, 1)
                        if c < PREP and not (last and j > 0):
                            job, slot = prep_job(e, j, c)
                            prep(job, slot, c)

            with act.Fori(0, E0 - 1) as e:
                expert(e, False)
            expert(E0 - 1, True)

        @block.vector
        def _(dve):
            def prep(job, j, part, bank=prep_ps):
                _, psum, (hi, lo) = prep_views(j, part, bank)
                split_lo(nc, dve, prep_, job, lo, psum, hi)

            nc.vector.memset(rl[:], 0.0).then_inc(rl_clear, 1)
            dve.sem_inc(xt_.split, 1)
            dve.sem_inc(hid_done, 1)
            dve.sem_inc(y_added, 2)
            for i in range(E0):
                nc.vector.memset(rev[:, :, i:i + 1], float(E0 - i))

            def tiles(b, last=False):
                for k in range(TPB):
                    split_lo(nc, dve, xt_, 1 + b * TPB + k, xnT[:, LO, :, ds((b * TPB + k) * P, P)],
                             y_ps[(k + 1) % 2][:].rearrange("p (k c) -> p k c", k=DK),
                             xnT[:, HI, :, ds((b * TPB + k) * P, P)])
                    if not last:
                        normalise_tile(nc, n, x, (b + 1) * TPB + k, xn[:, k, :])

            def copy_logits(b):
                dve.wait_ge(logits_ready, b + 1)
                nc.vector.tensor_copy(logits[:, ds(b * TPB, TPB), :],
                                      g_ps[1][:].rearrange("p (k e) -> p k e", k=TPB)[:, :, 0:E0]).then_inc(logits_done, 1)

            token_var(nc, n)
            token_rstd(nc, dve, n)
            for k in range(TPB):
                normalise_tile(nc, n, x, k, xn[:, k, :])
            split_lo(nc, dve, xt_, 0, gwT[:, LO].rearrange("p k e -> p (k e)"), y_ps[0][:, 0:DK * E0],
                     gwT[:, HI].rearrange("p k e -> p (k e)"))
            tiles(0)
            with dve.Fori(1, NB - 1) as b:
                tiles(b)
                copy_logits(b - 1)
            tiles(NB - 1, last=True)
            copy_logits(NB - 2)
            for j in range(2):
                for part in range(PREP):
                    prep(j * PREP + part, j, part, first_bank(j * PREP + part))
            copy_logits(NB - 1)
            nc.vector.drain()
            top_two(nc, dve, logits, rev, t)
            nc.vector.tensor_tensor(t.gap[:], t.top2[:], t.top1[:], ALU.subtract).then_inc(gap_ready, 1)
            dve.wait_ge(gap_exp, 1)
            nc.vector.tensor_scalar_add(t.den[:], t.e[:], 1.0)
            nc.vector.drain()
            nc.vector.reciprocal(t.w1[:], t.den[:])
            nc.vector.drain()
            nc.vector.tensor_tensor(t.w2[:], t.e[:], t.w1[:], ALU.mult)
            nc.vector.drain()
            wide = lambda a: a[:].unsqueeze(2).to_broadcast([P, TILES, E0])
            nc.vector.tensor_tensor(t.hot1[:], t.hot1[:], wide(t.w1), ALU.mult)
            nc.vector.tensor_tensor(t.hot2[:], t.hot2[:], wide(t.w2), ALU.mult)
            nc.vector.drain()
            nc.vector.tensor_tensor(weight[:], t.hot1[:], t.hot2[:], ALU.add)
            nc.vector.drain()

            def add(e, step, j, c, i):
                dve.wait_ge(y_ready, step * TPB + i + 1)
                at = ((j * NB + c) * TPB + i) % 3
                tile = c * TPB + i
                nc.vector.scalar_tensor_tensor(
                    out=x[:, tile, :], in0=y_ps[at][:], scalar=weight[:, tile, ds(e, 1)], in1=x[:, tile, :],
                    op0=ALU.mult, op1=ALU.add).then_inc(y_added, 1)

            def chunk_stats(c):
                for i in range(TPB):
                    tile_stats(nc, stats, x, c * TPB + i)

            def expert(e, last):
                for j in range(NF):
                    f = FW0[j]
                    for c in range(NB):
                        step = e * STEPS + j * NB + c
                        before = (step - 1, *((j, c - 1) if c else (j - 1, NB - 1)))
                        first = (j, c) == (0, 0)
                        dve.wait_ge(silu_done, step + 1)
                        dve.wait_ge(up_ready, step + 1)
                        nc.vector.tensor_tensor(hid[c % 2][0:f, :], u_ps[c % 2][0:f, :], silu[c % 2][0:f, :],
                                                ALU.mult).then_inc(hid_done, 1)
                        if not first:
                            add(e, *before, 0)
                        dve.wait_ge(hid_hi, step + 1)
                        nc.vector.tensor_tensor(hidS[c % 2][0:f, LO, :], hid[c % 2][0:f, :],
                                                fp32(hidS[c % 2][0:f, HI, :]), ALU.subtract).then_inc(hid_split, 1)
                        if not first:
                            for i in range(1, TPB):
                                add(e, *before, i)
                        if last and j == NF - 1 and c >= 2:
                            dve.wait_ge(y_added, (step - 1) * TPB + 2)
                            chunk_stats(c - 2)
                        if c < PREP and not (last and j > 0):
                            job, slot = prep_job(e, j, c)
                            prep(job, slot, c)
                for i in range(TPB):
                    add(e, e * STEPS + STEPS - 1, NF - 1, NB - 1, i)
                if last:
                    dve.wait_ge(y_added, E0 * STEPS * TPB + 2)
                    chunk_stats(NB - 2)
                    chunk_stats(NB - 1)

            with dve.Fori(0, E0 - 1) as e:
                expert(e, False)
            expert(E0 - 1, True)


GROUP = 4
GROUPS = B * HEADS // GROUP
QROWS, KROWS = 3 * HD + 2, 3 * HD
PAD = 32


def scratch(nc):
    def dram(name, shape, dt):
        return nc.dram_tensor(name, shape, dt, kind="Internal").ap()
    return {"q": dram("q_stack", [B * HEADS, QROWS, S], FP32),
            "k": dram("k_stack", [B * HEADS, KROWS, S], FP32),
            "v": dram("v_pad", [GROUPS, S, GROUP * PAD], FP32)}


QK_TILES = HEADS * HD // P
STORES = 6 * QK_TILES


class OddBatch:

    def __init__(self, nc, ctx):
        self.qkT = [ctx.enter_context(nc.sbuf_tensor(f"q_qkT{i}1", [P, 2, QK_TILES, S], FP32R)) for i in range(2)]
        self.stored = ctx.enter_context(nc.semaphore("q_odd_stored"))


def store_qk(sp, scr, qkT, batch, stored, which=range(STORES)):
    for j in which:
        i, block_row, ht = j // (3 * QK_TILES), j // QK_TILES % 3, j % QK_TILES
        part = ((HI, HI, LO), (HI, LO, HI))[i][block_row]
        to = scr["qk"[i]][ds(batch * HEADS, HEADS), block_row * HD:(block_row + 1) * HD, :]
        sp.dma_start(to[ht * (P // HD):(ht + 1) * (P // HD)], fp32(qkT[i][:, part, ht, :])).then_inc(stored, DMA)


def phase_qkv1(nc, io, x, ident, stats, odd):
    from contextlib import ExitStack
    io["scratch"] = scr = scratch(nc)
    ctx_dram = io["ctx_1024"].rearrange("b (t p) c -> p (b t) c", p=P)
    pos_dram = io["fside_BxSx2_0"].rearrange("b (t p) a -> p (b t) a", p=P)
    TWO_PI = 2.0 * np.pi
    c1 = float(np.float32(np.floor(TWO_PI * 2 ** 8) / 2 ** 8))
    c2 = float(np.floor((TWO_PI - c1) * 2 ** 20) / 2 ** 20)
    c3 = float(np.float32(TWO_PI - c1 - c2))
    ROUND = 1.5 * 2 ** 23
    PI_F = float(np.nextafter(np.float32(np.pi), np.float32(0)))
    AX, HALF = 2, HD // 4
    FREQS = [float(np.float32(ROPE_BASE) ** np.float32(-j / HALF)) for j in range(HALF)]
    HT = QK_TILES
    with ExitStack() as ctx:
        def sb(name, shape, dt=FP32):
            return ctx.enter_context(nc.sbuf_tensor(f"q_{name}", shape, dt))

        def ps(name, shape):
            return ctx.enter_context(nc.psum_tensor(f"q_{name}", shape, FP32))

        def sem(name):
            return ctx.enter_context(nc.semaphore(f"q_{name}"))

        wq_raw = sb("wq_raw", [P, DK, D])
        wkv_raw = sb("wkv_raw", [P, CK, 2 * D])
        wq = sb("wq", [P, 2, DK, D], FP32R)
        wkv = sb("wkv", [P, 2, CK, 2 * D], FP32R)
        pos = sb("pos", [P, TILES, AX])
        ang, turns, red, mag, sine, cosine, nsine = (
            sb(name, [P, TILES, AX * HALF]) for name in ("ang", "turns", "red", "mag", "sine", "cosine", "nsine"))
        cos2 = sb("cos2", [P, TILES, HD])
        ctx_raw = sb("ctx_raw", [P, 2 * TPB, CTX])
        xn = [sb(f"xn{i}", [P, D]) for i in range(2)]
        xnT = [sb(f"xnT{i}", [P, 2, DK, P], FP32R) for i in range(2)]
        ctxT = [sb(f"ctxT{i}", [P, 2, CK, P], FP32R) for i in range(2)]
        by_cos = [sb(f"by_cos{i}", [P, HEADS, HD]) for i in range(2)]
        by_sin = [sb(f"by_sin{i}", [P, HEADS, HD]) for i in range(2)]
        rot = [sb(f"rot{i}", [P, HEADS * HD]) for i in range(2)]
        qkT = [[sb(f"qkT{i}0", [P, 2, HT, S], FP32R) for i in range(2)], odd.qkT]
        vpad = [sb(f"vpad{i}", [P, HEADS, PAD]) for i in range(2)]
        zeros = sb("zeros", [P, 2, S])
        n = TokenNorm(nc, ctx, "qn", stats)
        in_ps = [ps("xnt", [P, D]), ps("ctxt", [P, S])]
        turn_ps = [ps(f"turn{i}", [P, S]) for i in range(2)]
        qk_ps = [ps("qp", [P, D]), ps("kp", [P, D])]
        v_ps = [ps(f"vp{i}", [P, D]) for i in range(2)]
        in_, turn_ = Split(nc, ctx, "qi"), Split(nc, ctx, "qt")
        w_in, pos_in, ctx_in = sem("w_in"), sem("pos_in"), sem("ctx_in")
        w_hi, w_split, red_ready, trig_ready = sem("w_hi"), sem("w_split"), sem("red_ready"), sem("trig_ready")
        qk_ready, rope_done, rot_done, v_ready, v_copied = (
            sem("qk_ready"), sem("rope_done"), sem("rot_done"), sem("v_ready"), sem("v_copied"))
        pads_set, out_zero = sem("pads_set"), sem("out_zero")
        out_q = [sem("out_q0"), odd.stored]
        out_v = [sem(f"out_v{i}") for i in range(2)]
        PAIR = 2 * TPB
        block = ctx.enter_context(nc.Block())

        @block.sync
        def _(sp):
            sp.dma_start(wq_raw[:], io["L1_xattn_Wq"].rearrange("(k p) n -> p k n", p=P)).then_inc(w_in, DMA)
            sp.dma_start(wkv_raw[:], io["L1_xattn_Wkv"].rearrange("(k p) n -> p k n", p=P)).then_inc(w_in, DMA)
            sp.dma_start(pos[:], pos_dram).then_inc(pos_in, DMA)

            def store(pair, e):
                sp.wait_ge(turn_.split, 2 * (pair * PAIR + (e + 1) * TPB) + 1)
                store_qk(sp, scr, qkT[e], 2 * pair + e, out_q[e])

            store(0, 0)
            with sp.Fori(1, B // 2) as pair:
                store(pair - 1, 1)
                store(pair, 0)
            sp.wait_ge(out_q[0], B // 2 * STORES * DMA)
            for i in range(2):
                sp.wait_ge(out_v[i], TILES // 2 * DMA)
            sp.wait_ge(out_zero, DMA)

        @block.tensor
        def _(pe):
            with pe.Fori(0, B // 2) as pair:
                def inputs(t):
                    tile = pair * PAIR + t
                    pe.wait_ge(n.xn_ready, tile + 1)
                    pe.wait_ge(in_.split, 2 * tile)
                    transposes(nc, in_, in_ps[0], [xn[t % 2][:, k * P:(k + 1) * P] for k in range(DK)], ident)
                    pe.wait_ge(in_.split, 2 * tile + 1)
                    last = None
                    for k in range(CK):
                        last = nc.tensor.transpose(in_ps[1][:, k * P:(k + 1) * P],
                                                   ctx_raw[:, t, k * P:(k + 1) * P], ident[:])
                    last.then_inc(in_.filled, 1)

                def turn(t):
                    for i in range(2):
                        job = 2 * (pair * PAIR + t) + i
                        pe.wait_ge(rot_done, job + 1)
                        pe.wait_ge(turn_.split, job)
                        transposes(nc, turn_, turn_ps[i], [rot[i][:, k * P:(k + 1) * P] for k in range(HT)], ident)

                pe.wait_ge(ctx_in, DMA * (pair + 1))
                inputs(0)
                pe.wait_ge(w_split, 2)
                for t in range(PAIR):
                    tile = pair * PAIR + t
                    if t + 1 < PAIR:
                        inputs(t + 1)
                    pe.wait_ge(in_.split, 2 * tile + 3)
                    pe.wait_ge(rope_done, 2 * tile)
                    product(nc, qk_ps[0][:], [([xnT[t % 2][:, h, k, :] for h in (HI, LO)],
                                               [wq[:, h, k, :] for h in (HI, LO)]) for k in range(DK)]).then_inc(qk_ready, 1)
                    product(nc, qk_ps[1][:], [([ctxT[t % 2][:, h, k, :] for h in (HI, LO)],
                                               [wkv[:, h, k, 0:D] for h in (HI, LO)]) for k in range(CK)]).then_inc(qk_ready, 1)
                    pe.wait_ge(v_copied, tile)
                    product(nc, v_ps[t % 2][:], [([ctxT[t % 2][:, h, k, :] for h in (HI, LO)],
                                                  [wkv[:, h, k, D:2 * D] for h in (HI, LO)]) for k in range(CK)]).then_inc(v_ready, 1)
                    if t:
                        turn(t - 1)
                turn(PAIR - 1)

        @block.scalar
        def _(act):
            act.wait_ge(w_in, 2 * DMA)
            nc.scalar.activation(wq[:, HI], wq_raw[:], ACT.Copy).then_inc(w_hi, 1)
            nc.scalar.activation(wkv[:, HI], wkv_raw[:], ACT.Copy).then_inc(w_hi, 1)
            token_std(nc, act, n)
            act.wait_ge(red_ready, 1)
            nc.scalar.activation(sine[:], red[:], ACT.Sin).then_inc(trig_ready, 1)
            nc.scalar.activation(cosine[:], mag[:], ACT.Sin).then_inc(trig_ready, 1)
            act.wait_ge(pads_set, 5)
            with act.Fori(0, B // 2) as pair:
                act.wait_ge(in_.filled, 2 * PAIR * pair)
                act.dma_start(ctx_raw[:], ctx_dram[:, ds(pair * PAIR, PAIR), :]).then_inc(ctx_in, DMA)
                def inputs(t):
                    for i, to in enumerate((xnT, ctxT)):
                        blocks = (DK, CK)[i]
                        split_hi(nc, act, in_, 2 * (pair * PAIR + t) + i, to[t % 2][:, HI],
                                 in_ps[i][:, 0:blocks * P].rearrange("p (k c) -> p k c", k=blocks))

                def turn(t):
                    e, cols = t // TPB, slice(t % TPB * P, (t % TPB + 1) * P)
                    if t % TPB == 0:
                        act.wait_ge(out_q[e], pair * (STORES * DMA))
                    for i in range(2):
                        split_hi(nc, act, turn_, 2 * (pair * PAIR + t) + i, qkT[e][i][:, HI, :, cols],
                                 turn_ps[i][:].rearrange("p (k c) -> p k c", k=HT))

                inputs(0)
                for t in range(PAIR):
                    tile = pair * PAIR + t
                    if t + 1 < PAIR:
                        inputs(t + 1)
                    act.wait_ge(v_ready, tile + 1)
                    act.wait_ge(out_v[t % 2], (pair * (PAIR // 2) + t // 2) * DMA)
                    nc.scalar.activation(vpad[t % 2][:, :, 0:HD], v_ps[t % 2][:].rearrange("p (h c) -> p h c", h=HEADS),
                                         ACT.Copy).then_inc(v_copied, 1)
                    if t:
                        turn(t - 1)
                turn(PAIR - 1)

        @block.gpsimd
        def _(pool):
            for i in range(2):
                nc.gpsimd.memset(vpad[i][:], 0.0).then_inc(pads_set, 1)
            nc.gpsimd.memset(zeros[:], 0.0).then_inc(pads_set, 1)
            pool.wait_ge(pads_set, 3)
            for i in range(2):
                nc.gpsimd.memset(vpad[i][:, :, HD:HD + 1], 1.0).then_inc(pads_set, 1)
            pool.dma_start(scr["q"][:, 3 * HD:QROWS, :], zeros[:]).then_inc(out_zero, DMA)
            with pool.Fori(0, B // 2) as pair:
                for t in range(PAIR):
                    tile = pair * PAIR + t
                    for i in range(2):
                        pool.wait_ge(rope_done, 2 * tile + i + 1)
                        pool.wait_ge(turn_.filled, 2 * (tile - 1) + i + 1 if t else 2 * tile)
                        nc.gpsimd.tensor_tensor(rot[i][:], by_cos[i][:].rearrange("p h c -> p (h c)"),
                                                by_sin[i][:].rearrange("p h c -> p (h c)"), ALU.add).then_inc(rot_done, 1)
                    pool.wait_ge(v_copied, tile + 1)
                    groups = HEADS // GROUP
                    pool.dma_start(scr["v"][ds((2 * pair + t // TPB) * groups, groups), t % TPB * P:(t % TPB + 1) * P, :]
                                   .rearrange("g p c -> p g c"),
                                   vpad[t % 2][:].rearrange("p (g h) c -> p g (h c)", h=GROUP)).then_inc(out_v[t % 2], DMA)

        @block.vector
        def _(dve):
            dve.sem_inc(in_.split, 1)
            dve.sem_inc(turn_.split, 1)
            token_var(nc, n)
            dve.wait_ge(pos_in, DMA)
            ang4 = ang[:].rearrange("p t (a j) -> p t a j", a=AX)
            for j in range(HALF):
                nc.vector.tensor_scalar(ang4[:, :, :, j], pos[:], FREQS[j], None, ALU.mult)
            nc.vector.drain()
            nc.vector.tensor_scalar(turns[:], ang[:], float(1.0 / TWO_PI), ROUND, ALU.mult, ALU.add)
            nc.vector.drain()
            nc.vector.tensor_scalar(turns[:], turns[:], -ROUND, None, ALU.add)
            nc.vector.drain()
            source = ang
            for part in (c1, c2, c3):
                nc.vector.scalar_tensor_tensor(out=red[:], in0=turns[:], scalar=-part, in1=source[:], op0=ALU.mult, op1=ALU.add)
                nc.vector.drain()
                source = red
            nc.vector.tensor_scalar(red[:], red[:], PI_F, -PI_F, ALU.min, ALU.max)
            nc.vector.drain()
            nc.vector.tensor_scalar(mag[:], red[:], -1.0, None, ALU.mult)
            nc.vector.drain()
            nc.vector.tensor_tensor(mag[:], mag[:], red[:], ALU.max)
            nc.vector.drain()
            nc.vector.tensor_scalar(mag[:], mag[:], -1.0, float(np.pi / 2), ALU.mult, ALU.add).then_inc(red_ready, 1)
            dve.wait_ge(trig_ready, 2)
            nc.vector.tensor_scalar(nsine[:], sine[:], -1.0, None, ALU.mult)
            for r in range(2):
                nc.vector.tensor_copy(cos2[:].rearrange("p t (f r) -> p t f r", r=2)[:, :, :, r], cosine[:])
            for i, (w, raw) in enumerate(((wq, wq_raw), (wkv, wkv_raw))):
                dve.wait_ge(w_hi, i + 1)
                nc.vector.tensor_tensor(w[:, LO], raw[:], fp32(w[:, HI]), ALU.subtract).then_inc(w_split, 1)
            token_rstd(nc, dve, n)
            with dve.Fori(0, B // 2) as pair:
                def inputs(t):
                    for i, to in enumerate((xnT, ctxT)):
                        blocks = (DK, CK)[i]
                        split_lo(nc, dve, in_, 2 * (pair * PAIR + t) + i, to[t % 2][:, LO],
                                 in_ps[i][:, 0:blocks * P].rearrange("p (k c) -> p k c", k=blocks), to[t % 2][:, HI])

                def turn(t):
                    e, cols = t // TPB, slice(t % TPB * P, (t % TPB + 1) * P)
                    for i in range(2):
                        split_lo(nc, dve, turn_, 2 * (pair * PAIR + t) + i, qkT[e][i][:, LO, :, cols],
                                 turn_ps[i][:].rearrange("p (k c) -> p k c", k=HT), qkT[e][i][:, HI, :, cols])

                for t in range(2):
                    normalise_tile(nc, n, x, pair * PAIR + t, xn[t][:])
                inputs(0)
                for t in range(PAIR):
                    tile = pair * PAIR + t
                    if t + 1 < PAIR:
                        inputs(t + 1)
                    for i in range(2):
                        dve.wait_ge(qk_ready, 2 * tile + i + 1)
                        dve.wait_ge(rot_done, 2 * (tile - 1) + i + 1 if t else 2 * tile)
                        src = qk_ps[i][:].rearrange("p (h c) -> p h c", h=HEADS)
                        nc.vector.tensor_tensor(by_cos[i][:], src, cos2[:, ds(tile, 1), :].to_broadcast([P, HEADS, HD]), ALU.mult)
                        pairs = qk_ps[i][:].rearrange("p (h f r) -> p h f r", h=HEADS, r=2)
                        swapped = by_sin[i][:].rearrange("p h (f r) -> p h f r", r=2)
                        for r, table in ((0, nsine), (1, sine)):
                            last = nc.vector.tensor_tensor(swapped[:, :, :, r], pairs[:, :, :, 1 - r],
                                                           table[:, ds(tile, 1), :].to_broadcast([P, HEADS, HD // 2]), ALU.mult)
                        last.then_inc(rope_done, 1)
                    if t + 2 < PAIR:
                        dve.wait_ge(in_.filled, 2 * tile + 1)
                        normalise_tile(nc, n, x, tile + 2, xn[t % 2][:])
                    if t:
                        turn(t - 1)
                turn(PAIR - 1)


RING = 4


def phase_rope_attention1(nc, io, x, ident, odd, attn):
    from contextlib import ExitStack
    scr = io["scratch"]
    KT = S // P
    SCALE = 1.0 / float(np.sqrt(HD))
    with ExitStack() as ctx:
        def sb(name, shape, dt=FP32):
            return ctx.enter_context(nc.sbuf_tensor(f"r_{name}", shape, dt))

        def ps(name, shape):
            return ctx.enter_context(nc.psum_tensor(f"r_{name}", shape, FP32))

        def sem(name):
            return ctx.enter_context(nc.semaphore(f"r_{name}"))

        kM = [sb(f"kM{s}", [P, GROUP, S], FP32R) for s in range(RING)]
        qS = [sb(f"qS{s}", [P, GROUP // 2, S], FP32R) for s in range(RING)]
        v = [sb(f"v{s}", [P, KT, GROUP * PAD]) for s in range(RING)]
        probs = [sb(f"probs{k}", [P, GROUP, S]) for k in range(KT)]
        top = [sb(f"top{i}", [P, KT, GROUP]) for i in range(2)]
        shift = [sb(f"shift{i}", [P, KT, GROUP, 2], FP32R) for i in range(2)]
        shiftT = [sb(f"shiftT{i}", [2 * GROUP, S], FP32R) for i in range(2)]
        outT = sb("outT", [P, S])
        rinv = sb("rinv", [P, KT * GROUP])
        bout = sb("bout", [P, D])
        st_ps = [ps(f"st{i}", [P, 2, S]) for i in range(2)]
        out_ps = ps("out", [P, S])
        ring_ps = [ps(f"ring{i}", [P, S]) for i in range(3)]
        PLACES = KT * GROUP + 2
        SHIFT_PLACE, OUT_PLACE = GROUP, 2 * GROUP + 1

        def place(q, h):
            return q * GROUP + h + min(q, 2)

        def ring(at):
            return ring_ps[at % 3]

        slot_set_pool = sem("slot_set_pool")
        slot_set = [sem(f"slot_set{s}") for s in range(RING)]
        kqv_in = [sem(f"kqv_in{s}") for s in range(RING)]
        shift_in = [sem(f"shift_in{s}") for s in range(RING)]
        bout_in = sem("bout_in")
        max_ready, max_read, shift_made = sem("max_ready"), sem("max_read"), sem("shift_made")
        shift_turned, shift_copied = sem("shift_turned"), sem("shift_copied")
        scores_ready, exp_done = sem("scores_ready"), sem("exp_done")
        out_ready, out_copied, out_turned, out_done = sem("out_ready"), sem("out_copied"), sem("out_turned"), sem("out_done")
        LOADS, SHIFTS = 5, 4
        block = ctx.enter_context(nc.Block())

        def steps(engine, step):
            rings = GROUPS // RING
            for s in range(RING):
                step(s, 0, s, s == 0, RING)
            with engine.Fori(1, rings - 1) as i:
                for s in range(RING):
                    step(i * RING + s, i, s, False, RING)
            for s in range(RING):
                step((rings - 1) * RING + s, rings - 1, s, False, RING - 1 - s)

        CONST_ROWS = 6

        def set_slot(memset, s, halves=(0, 1), each=lambda done: None):
            done = 0
            for half in halves:
                tail = slice(64 * half + 32, 64 * half + 64)
                other = slice(64 * (1 - half), 64 * (1 - half) + 64)
                for rows, value in ((qS[s][tail, :, :], 0.0), (kM[s][tail, half:GROUP:2, :], 1.0),
                                    (kM[s][other, half:GROUP:2, :], 0.0)):
                    memset(fp32(rows), value).then_inc(slot_set_pool if halves == (1,) else slot_set[s], 1)
                    done += 1
                    each(done)

        @block.gpsimd
        def _(pool):
            set_slot(nc.gpsimd.memset, 0, (1,), lambda done: pool.wait_ge(slot_set_pool, done))
            for s in range(1, RING):
                set_slot(nc.gpsimd.memset, s, (0, 1), lambda done: pool.wait_ge(slot_set[s], done))
            pool.wait_ge(bout_in, DMA)
            with pool.Fori(0, TILES) as tile:
                nc.gpsimd.tensor_tensor(x[:, ds(tile, 1), :], x[:, ds(tile, 1), :],
                                        bout[:].rearrange("p (a c) -> p a c", a=1), ALU.add)

        @block.sync
        def _(sp):
            def load(g, s):
                for half in range(2):
                    rows = 64 * half
                    heads = slice(half, GROUP, 2)
                    sp.dma_start(fp32(kM[s][rows:rows + KROWS, heads, :]),
                                 scr["k"][ds(g * GROUP, GROUP), :, :][heads].rearrange("h r n -> r h n")).then_inc(kqv_in[s], DMA)
                    sp.dma_start(fp32(qS[s][rows:rows + QROWS, :, :]),
                                 scr["q"][ds(g * GROUP, GROUP), :, :][heads].rearrange("h r n -> r h n")).then_inc(kqv_in[s], DMA)
                sp.dma_start(v[s][:], scr["v"][ds(g, 1), :, :].rearrange("g (k p) c -> p (g k) c", p=P)).then_inc(kqv_in[s], DMA)

            def shifts(g, s):
                sp.wait_ge(shift_copied, g + 1)
                for h in range(GROUP):
                    row = 64 * (h % 2) + 3 * HD
                    sp.dma_start(fp32(qS[s][row:row + 2, h // 2, :]), fp32(shiftT[s % 2][2 * h:2 * h + 2, :])).then_inc(shift_in[s], DMA)

            sp.wait_ge(slot_set[0], CONST_ROWS // 2)
            sp.wait_ge(slot_set_pool, CONST_ROWS // 2)
            load(0, 0)
            sp.wait_ge(slot_set[1], CONST_ROWS)
            load(1, 1)
            sp.dma_start(bout[:], io["L1_xattn_bout"].rearrange("(a n) -> a n", a=1).to_broadcast([P, D])).then_inc(bout_in, DMA)
            shifts(0, 0)
            sp.wait_ge(slot_set[2], CONST_ROWS)
            load(2, 2)
            sp.wait_ge(slot_set[3], CONST_ROWS)

            def step(g, i, s, first, left):
                if isinstance(g, int) and g < RING:
                    store_qk(sp, scr, odd.qkT, B - 1, odd.stored, range(g * STORES // RING, (g + 1) * STORES // RING))
                    if g == RING - 1:
                        sp.wait_ge(odd.stored, B // 2 * STORES * DMA)
                if left >= RING - 1:
                    sp.wait_ge(out_ready, g)
                    load(g + RING - 1, (s + RING - 1) % RING)
                if left >= 1:
                    shifts(g + 1, (s + 1) % RING)

            steps(sp, step)

        @block.tensor
        def _(pe):
            def bank_free(g, at):
                exists = lambda n, low, high: not isinstance(n, int) or low <= n <= high
                while True:
                    at -= 3
                    if at < 0:
                        at, g = at + PLACES, g - 1
                    if isinstance(g, int) and g < 0:
                        return
                    if at == SHIFT_PLACE:
                        if exists(g, 1, GROUPS):
                            pe.wait_ge(shift_copied, g)
                            return
                    elif at == OUT_PLACE:
                        if exists(g, 3, GROUPS + 2):
                            pe.wait_ge(out_done, g - 2)
                            return
                    elif exists(g, 0, GROUPS - 1):
                        before = at - (at > SHIFT_PLACE) - (at > OUT_PLACE)
                        pe.wait_ge(max_read, g * (KT * GROUP) + before + 1)
                        return

            def scores(g, i, s, k, pair):
                if k == 0 and pair == 0:
                    pe.wait_ge(shift_in[s], (i + 1) * SHIFTS * DMA)
                pe.wait_ge(exp_done, (g * KT + k) * 2 + pair)
                last = None
                for j in range(2):
                    last = nc.tensor.matmul(st_ps[pair][:, j, :], kM[s][:, 2 * pair + j, k * P:(k + 1) * P],
                                            qS[s][:, pair, :], start=True, stop=True)
                last.then_inc(scores_ready, 1)

            def maxima(g, i, s, q, heads):
                for h in heads:
                    if q == 0 and h == 0:
                        pe.wait_ge(kqv_in[s], (i + 1) * LOADS * DMA)
                    bank_free(g, place(q, h))
                    nc.tensor.matmul(ring(place(q, h))[:], qS[s][:, h // 2, q * P:(q + 1) * P], kM[s][:, h, :],
                                     start=True, stop=True).then_inc(max_ready, 1)

            def turn_shifts(g, s):
                pe.wait_ge(shift_made, g + 1)
                bank_free(g + 1, SHIFT_PLACE)
                last = None
                for q in range(KT):
                    last = nc.tensor.transpose(ring(SHIFT_PLACE)[0:2 * GROUP, q * P:(q + 1) * P],
                                               fp32(shift[s % 2][:, q].rearrange("p h a -> p (h a)")), ident[:])
                last.then_inc(shift_turned, 1)

            def values(g, s, k):
                pe.wait_ge(exp_done, (g * KT + k) * 2 + 3)
                if k == 0:
                    pe.wait_ge(out_copied, g)
                last = None
                for h in range(GROUP):
                    last = nc.tensor.matmul(out_ps[h * PAD:(h + 1) * PAD, :], v[s][:, k, h * PAD:(h + 1) * PAD],
                                            probs[k][:, h, :], start=(k == 0), stop=(k == KT - 1))
                if k == KT - 1:
                    last.then_inc(out_ready, 1)

            def turn_out(g):
                pe.wait_ge(out_copied, g + 1)
                bank_free(g + 3, OUT_PLACE)
                last = None
                for q in range(KT):
                    last = nc.tensor.transpose(ring(OUT_PLACE)[:, q * P:(q + 1) * P], outT[:, q * P:(q + 1) * P], ident[:])
                last.then_inc(out_turned, 1)

            for g in range(2):
                for q in range(KT):
                    maxima(g, 0, g, q, range(GROUP))
                    if (g, q) == (1, 0):
                        turn_shifts(0, 0)

            def step(g, i, s, first, left):
                for k in range(KT):
                    def maxima_of(*heads):
                        if left >= 2:
                            maxima(g + 2, i + (s + 2) // RING, (s + 2) % RING, k, heads)

                    maxima_of(0)
                    scores(g, i, s, k, 0)
                    maxima_of(1)
                    scores(g, i, s, k, 1)
                    maxima_of(2, 3)
                    if k == 0:
                        if not first:
                            values(g - 1, (s - 1) % RING, KT - 1)
                        if left >= 1:
                            turn_shifts(g + 1, (s + 1) % RING)
                    else:
                        values(g, s, k - 1)
                        if k == 1 and not first:
                            turn_out(g - 1)

            steps(pe, step)
            values(GROUPS - 1, RING - 1, KT - 1)
            turn_out(GROUPS - 1)

        @block.scalar
        def _(act):
            def copy_shifts(g, s):
                act.wait_ge(shift_turned, g + 1)
                nc.scalar.activation(shiftT[s % 2][:], ring(SHIFT_PLACE)[0:2 * GROUP, :], ACT.Copy).then_inc(shift_copied, 1)

            def copy_out(g):
                act.wait_ge(out_ready, g + 1)
                nc.scalar.activation(outT[:], out_ps[:], ACT.Copy).then_inc(out_copied, 1)

            copy_shifts(0, 0)

            def step(g, i, s, first, left):
                for k in range(KT):
                    for pair in range(2):
                        act.wait_ge(scores_ready, (g * KT + k) * 2 + pair + 1)
                        nc.scalar.activation(probs[k][:, 2 * pair:2 * pair + 2, :], st_ps[pair][:], ACT.Exp,
                                             scale=SCALE).then_inc(exp_done, 1)
                    if k == 0:
                        if not first:
                            copy_out(g - 1)
                        if left >= 1:
                            copy_shifts(g + 1, (s + 1) % RING)

            steps(act, step)
            copy_out(GROUPS - 1)

        @block.vector
        def _(dve):
            def read_maxima(g, s, q):
                for h in range(GROUP):
                    dve.wait_ge(max_ready, (g * KT + q) * GROUP + h + 1)
                    nc.vector.reduce_max(top[s % 2][:, q, h:h + 1], ring(place(q, h))[:], AXIS_X).then_inc(max_read, 1)

            def make_shifts(s):
                nc.vector.drain()
                nc.vector.tensor_scalar(shift[s % 2][:, :, :, 0], top[s % 2][:], -1.0, None, ALU.mult)
                nc.vector.drain()
                nc.vector.scalar_tensor_tensor(out=shift[s % 2][:, :, :, 1], in0=top[s % 2][:], scalar=-1.0,
                                               in1=fp32(shift[s % 2][:, :, :, 0]), op0=ALU.mult,
                                               op1=ALU.subtract).then_inc(shift_made, 1)

            def normalise(g):
                dve.wait_ge(out_turned, g + 1)
                turned = ring(OUT_PLACE)[:].rearrange("p (a c) -> p a c", c=PAD)
                nc.vector.reciprocal(rinv[:], turned[:, :, HD])
                nc.vector.drain()
                nc.vector.tensor_tensor(attn[:, ds(g, 1), :, :].rearrange("p g a c -> p (g a) c"), turned[:, :, 0:HD],
                                        rinv[:].unsqueeze(2).to_broadcast([P, KT * GROUP, HD]), ALU.mult).then_inc(out_done, 1)

            set_slot(nc.vector.memset, 0, (0,))
            dve.sem_inc(exp_done, 1)
            for g in range(2):
                for q in range(KT):
                    read_maxima(g, g, q)
                make_shifts(g)

            def step(g, i, s, first, left):
                for q in range(KT):
                    if left >= 2:
                        read_maxima(g + 2, s, q)
                    if q == 1 and not first:
                        normalise(g - 1)
                if left >= 2:
                    make_shifts((s + 2) % RING)

            steps(dve, step)
            normalise(GROUPS - 1)


def phase_out1(nc, io, x, ident, stats, attn):
    from contextlib import ExitStack
    with ExitStack() as ctx:
        def sb(name, shape, dt=FP32):
            return ctx.enter_context(nc.sbuf_tensor(f"o_{name}", shape, dt))

        def ps(name, shape):
            return ctx.enter_context(nc.psum_tensor(f"o_{name}", shape, FP32))

        def sem(name):
            return ctx.enter_context(nc.semaphore(f"o_{name}"))

        w_raw = sb("w_raw", [P, DK, D])
        w = sb("w", [P, 2, DK, D], FP32R)
        rows = [sb(f"rows{i}", [P, D]) for i in range(2)]
        aT = [sb(f"aT{i}", [P, 2, DK, P], FP32R) for i in range(2)]
        tp = [ps(f"tp{i}", [P, D]) for i in range(2)]
        y_ps = [ps(f"y{i}", [P, D]) for i in range(2)]
        t_ = Split(nc, ctx, "ot")
        w_in, w_hi, w_split, rows_ready, y_ready, y_added = (
            sem("w_in"), sem("w_hi"), sem("w_split"), sem("rows_ready"), sem("y_ready"), sem("y_added"))
        block = ctx.enter_context(nc.Block())

        @block.sync
        def _(sp):
            sp.dma_start(w_raw[:], io["L1_xattn_Wout"].rearrange("(k p) n -> p k n", p=P)).then_inc(w_in, DMA)

        @block.tensor
        def _(pe):
            def out_product(tile, t):
                pe.wait_ge(t_.split, tile + 2)
                pe.wait_ge(y_added, tile)
                product(nc, y_ps[t % 2][:], [([aT[t % 2][:, h, k, :] for h in (HI, LO)],
                                              [w[:, h, k, :] for h in (HI, LO)]) for k in range(DK)]).then_inc(y_ready, 1)

            with pe.Fori(0, B) as b:
                for t in range(TPB):
                    tile = b * TPB + t
                    pe.wait_ge(rows_ready, tile + 1)
                    pe.wait_ge(t_.split, tile)
                    transposes(nc, t_, tp[t % 2], [rows[t % 2][:, k * P:(k + 1) * P] for k in range(DK)], ident)
                    if t == 0:
                        pe.wait_ge(w_split, 1)
                    if t:
                        out_product(tile - 1, t - 1)
                out_product(b * TPB + TPB - 1, TPB - 1)

        @block.scalar
        def _(act):
            act.wait_ge(w_in, DMA)
            nc.scalar.activation(w[:, HI], w_raw[:], ACT.Copy).then_inc(w_hi, 1)
            with act.Fori(0, B) as b:
                for t in range(TPB):
                    tile = b * TPB + t
                    act.wait_ge(t_.filled, tile - 1 if t else b * TPB)
                    nc.scalar.activation(rows[t % 2][:].rearrange("p (g c) -> p g c", g=HEADS // GROUP),
                                         attn[:, ds(b * (HEADS // GROUP), HEADS // GROUP), t * GROUP:(t + 1) * GROUP, :]
                                         .rearrange("p g a c -> p g (a c)"), ACT.Copy).then_inc(rows_ready, 1)
                    split_hi(nc, act, t_, tile, aT[t % 2][:, HI], tp[t % 2][:].rearrange("p (k c) -> p k c", k=DK))

        @block.vector
        def _(dve):
            dve.sem_inc(t_.split, 1)
            dve.sem_inc(y_added, 1)
            dve.wait_ge(w_hi, 1)
            nc.vector.tensor_tensor(w[:, LO], w_raw[:], fp32(w[:, HI]), ALU.subtract).then_inc(w_split, 1)

            def add(tile, t):
                dve.wait_ge(y_ready, tile + 1)
                nc.vector.tensor_tensor(x[:, ds(tile, 1), :], y_ps[t % 2][:].rearrange("p (a c) -> p a c", a=1),
                                        x[:, ds(tile, 1), :], ALU.add).then_inc(y_added, 1)

            def out_stats(tile):
                dve.wait_ge(y_added, tile + 2)
                tile_stats(nc, stats, x, tile)

            with dve.Fori(0, B) as b:
                for t in range(TPB):
                    tile = b * TPB + t
                    split_lo(nc, dve, t_, tile, aT[t % 2][:, LO], tp[t % 2][:].rearrange("p (k c) -> p k c", k=DK), aT[t % 2][:, HI])
                    if t >= 2:
                        out_stats(tile - 2)
                    if t:
                        add(tile - 1, t - 1)
                out_stats(b * TPB + TPB - 2)
                add(b * TPB + TPB - 1, TPB - 1)
                out_stats(b * TPB + TPB - 1)


def phase_rope1(nc, io, x, ident, stats):
    from contextlib import ExitStack
    with ExitStack() as ctx:
        odd = OddBatch(nc, ctx)
        phase_qkv1(nc, io, x, ident, stats, odd)
        attn = ctx.enter_context(nc.sbuf_tensor("attn", [P, GROUPS, TPB * GROUP, HD], FP32))
        phase_rope_attention1(nc, io, x, ident, odd, attn)
        phase_out1(nc, io, x, ident, stats, attn)


def phase_ffn1(nc, io, x, ident, stats):
    from contextlib import ExitStack
    ER = E1 * R1
    NF = DFF // P
    HALVES = 2
    CH = B // HALVES
    HT, HTOK = CH * TPB, CH * S
    STEPS = NF * CH
    PREP = 4
    USES = TPB + 2
    gate_dram, up_dram, down_dram = io["L1_ffn_Wg"], io["L1_ffn_Wu"], io["L1_ffn_Wd"]
    out_dram = io["out"].rearrange("b (t p) d -> p (b t) d", p=P)
    with ExitStack() as ctx:
        def sb(name, shape, dt=FP32):
            return ctx.enter_context(nc.sbuf_tensor(f"f_{name}", shape, dt))

        def ps(name, shape):
            return ctx.enter_context(nc.psum_tensor(f"f_{name}", shape, FP32))

        def sem(name):
            return ctx.enter_context(nc.semaphore(f"f_{name}"))

        xnT = sb("xnT", [P, 2, DK, HTOK], FP32R)
        agT, auT = sb("agT", [P, 2, DK, ER], FP32R), sb("auT", [P, 2, DK, ER], FP32R)
        wrT = sb("wrT", [P, 2, DK, E1], FP32R)
        bdT = sb("bdT", [ER, 2, D], FP32R)
        wr_raw = sb("wr_raw", [E1, D])
        gate_raw, up_raw, down_raw = sb("gate_raw", [P, D]), sb("up_raw", [P, D]), sb("down_raw", [P, DK, P])
        lora_raw = sb("lora_raw", [P, 3, P])
        gateT = [sb(f"gateT{s}", [P, 2, DK, P], FP32R) for s in range(2)]
        upT = [sb(f"upT{s}", [P, 2, DK, P], FP32R) for s in range(2)]
        downT = [sb(f"downT{s}", [P, 2, D], FP32R) for s in range(2)]
        loraT = [sb(f"loraT{s}", [P, 2, 3, P], FP32R) for s in range(2)]
        rl = sb("rl", [P, S])
        logits = sb("logits", [P, HT, E1])
        shifted = sb("shifted", [P, HT, E1])
        rev = sb("rev", [P, HT, E1])
        hots = sb("hots", [P, HT, 4, E1])
        am = sb("am", [P, 2, 2, 2, HTOK], FP32R)
        down_acc = sb("down_acc", [P, 2, HTOK])
        hidS = [sb(f"hidS{c}", [P, 3, 2, S], FP32R) for c in range(2)]
        work = sb("work", [P, 10, S])

        def hid(c, var):
            return work[:, 4 + 3 * c + var, :]

        mk = [work[:, 4, :], work[:, 9, :]]
        maskT = work[:, 5:9, :].rearrange("p (k c) n -> p k (c n)", k=2)
        xn = work[:, 0:4, :]
        n = TokenNorm(nc, ctx, "fn", stats)
        t = TopTwo(nc, ctx, "ft", HT, E1)
        g_ps = [ps(f"g{c}", [P, S]) for c in range(CH)]
        u_ps = [ps(f"u{c}", [P, S]) for c in range(CH)]
        prep_ps = ps("prep", [P, S])
        y_ps = [ps(f"y{i}", [P, S]) for i in range(3)]
        c_, xt_, prep_ = Split(nc, ctx, "fc"), Split(nc, ctx, "fx"), Split(nc, ctx, "fp")
        am_ = Split(nc, ctx, "fa")
        const_in, raw_in = sem("const_in"), sem("raw_in")
        router_ready, router_copied, logits_ready, logits_done = (
            sem("router_ready"), sem("router_copied"), sem("logits_ready"), sem("logits_done"))
        gap_ready, gap_exp, rl_clear = sem("gap_ready"), sem("gap_exp"), sem("rl_clear")
        mk_made, mk_turned, mask_copied, a_ready, a_used, acc_clear = (
            sem("mk_made"), sem("mk_turned"), sem("mask_copied"), sem("a_ready"), sem("a_used"), sem("acc_clear"))
        gate_ready, up_ready = sem("gate_ready"), sem("up_ready")
        silu_done, hid_done, hid_hi, hid_split = sem("silu_done"), sem("hid_done"), sem("hid_hi"), sem("hid_split")
        y_ready, y_added = sem("y_ready"), sem("y_added")
        z_ready, z_hi, z_split, z_out, z_added, stored = (
            sem("z_ready"), sem("z_hi"), sem("z_split"), sem("z_out"), sem("z_added"), sem("stored"))
        am_split2 = sem("am_split2")
        CONST_JOBS = 4
        a_ps = [[g_ps[c], u_ps[c]] for c in range(CH)]
        block = ctx.enter_context(nc.Block())

        def first_bank(job):
            return (prep_ps, y_ps[2])[job % 2]

        def const_views(job):
            bank = first_bank(job)
            if job < 2:
                raw, to = ((gate_raw, agT), (up_raw, auT))[job]
                return ([raw[:, k * P:(k + 1) * P] for k in range(DK)],
                        bank[:].rearrange("p (k c) -> p k c", k=DK), [to[:, h] for h in (HI, LO)])
            if job == 2:
                return ([wr_raw[:, k * P:(k + 1) * P] for k in range(DK)],
                        bank[:, 0:DK * E1].rearrange("p (k c) -> p k c", k=DK), [wrT[:, h] for h in (HI, LO)])
            return ([down_raw[:, k, :] for k in range(DK)], bank[:], [bdT[:, h] for h in (HI, LO)])

        def prep_views(s, part, bank=prep_ps):
            if part < 2:
                raw, to = ((gate_raw, gateT), (up_raw, upT))[part]
                return ([raw[:, k * P:(k + 1) * P] for k in range(DK)],
                        bank[:].rearrange("p (k c) -> p k c", k=DK), [to[s][:, h] for h in (HI, LO)])
            if part == 2:
                return ([down_raw[:, k, :] for k in range(DK)], bank[:], [downT[s][:, h] for h in (HI, LO)])
            return ([lora_raw[:, k, :] for k in range(3)], bank[:, 0:3 * P].rearrange("p (k c) -> p k c", k=3),
                    [loraT[s][:, h] for h in (HI, LO)])

        def tiles(engine, half, tile):
            tile(0, 0, True, False)
            tile(1, 1, False, False)
            with engine.Fori(1, (NF - 1) // 2) as i:
                for s in range(2):
                    tile(2 * i + s, s, False, False)
            tile(NF - 1, 0, False, True)

        def ring(c, use):
            return y_ps[(c * USES + use) % 3]

        @block.sync
        def _(sp):
            sp.dma_start(wr_raw[:], io["L1_ffn_Wr"]).then_inc(const_in, DMA)
            sp.dma_start(gate_raw[:], io["L1_ffn_Ag"].rearrange("e r d -> (e r) d")).then_inc(const_in, DMA)
            sp.dma_start(up_raw[:], io["L1_ffn_Au"].rearrange("e r d -> (e r) d")).then_inc(const_in, DMA)
            for k in range(DK):
                sp.dma_start(down_raw[:, k, :].rearrange("p (e r) -> p e r", e=E1),
                             io["L1_ffn_Bd"][:, k * P:(k + 1) * P, :].rearrange("e p r -> p e r")).then_inc(const_in, DMA)
            sp.wait_ge(c_.filled, CONST_JOBS)

            def load(h, f):
                sp.wait_ge(prep_.filled, (h * NF + f) * PREP)
                sp.dma_start(gate_raw[:], gate_dram[ds(f * P, P), :]).then_inc(raw_in, DMA)
                sp.dma_start(up_raw[:], up_dram[ds(f * P, P), :]).then_inc(raw_in, DMA)
                sp.dma_start(down_raw[:], down_dram[:, ds(f * P, P)].rearrange("(k p) f -> p k f", p=P)).then_inc(raw_in, DMA)
                for i, name in enumerate(("L1_ffn_Bg", "L1_ffn_Bu")):
                    sp.dma_start(lora_raw[:, i, :].rearrange("p (e r) -> p e r", e=E1),
                                 io[name][:, ds(f * P, P), :].rearrange("e f r -> f e r")).then_inc(raw_in, DMA)
                sp.dma_start(lora_raw[:, 2, :], io["L1_ffn_Ad"].rearrange("e r f -> (e r) f")[:, ds(f * P, P)]).then_inc(raw_in, DMA)

            with sp.Fori(0, HALVES) as h:
                with sp.Fori(0, NF) as f:
                    load(h, f)
                for c in range(CH):
                    sp.wait_ge(z_added, h * HT + (c + 1) * TPB)
                    sp.dma_start(out_dram[:, ds(h * HT + c * TPB, TPB), :], x[:, ds(h * HT + c * TPB, TPB), :]).then_inc(stored, DMA)
            sp.wait_ge(stored, HALVES * CH * DMA)

        LOADS = 6

        @block.tensor
        def _(pe):
            def prep(h, f, s, part):
                job = (h * NF + f) * PREP + part
                if part == 0:
                    pe.wait_ge(raw_in, (h * NF + f + 1) * LOADS * DMA)
                pe.wait_ge(prep_.split, job)
                transposes(nc, prep_, prep_ps, prep_views(s, part)[0], ident)

            pe.wait_ge(const_in, (3 + DK) * DMA)
            for job in range(CONST_JOBS):
                if job >= 2:
                    pe.wait_ge(c_.split, job - 1)
                transposes(nc, c_, first_bank(job), const_views(job)[0], ident)
            pe.wait_ge(c_.split, CONST_JOBS)
            with pe.Fori(0, HALVES) as h:
                def token_tile(c, k):
                    job = (h * CH + c) * TPB + k
                    pe.wait_ge(n.xn_ready, job + 1)
                    pe.wait_ge(xt_.split, job)
                    transposes(nc, xt_, (g_ps, u_ps)[k % 2][0], [xn[:, k, i * P:(i + 1) * P] for i in range(DK)], ident)

                def router(c, k):
                    if k == 0:
                        pe.wait_ge(xt_.split, (h * CH + c + 1) * TPB + 1)
                        pe.wait_ge(router_copied, h * CH + c)
                    last = add_product(nc, g_ps[1][0:E1, :], [wrT[:, i, k, :] for i in (HI, LO)],
                                       [xnT[:, i, k, c * S:(c + 1) * S] for i in (HI, LO)], start=(k == 0))
                    if k == DK - 1:
                        last.then_inc(router_ready, 1)

                def turn_logits(c):
                    pe.wait_ge(router_copied, h * CH + c + 1)
                    pe.wait_ge(logits_done, h * CH + c)
                    last = None
                    for k in range(TPB):
                        last = nc.tensor.transpose(u_ps[1][:, k * P:(k + 1) * P], rl[:, k * P:(k + 1) * P], ident[:])
                    last.then_inc(logits_ready, 1)

                for c in range(CH):
                    for k in range(TPB):
                        token_tile(c, k)
                        if c:
                            router(c - 1, k)
                    if c:
                        turn_logits(c - 1)
                for k in range(DK):
                    router(CH - 1, k)
                pe.wait_ge(raw_in, (h * NF + 1) * LOADS * DMA)
                for part in range(PREP):
                    pe.wait_ge(prep_.split, h * NF * PREP + max(part - 1, 0))
                    transposes(nc, prep_, first_bank(part), prep_views(0, part, first_bank(part))[0], ident)
                turn_logits(CH - 1)

                def turn_masks(base):
                    for i in range(HT):
                        pe.wait_ge(mk_made, base + i + 1)
                        pe.wait_ge(mask_copied, base + i)
                        for k in range(4):
                            last = nc.tensor.transpose(y_ps[i % 2][:, k * P:(k + 1) * P], mk[i % 2][:, k * P:(k + 1) * P], ident[:])
                        last.then_inc(mk_turned, 1)

                pe.wait_ge(logits_done, h * CH + CH)
                for c in range(CH):
                    for i, a in enumerate((agT, auT)):
                        if (c, i) == (CH - 1, 1):
                            turn_masks(h * 2 * HT)
                        product(nc, a_ps[c][i][:], [([a[:, j, k, :] for j in (HI, LO)],
                                                     [xnT[:, j, k, c * S:(c + 1) * S] for j in (HI, LO)])
                                                    for k in range(DK)]).then_inc(a_ready, 1)

                def ring_wait(step, use):
                    pe.wait_ge(y_added, step * USES + use)

                def down(step, s, c):
                    pe.wait_ge(hid_split, 3 * step + 3 + 1)
                    for i in range(TPB):
                        ring_wait(step, i)
                        product(nc, ring(c, i)[:], [([hidS[c][:, 0, j, i * P:(i + 1) * P] for j in (HI, LO)],
                                                     [downT[s][:, j, :] for j in (HI, LO)])]).then_inc(y_ready, 1)

                def down_lora(step, s, c):
                    for k in range(2):
                        pe.wait_ge(hid_split, 3 * step + 3 + 2 + k)
                        ring_wait(step, TPB + k)
                        product(nc, ring(c, TPB + k)[:], [([loraT[s][:, j, 2, :] for j in (HI, LO)],
                                                          [hidS[c][:, 1 + k, j, :] for j in (HI, LO)])]).then_inc(y_ready, 1)

                def lora(step, s, c, var):
                    pe.wait_ge(hid_done, 3 * step + var + 3)
                    if var == 1:
                        pe.wait_ge(am_.split, (h + 1) * CH * 2)
                        pe.wait_ge(am_split2, (h + 1) * CH * 2)
                    for i, (to, ready) in enumerate(((g_ps[c], gate_ready), (u_ps[c], up_ready))):
                        add_product(nc, to[:], [loraT[s][:, j, i, :] for j in (HI, LO)],
                                    [am[:, i, var - 1, j, c * S:(c + 1) * S] for j in (HI, LO)]).then_inc(ready, 1)

                def tile(f, s, first, last):
                    pe.wait_ge(prep_.split, (h * NF + f + 1) * PREP)
                    for c in range(CH):
                        step = h * STEPS + f * CH + c
                        before = (step - 1, s if c else 1 - s, 1 - c)
                        has_before = not (first and c == 0)
                        if first:
                            pe.wait_ge(a_used, (h * CH + c + 1) * 4)
                        pe.wait_ge(hid_done, 3 * step)
                        product(nc, g_ps[c][:], [([gateT[s][:, j, k, :] for j in (HI, LO)],
                                                  [xnT[:, j, k, c * S:(c + 1) * S] for j in (HI, LO)])
                                                 for k in range(DK)]).then_inc(gate_ready, 1)
                        if not last:
                            prep(h, f + 1, 1 - s, 2 * c)
                        product(nc, u_ps[c][:], [([upT[s][:, j, k, :] for j in (HI, LO)],
                                                  [xnT[:, j, k, c * S:(c + 1) * S] for j in (HI, LO)])
                                                 for k in range(DK)]).then_inc(up_ready, 1)
                        if has_before:
                            down(*before)
                        lora(step, s, c, 1)
                        if not last:
                            prep(h, f + 1, 1 - s, 2 * c + 1)
                        if has_before:
                            down_lora(*before)
                        lora(step, s, c, 2)

                tiles(pe, h, tile)
                end = (h * STEPS + STEPS - 1, 0, CH - 1)
                down(*end)
                down_lora(*end)
                pe.wait_ge(y_added, (h + 1) * STEPS * USES + 2)
                turn_masks(h * 2 * HT + HT)
                pe.wait_ge(z_split, h + 1)
                for i in range(HT):
                    pe.wait_ge(z_added, h * HT + i - 1 if i else h * HT)
                    product(nc, y_ps[i % 2][:], [([am[:, 0, 0, j, i * P:(i + 1) * P] for j in (HI, LO)],
                                                 [bdT[:, j, :] for j in (HI, LO)])]).then_inc(z_out, 1)

        @block.scalar
        def _(act):
            def prep(h, f, s, part, bank=prep_ps):
                _, psum, (hi, lo) = prep_views(s, part, bank)
                split_hi(nc, act, prep_, (h * NF + f) * PREP + part, hi, psum)

            token_std(nc, act, n)
            for job in range(CONST_JOBS):
                _, psum, (hi, lo) = const_views(job)
                split_hi(nc, act, c_, job, hi, psum)
            act.wait_ge(rl_clear, 1)
            with act.Fori(0, HALVES) as h:
                def copy_router(c):
                    act.wait_ge(router_ready, h * CH + c + 1)
                    nc.scalar.activation(rl[0:E1, :], g_ps[1][0:E1, :], ACT.Copy).then_inc(router_copied, 1)

                for c in range(CH):
                    for k in range(TPB):
                        at = (c * TPB + k) * P
                        split_hi(nc, act, xt_, (h * CH + c) * TPB + k, xnT[:, HI, :, at:at + P],
                                 (g_ps, u_ps)[k % 2][0][:].rearrange("p (k c) -> p k c", k=DK))
                    if c:
                        copy_router(c - 1)
                copy_router(CH - 1)
                for part in range(PREP):
                    prep(h, 0, 0, part, first_bank(part))
                act.wait_ge(gap_ready, h + 1)
                nc.scalar.activation(shifted[:], shifted[:], ACT.Exp).then_inc(gap_exp, 1)
                nc.scalar.activation(t.e[:], t.gap[:], ACT.Exp).then_inc(gap_exp, 1)

                def copy_masks(base, part):
                    for i in range(HT):
                        act.wait_ge(mk_turned, base + i + 1)
                        nc.scalar.activation(maskT[:, :, i * P:(i + 1) * P],
                                             y_ps[i % 2][:, part * 2 * P:(part + 1) * 2 * P].rearrange("p (k c) -> p k c", k=2),
                                             ACT.Copy).then_inc(mask_copied, 1)

                copy_masks(h * 2 * HT, 0)
                for c in range(CH):
                    for i in range(2):
                        for k in range(2):
                            job = 4 * (h * CH + c) + 2 * i + k
                            act.wait_ge(a_used, job + 1)
                            nc.scalar.activation(am[:, i, k, HI, c * S:(c + 1) * S], work[:, 2 * i + k, :], ACT.Copy).then_inc(am_.hi_done, 1)

                def tile(f, s, first, last):
                    for c in range(CH):
                        step = h * STEPS + f * CH + c

                        def silu(var):
                            act.wait_ge(gate_ready, 3 * step + var + 1)
                            nc.scalar.activation(hid(c, var), g_ps[c][:], ACT.Silu).then_inc(silu_done, 1)

                        def hi(var):
                            act.wait_ge(hid_done, 3 * step + var + 1 + 3)
                            nc.scalar.activation(hidS[c][:, var, HI, :], hid(c, var), ACT.Copy).then_inc(hid_hi, 1)

                        act.wait_ge(hid_split, 3 * step)
                        silu(0)
                        if not last:
                            prep(h, f + 1, 1 - s, 2 * c)
                        hi(0)
                        silu(1)
                        if not last:
                            prep(h, f + 1, 1 - s, 2 * c + 1)
                        hi(1)
                        silu(2)
                        hi(2)

                tiles(act, h, tile)
                copy_masks(h * 2 * HT + HT, 1)
                act.wait_ge(z_ready, h + 1)
                nc.scalar.activation(am[:, 0, 0, HI, :], down_acc[:, 0, :], ACT.Copy).then_inc(z_hi, 1)

        @block.gpsimd
        def _(pool):
            pool.sem_inc(hid_split, 3)
            with pool.Fori(0, HALVES) as h:
                for c in range(CH):
                    for i in range(2):
                        pool.wait_ge(am_.hi_done, 4 * (h * CH + c) + 2 * i + 2)
                        nc.gpsimd.tensor_tensor(am[:, i, 1, LO, c * S:(c + 1) * S], work[:, 2 * i + 1, :],
                                                fp32(am[:, i, 1, HI, c * S:(c + 1) * S]), ALU.subtract).then_inc(am_split2, 1)
                nc.gpsimd.memset(down_acc[:], 0.0).then_inc(acc_clear, 1)

                def tile(f, s, first, last):
                    for c in range(CH):
                        step = h * STEPS + f * CH + c
                        for var in range(3):
                            pool.wait_ge(hid_hi, 3 * step + var + 1)
                            nc.gpsimd.tensor_tensor(hidS[c][:, var, LO, :], hid(c, var), fp32(hidS[c][:, var, HI, :]),
                                                    ALU.subtract).then_inc(hid_split, 1)

                tiles(pool, h, tile)

        @block.vector
        def _(dve):
            def prep(h, f, s, part, bank=prep_ps):
                _, psum, (hi, lo) = prep_views(s, part, bank)
                split_lo(nc, dve, prep_, (h * NF + f) * PREP + part, lo, psum, hi)

            nc.vector.memset(rl[:], 0.0).then_inc(rl_clear, 1)
            dve.sem_inc(xt_.split, 1)
            dve.sem_inc(mask_copied, 1)
            dve.sem_inc(hid_done, 3)
            dve.sem_inc(y_added, 2)
            for i in range(E1):
                nc.vector.memset(rev[:, :, i:i + 1], float(E1 - i))
            token_var(nc, n)
            token_rstd(nc, dve, n)
            for job in range(CONST_JOBS):
                _, psum, (hi, lo) = const_views(job)
                split_lo(nc, dve, c_, job, lo, psum, hi)
            with dve.Fori(0, HALVES) as h:
                def copy_logits(c):
                    dve.wait_ge(logits_ready, h * CH + c + 1)
                    nc.vector.tensor_copy(logits[:, c * TPB:(c + 1) * TPB, :],
                                          u_ps[1][:].rearrange("p (k e) -> p k e", k=TPB)[:, :, 0:E1]).then_inc(logits_done, 1)

                for k in range(TPB):
                    normalise_tile(nc, n, x, h * HT + k, xn[:, k, :])
                for c in range(CH):
                    for k in range(TPB):
                        at = (c * TPB + k) * P
                        split_lo(nc, dve, xt_, (h * CH + c) * TPB + k, xnT[:, LO, :, at:at + P],
                                 (g_ps, u_ps)[k % 2][0][:].rearrange("p (k c) -> p k c", k=DK), xnT[:, HI, :, at:at + P])
                        if c + 1 < CH:
                            normalise_tile(nc, n, x, h * HT + (c + 1) * TPB + k, xn[:, k, :])
                    if c:
                        copy_logits(c - 1)
                for part in range(PREP):
                    prep(h, 0, 0, part, first_bank(part))
                copy_logits(CH - 1)
                nc.vector.drain()
                top_two(nc, dve, logits, rev, t)
                wide = lambda a: a[:].unsqueeze(2).to_broadcast([P, HT, E1])
                nc.vector.tensor_tensor(shifted[:], logits[:], wide(t.top1), ALU.subtract)
                nc.vector.tensor_tensor(t.gap[:], t.top2[:], t.top1[:], ALU.subtract)
                nc.vector.drain().then_inc(gap_ready, 1)
                dve.wait_ge(gap_exp, 2 * h + 2)
                nc.vector.reduce_sum(t.den[:], shifted[:], AXIS_X)
                nc.vector.drain()
                nc.vector.reciprocal(t.w1[:], t.den[:])
                nc.vector.drain()
                nc.vector.tensor_tensor(t.w2[:], t.e[:], t.w1[:], ALU.mult)
                nc.vector.tensor_copy(hots[:, :, 0, :], t.hot1[:])
                nc.vector.tensor_tensor(hots[:, :, 1, :], t.hot2[:], t.hot1[:], ALU.subtract)
                nc.vector.drain()
                nc.vector.tensor_tensor(hots[:, :, 2, :], t.hot1[:], wide(t.w1), ALU.mult)
                nc.vector.tensor_tensor(hots[:, :, 3, :], t.hot2[:], wide(t.w2), ALU.mult)
                nc.vector.drain()

                def make_masks(base):
                    for i in range(HT):
                        if i >= 2:
                            dve.wait_ge(mk_turned, base + i - 1)
                        nc.vector.tensor_copy(mk[i % 2].rearrange("p (e r) -> p e r", r=R1),
                                              hots[:, i].rearrange("p k e -> p (k e)").unsqueeze(2)
                                              .to_broadcast([P, 4 * E1, R1])).then_inc(mk_made, 1)

                make_masks(h * 2 * HT)
                for c in range(CH):
                    dve.wait_ge(mask_copied, h * 2 * HT + (c + 1) * TPB + 1)
                    dve.wait_ge(am_split2, 2 * (h * CH + c))
                    for i, src in enumerate(a_ps[c]):
                        dve.wait_ge(a_ready, 2 * (h * CH + c) + i + 1)
                        for k in range(2):
                            nc.vector.scalar_tensor_tensor(out=work[:, 2 * i + k, :], in0=src[:], scalar=SCALING1,
                                                           in1=maskT[:, k, c * S:(c + 1) * S], op0=ALU.mult,
                                                           op1=ALU.mult).then_inc(a_used, 1)
                    for i in range(2):
                        dve.wait_ge(am_.hi_done, 4 * (h * CH + c) + 2 * i + 1)
                        nc.vector.tensor_tensor(am[:, i, 0, LO, c * S:(c + 1) * S], work[:, 2 * i, :],
                                                fp32(am[:, i, 0, HI, c * S:(c + 1) * S]), ALU.subtract).then_inc(am_.split, 1)
                    dve.wait_ge(am_.split, 2 * (h * CH + c) + 2)
                dve.wait_ge(acc_clear, h + 1)

                def add_down(step, c, i):
                    dve.wait_ge(y_ready, step * USES + i + 1)
                    at = ds(h * HT + c * TPB + i, 1)
                    nc.vector.tensor_tensor(x[:, at, :], ring(c, i)[:].rearrange("p (a c) -> p a c", a=1), x[:, at, :],
                                            ALU.add).then_inc(y_added, 1)

                def add_down_lora(step, c, k):
                    dve.wait_ge(y_ready, step * USES + TPB + k + 1)
                    acc = down_acc[:, k, c * S:(c + 1) * S]
                    nc.vector.tensor_tensor(acc, ring(c, TPB + k)[:], acc, ALU.add).then_inc(y_added, 1)

                def tile(f, s, first, last):
                    for c in range(CH):
                        step = h * STEPS + f * CH + c
                        before = (step - 1, 1 - c)
                        has_before = not (first and c == 0)

                        def hidden(var):
                            dve.wait_ge(silu_done, 3 * step + var + 1)
                            dve.wait_ge(up_ready, 3 * step + var + 1)
                            nc.vector.tensor_tensor(hid(c, var), hid(c, var), u_ps[c][:], ALU.mult).then_inc(hid_done, 1)

                        if not last:
                            prep(h, f + 1, 1 - s, 2 * c)
                        hidden(0)
                        if has_before:
                            for i in range(TPB):
                                add_down(*before, i)
                        hidden(1)
                        if not last:
                            prep(h, f + 1, 1 - s, 2 * c + 1)
                        if has_before:
                            for k in range(2):
                                add_down_lora(*before, k)
                        hidden(2)

                tiles(dve, h, tile)
                end = (h * STEPS + STEPS - 1, CH - 1)
                for i in range(TPB):
                    add_down(*end, i)
                for k in range(2):
                    add_down_lora(*end, k)
                dve.wait_ge(hid_split, 3 * (h + 1) * STEPS + 3)
                make_masks(h * 2 * HT + HT)
                dve.wait_ge(mask_copied, h * 2 * HT + 2 * HT + 1)
                dve.wait_ge(y_added, (h + 1) * STEPS * USES + 2)
                nc.vector.tensor_tensor(down_acc[:, 0, :], down_acc[:, 0, :], maskT[:, 0, :], ALU.mult)
                nc.vector.tensor_tensor(down_acc[:, 1, :], down_acc[:, 1, :], maskT[:, 1, :], ALU.mult)
                nc.vector.drain()
                nc.vector.tensor_tensor(down_acc[:, 0, :], down_acc[:, 0, :], down_acc[:, 1, :], ALU.add).then_inc(z_ready, 1)
                dve.wait_ge(z_hi, h + 1)
                nc.vector.tensor_tensor(am[:, 0, 0, LO, :], down_acc[:, 0, :], fp32(am[:, 0, 0, HI, :]), ALU.subtract).then_inc(z_split, 1)
                for i in range(HT):
                    dve.wait_ge(z_out, h * HT + i + 1)
                    at = h * HT + i
                    nc.vector.scalar_tensor_tensor(out=x[:, ds(at, 1), :], in0=y_ps[i % 2][:].rearrange("p (a c) -> p a c", a=1),
                                                   scalar=SCALING1, in1=x[:, ds(at, 1), :], op0=ALU.mult, op1=ALU.add).then_inc(z_added, 1)
                dve.wait_ge(z_added, (h + 1) * HT)


def program(nc, io):
    with nc.sbuf_tensor("x_tokens", [P, TILES, D], FP32) as x, nc.sbuf_tensor("identity", [P, P], FP32) as ident, \
            nc.sbuf_tensor("token_stats", [P, TILES, 6], FP32) as stats:
        phase_attention0(nc, io, x, ident, stats)
        phase_moe0(nc, io, x, ident, stats)
        phase_rope1(nc, io, x, ident, stats)
        phase_ffn1(nc, io, x, ident, stats)


_INS = ["x", "ctx_1024", "fside_BxSx2_0", "L0_xattn_Wq", "L0_xattn_bq", "L0_xattn_Wk", "L0_xattn_bk",
        "L0_ffn_gate_w", "L0_ffn_gate_proj", "L0_ffn_up_proj", "L0_ffn_down_proj",
        "L1_xattn_Wq", "L1_xattn_Wkv", "L1_xattn_Wout", "L1_xattn_bout",
        "L1_ffn_Wg", "L1_ffn_Wu", "L1_ffn_Wd", "L1_ffn_Wr", "L1_ffn_Ag", "L1_ffn_Bg", "L1_ffn_Au", "L1_ffn_Bu",
        "L1_ffn_Ad", "L1_ffn_Bd"]
_OUT = ((4, 512, 512), "float32")


def kernel(**inputs):
    import numpy as _np
    import concourse.bacc as _bacc
    from concourse import mybir as _mybir
    from concourse.bass_utils import run_bass_kernel_spmd as _run

    nc = _bacc.Bacc("TRN2", target_bir_lowering=False, num_devices=1)
    arrays, io = {}, {}
    for name in _INS:
        a = _np.ascontiguousarray(inputs[name])
        arrays[f"in_{name}"] = a
        io[name] = nc.dram_tensor(f"in_{name}", a.shape, _mybir.dt.from_np(a.dtype), kind="ExternalInput").ap()
    shape, dtype = _OUT
    io["out"] = nc.dram_tensor("out_0", shape, _mybir.dt.from_np(_np.dtype(dtype)), kind="ExternalOutput").ap()
    program(nc, io)
    r = _run(nc, [arrays], core_ids=[0])
    return r.results[0]["out_0"]
```

```python
import numpy as np

import concourse.bass as bass
from concourse import mybir

FP32 = mybir.dt.float32
FP32R = mybir.dt.float32r
ALU = mybir.AluOpType
ACT = mybir.ActivationFunctionType
AXIS_X = mybir.AxisListType.X

P = 128
B, S, D = 4, 512, 512
TOKENS = B * S
TILES = TOKENS // P
TPB = S // P
DK = D // P
CTX = 256
CK = CTX // P
QK0 = 128
EPS = 1e-5
DMA = 16

E0, F0 = 8, 352
E1, R1, DFF = 8, 16, 1408
SCALING1 = 2.0

HEADS, HD = 32, 16
ROPE_BASE = 10000.0
HI, LO = 0, 1


def ds(start, size):
    return bass.ds(start, size)


def fp32(ap):
    return ap.bitcast(FP32)


def product(nc, out, pairs):
    passes = [(l[a], r[b]) for l, r in pairs for a, b in ((HI, HI), (HI, LO), (LO, HI))]
    last = None
    for i, (l, r) in enumerate(passes):
        last = nc.tensor.matmul(out, l, r, start=(i == 0), stop=(i == len(passes) - 1))
    return last


def add_product(nc, out, l, r, start=False):
    last = None
    for i, (a, b) in enumerate(((HI, HI), (HI, LO), (LO, HI))):
        last = nc.tensor.matmul(out, l[a], r[b], start=(start and i == 0), stop=True, skip_group_check=True)
    return last


class TokenNorm:

    def __init__(self, nc, ctx, tag, stats):
        sb = lambda name, shape: ctx.enter_context(nc.sbuf_tensor(f"{tag}_{name}", shape, FP32))
        self.stats = stats
        self.moments = sb("moments", [P, TILES, 2])
        self.var, self.std, self.rstd = (sb(name, [P, TILES]) for name in ("var", "std", "rstd"))
        sem = lambda name: ctx.enter_context(nc.semaphore(f"{tag}_{name}"))
        self.var_ready = sem("var_ready")
        self.std_ready = sem("std_ready")
        self.xn_ready = sem("xn_ready")


def tile_stats(nc, stats, x, tile):
    nc.vector.bn_stats(stats[:, ds(tile, 1), :].rearrange("p t s -> p (t s)"),
                       x[:, ds(tile, 1), :].rearrange("p t d -> p (t d)"))


def token_var(nc, n):
    for t in range(TILES):
        nc.vector.bn_aggr(n.moments[:, t, :], n.stats[:, t, :])
    nc.vector.drain()
    nc.vector.tensor_scalar_add(n.var[:], n.moments[:, :, 1], EPS).then_inc(n.var_ready, 1)


def token_rstd(nc, dve, n):
    dve.wait_ge(n.std_ready, 1)
    nc.vector.reciprocal(n.rstd[:], n.std[:])
    nc.vector.drain()


def token_std(nc, act, n):
    act.wait_ge(n.var_ready, 1)
    nc.scalar.activation(n.std[:], n.var[:], ACT.Sqrt).then_inc(n.std_ready, 1)


def normalise_tile(nc, n, x, tile, out):
    nc.vector.tensor_scalar(out.rearrange("p (t d) -> p t d", t=1), x[:, ds(tile, 1), :], n.moments[:, ds(tile, 1), 0],
                            n.rstd[:, ds(tile, 1)], ALU.subtract, ALU.mult).then_inc(n.xn_ready, 1)


START = 1


def start_counts(engine, *sems):
    for s in sems:
        engine.sem_inc(s, START)


class Split:

    def __init__(self, nc, ctx, tag):
        sem = lambda name: ctx.enter_context(nc.semaphore(f"{tag}_{name}"))
        self.filled = sem("filled")
        self.hi_done = sem("hi_done")
        self.split = sem("split")


def split_hi(nc, act, s, job, hi, psum):
    act.wait_ge(s.filled, START + job + 1)
    nc.scalar.activation(hi, psum, ACT.Copy).then_inc(s.hi_done, 1)


def split_lo(nc, dve, s, job, lo, psum, hi):
    dve.wait_ge(s.hi_done, job + 1)
    nc.vector.tensor_tensor(lo, psum, fp32(hi), ALU.subtract).then_inc(s.split, 1)


def transposes(nc, s, bank, ins, ident):
    last = None
    at = 0
    for a in ins:
        rows, cols = a.shape[0], a.shape[1]
        last = nc.tensor.transpose(bank[0:cols, at:at + rows], a, ident[0:rows, 0:rows])
        at += rows
    last.then_inc(s.filled, 1)


def phase_attention0(nc, io, x, ident, stats):
    from contextlib import ExitStack
    x_dram = io["x"].rearrange("b (t p) d -> p (b t) d", p=P)
    ctx_dram = io["ctx_1024"].rearrange("b (t p) c -> p (b t) c", p=P)
    with ExitStack() as ctx:
        def sb(name, shape, dt=FP32):
            return ctx.enter_context(nc.sbuf_tensor(f"a0_{name}", shape, dt))

        def ps(name, shape):
            return ctx.enter_context(nc.psum_tensor(f"a0_{name}", shape, FP32))

        own_sems = []

        def sem(name):
            own_sems.append(nc.alloc_semaphore(name=f"a0_{name}"))
            return own_sems[-1]

        ctx.callback(nc.all_engine_barrier)
        ctx.callback(lambda: nc.clear_and_free_semaphores(own_sems))

        wq_raw = sb("wq_raw", [P, CTX])
        wk_raw = sb("wk_raw", [P, CTX])
        bias = sb("bias", [P, 2])
        wT = sb("wT", [P, 2, 2, CK, P], FP32R)
        ctx_raw = sb("ctx_raw", [P, TPB, CTX])
        ctxT = sb("ctxT", [P, 2, CK, S], FP32R)
        xnT = sb("xnT", [P, 2, DK, S], FP32R)
        qkT = sb("qkT", [P, 2, 2, S], FP32R)
        att = sb("att", [P, TPB, S])
        attT = sb("attT", [P, 2, DK, S], FP32R)
        rowmax = sb("rowmax", [P, TPB])
        negmax = sb("negmax", [P, TPB])
        rowsum = sb("rowsum", [P, TPB])
        rinv = sb("rinv", [P, TPB])
        stats_in = sb("stats_in", [P, TPB, 6])
        moments = sb("moments", [P, TPB, 2])
        var, std, rstd, shift = (sb(name, [P, TPB]) for name in ("var", "std", "rstd", "shift"))
        xn = sb("xn", [P, TPB, D])
        tp = [ps(f"tp{i}", [P, S]) for i in range(2)]
        mm = [ps(f"mm{i}", [P, S]) for i in range(2)]
        en = [ps(f"en{i}", [P, S]) for i in range(TPB)]
        t_ = Split(nc, ctx, "a0t")
        qk_ = Split(nc, ctx, "a0qk")
        w_in, x_in, ctx_in = sem("w_in"), sem("x_in"), sem("ctx_in")
        energy_ready, negmax_ready, exp_ready, att_ready = (
            sem("energy_ready"), sem("negmax_ready"), sem("exp_ready"), sem("att_ready"))
        mix_ready, x_added = sem("mix_ready"), sem("x_added")
        var_ready, std_ready, rstd_ready, xn_ready, rinv_ready = (
            sem("var_ready"), sem("std_ready"), sem("rstd_ready"), sem("xn_ready"), sem("rinv_ready"))
        ident_ready = sem("ident_ready")
        FIRST_JOBS, JOBS = 1 + CK, 2 * TPB + CK
        block = ctx.enter_context(nc.Block())

        def bank(job_in_batch):
            return tp[(FIRST_JOBS + job_in_batch) % 2]

        def by_block(psum):
            return psum[:].rearrange("p (k c) -> p k c", k=DK)

        @block.gpsimd
        def _(pool):
            nc.gpsimd.memset(ident[:], 0.0).then_inc(ident_ready, 1)
            pool.wait_ge(ident_ready, 1)
            nc.gpsimd.affine_select(out=ident[:], in_=ident[:], compare_op=ALU.not_equal, fill=1.0, base=0,
                                    pattern=[[-1, P]], channel_multiplier=1).then_inc(ident_ready, 1)

        @block.sync
        def _(sp):
            sp.dma_start(wq_raw[:], io["L0_xattn_Wq"]).then_inc(w_in, DMA)
            sp.dma_start(wk_raw[:], io["L0_xattn_Wk"]).then_inc(w_in, DMA)
            sp.dma_start(bias[:, 0:1], io["L0_xattn_bq"].rearrange("(p a) -> p a", a=1)).then_inc(w_in, DMA)
            sp.dma_start(bias[:, 1:2], io["L0_xattn_bk"].rearrange("(p a) -> p a", a=1)).then_inc(w_in, DMA)

            def load_x(b):
                sp.dma_start(x[:, ds(b * TPB, TPB), :], x_dram[:, ds(b * TPB, TPB), :]).then_inc(x_in, DMA)

            def load_context(b):
                sp.dma_start(ctx_raw[:], ctx_dram[:, ds(b * TPB, TPB), :]).then_inc(ctx_in, DMA)

            load_context(0)
            load_x(0)
            sp.wait_ge(x_in, DMA)
            load_x(1)
            sp.wait_ge(t_.filled, START + FIRST_JOBS)
            load_context(1)
            with sp.Fori(2, B) as b:
                sp.wait_ge(x_in, b * DMA)
                load_x(b)
                sp.wait_ge(t_.filled, START + FIRST_JOBS + (b - 2) * JOBS + CK)
                load_context(b)

        @block.tensor
        def _(pe):
            start_counts(pe, t_.filled, qk_.filled)
            def context(job, psum, b):
                pe.wait_ge(ctx_in, DMA * (b + 1))
                for k in range(CK):
                    pe.wait_ge(t_.split, START + job + k)
                    transposes(nc, t_, psum[k], [ctx_raw[:, t, k * P:(k + 1) * P] for t in range(TPB)], ident)

            def query_key(job, b, i):
                if i == 0:
                    pe.wait_ge(t_.split, START + job + 1)
                    if not isinstance(b, int):
                        pe.wait_ge(x_added, START + (b - 1) * TPB)
                product(nc, mm[i][:], [([wT[:, h, i, k, :] for h in (HI, LO)],
                                        [ctxT[:, h, k, :] for h in (HI, LO)]) for k in range(CK)]
                        ).then_inc(qk_.filled, 1)

            def energy(b):
                pe.wait_ge(qk_.split, START + 2 * b + 2)
                pe.wait_ge(exp_ready, b * TPB)
                for m in range(TPB):
                    product(nc, en[m][:], [([qkT[:, h, 0, m * P:(m + 1) * P] for h in (HI, LO)],
                                            [qkT[:, h, 1, :] for h in (HI, LO)])]).then_inc(energy_ready, 1)

            def batch(b, last):
                job = FIRST_JOBS + b * JOBS
                ahead = 0 if last else CK
                if not last:
                    context(job, [bank(k) for k in range(CK)], b + 1)
                for t in range(TPB):
                    pe.wait_ge(xn_ready, b * TPB + t + 1)
                    pe.wait_ge(t_.split, START + job + ahead + t)
                    transposes(nc, t_, bank(ahead + t), [xn[:, t, k * P:(k + 1) * P] for k in range(DK)], ident)
                    if t % 2 and not last:
                        query_key(job + CK, b + 1, t // 2)
                for m in range(TPB):
                    at = ahead + TPB + m
                    pe.wait_ge(att_ready, b * TPB + m + 1)
                    pe.wait_ge(t_.split, START + job + at)
                    transposes(nc, t_, bank(at), [att[:, m, k * P:(k + 1) * P] for k in range(DK)], ident)
                if not last:
                    energy(b + 1)
                pe.wait_ge(t_.split, START + job + ahead + 2 * TPB + 1)
                for t in range(TPB):
                    if t >= 2:
                        pe.wait_ge(x_added, START + b * TPB + t - 1)
                    product(nc, mm[t % 2][:], [([xnT[:, h, k, t * P:(t + 1) * P] for h in (HI, LO)],
                                                [attT[:, h, k, :] for h in (HI, LO)]) for k in range(DK)]
                            ).then_inc(mix_ready, 1)

            pe.wait_ge(ident_ready, 2)
            pe.wait_ge(w_in, 4 * DMA)
            transposes(nc, t_, tp[0], [w[:, k * P:(k + 1) * P] for w in (wq_raw, wk_raw) for k in range(CK)], ident)
            context(1, [tp[(1 + k) % 2] for k in range(CK)], 0)
            for i in range(2):
                query_key(FIRST_JOBS, 0, i)
            energy(0)
            with pe.Fori(0, B - 1) as b:
                batch(b, False)
            pe.wait_ge(x_added, START + (B - 1) * TPB)
            batch(B - 1, True)

        @block.scalar
        def _(act):
            def context(job, psum):
                for k in range(CK):
                    split_hi(nc, act, t_, job + k, ctxT[:, HI, k, :], psum[k][:])

            def query_key(b, i):
                act.wait_ge(qk_.filled, START + 2 * b + i + 1)
                nc.scalar.activation(qkT[:, HI, i, :], mm[i][:], ACT.Identity,
                                     bias=bias[:, i:i + 1]).then_inc(qk_.hi_done, 1)

            def softmax_and_norm(b):
                for m in range(TPB):
                    act.wait_ge(negmax_ready, b * TPB + m + 1)
                    nc.scalar.activation(att[:, m, :], en[m][:], ACT.Exp, bias=negmax[:, m:m + 1],
                                         accum_out=rowsum[:, m:m + 1]).then_inc(exp_ready, 1)
                act.wait_ge(var_ready, b + 1)
                nc.scalar.activation(std[:], var[:], ACT.Sqrt).then_inc(std_ready, 1)
                act.wait_ge(rstd_ready, b + 1)
                for t in range(TPB):
                    nc.scalar.activation(xn[:, t, :].rearrange("p (a d) -> p a d", a=1), x[:, ds(b * TPB + t, 1), :],
                                         ACT.Identity, bias=shift[:, t:t + 1], scale=rstd[:, t:t + 1]).then_inc(xn_ready, 1)
                act.wait_ge(rinv_ready, b + 1)
                for m in range(TPB):
                    nc.scalar.activation(att[:, m, :], att[:, m, :], ACT.Copy, scale=rinv[:, m:m + 1]).then_inc(att_ready, 1)

            def batch(b, last):
                job = FIRST_JOBS + b * JOBS
                ahead = 0 if last else CK
                if not last:
                    context(job, [bank(k) for k in range(CK)])
                for t in range(TPB):
                    split_hi(nc, act, t_, job + ahead + t, xnT[:, HI, :, t * P:(t + 1) * P], by_block(bank(ahead + t)))
                    if t % 2 and not last:
                        query_key(b + 1, t // 2)
                for m in range(TPB):
                    at = ahead + TPB + m
                    split_hi(nc, act, t_, job + at, attT[:, HI, :, m * P:(m + 1) * P], by_block(bank(at)))
                if not last:
                    softmax_and_norm(b + 1)

            split_hi(nc, act, t_, 0, wT[:, HI].rearrange("p a k c -> p (a k c)"), tp[0][:])
            context(1, [tp[(1 + k) % 2] for k in range(CK)])
            for i in range(2):
                query_key(0, i)
            softmax_and_norm(0)
            with act.Fori(0, B - 1) as b:
                batch(b, False)
            batch(B - 1, True)

        @block.vector
        def _(dve):
            start_counts(dve, t_.split, qk_.split, x_added)
            def context(job, psum):
                for k in range(CK):
                    split_lo(nc, dve, t_, job + k, ctxT[:, LO, k, :], psum[k][:], ctxT[:, HI, k, :])

            def query_key(b, i):
                dve.wait_ge(qk_.hi_done, 2 * b + i + 1)
                nc.vector.scalar_tensor_tensor(out=qkT[:, LO, i, :], in0=mm[i][:], scalar=bias[:, i:i + 1],
                                               in1=fp32(qkT[:, HI, i, :]), op0=ALU.add,
                                               op1=ALU.subtract).then_inc(qk_.split, 1)

            def maxima(b):
                for m in range(TPB):
                    dve.wait_ge(energy_ready, b * TPB + m + 1)
                    nc.vector.reduce_max(rowmax[:, m:m + 1], en[m][:], AXIS_X)
                    nc.vector.drain()
                    nc.vector.tensor_scalar(negmax[:, m:m + 1], rowmax[:, m:m + 1], -1.0, None,
                                            ALU.mult).then_inc(negmax_ready, 1)

            def sums(b):
                dve.wait_ge(exp_ready, (b + 1) * TPB)
                nc.vector.reciprocal(rinv[:], rowsum[:]).then_inc(rinv_ready, 1)

            def variances(b):
                dve.wait_ge(x_in, DMA * (b + 1))
                for t in range(TPB):
                    nc.vector.bn_stats(stats_in[:, t, :], x[:, ds(b * TPB + t, 1), :].rearrange("p a d -> p (a d)"))
                nc.vector.drain()
                for t in range(TPB):
                    nc.vector.bn_aggr(moments[:, t, :], stats_in[:, t, :])
                nc.vector.drain()
                nc.vector.tensor_scalar_add(var[:], moments[:, :, 1], EPS).then_inc(var_ready, 1)

            def reciprocals(b):
                dve.wait_ge(std_ready, b + 1)
                nc.vector.reciprocal(rstd[:], std[:])
                nc.vector.drain()
                nc.vector.scalar_tensor_tensor(out=shift[:], in0=moments[:, :, 0], scalar=-1.0, in1=rstd[:],
                                               op0=ALU.mult, op1=ALU.mult).then_inc(rstd_ready, 1)

            def final_stats(b, t):
                dve.wait_ge(x_added, START + b * TPB + t + 1)
                tile_stats(nc, stats, x, b * TPB + t)

            def batch(b, last):
                job = FIRST_JOBS + b * JOBS
                ahead = 0 if last else CK
                if not last:
                    context(job, [bank(k) for k in range(CK)])
                for t in range(TPB):
                    split_lo(nc, dve, t_, job + ahead + t, xnT[:, LO, :, t * P:(t + 1) * P], by_block(bank(ahead + t)),
                             xnT[:, HI, :, t * P:(t + 1) * P])
                    if t % 2 and not last:
                        query_key(b + 1, t // 2)
                for m in range(TPB):
                    at = ahead + TPB + m
                    split_lo(nc, dve, t_, job + at, attT[:, LO, :, m * P:(m + 1) * P], by_block(bank(at)),
                             attT[:, HI, :, m * P:(m + 1) * P])
                if not last:
                    maxima(b + 1)
                    variances(b + 1)
                for t in range(TPB):
                    dve.wait_ge(mix_ready, b * TPB + t + 1)
                    tile = x[:, ds(b * TPB + t, 1), :]
                    nc.vector.tensor_tensor(tile, mm[t % 2][:].rearrange("p (a c) -> p a c", a=1), tile,
                                            ALU.add).then_inc(x_added, 1)
                    if t == 0 and not last:
                        reciprocals(b + 1)
                        sums(b + 1)
                    if t:
                        final_stats(b, t - 1)
                final_stats(b, TPB - 1)

            dve.sem_inc(t_.split, 1)
            split_lo(nc, dve, t_, 0, wT[:, LO].rearrange("p a k c -> p (a k c)"), tp[0][:],
                     wT[:, HI].rearrange("p a k c -> p (a k c)"))
            context(1, [tp[(1 + k) % 2] for k in range(CK)])
            variances(0)
            for i in range(2):
                query_key(0, i)
            maxima(0)
            reciprocals(0)
            sums(0)
            with dve.Fori(0, B - 1) as b:
                batch(b, False)
            batch(B - 1, True)


def top_two(nc, dve, logits, rev, t):
    def wide(a):
        return a[:].unsqueeze(2).to_broadcast(list(logits.shape))

    for source, top, hot in ((logits, t.top1, t.hot1), (t.rest, t.top2, t.hot2)):
        nc.vector.reduce_max(top[:], source[:], AXIS_X)
        nc.vector.drain()
        nc.vector.tensor_tensor(t.score[:], source[:], wide(top), ALU.is_equal)
        nc.vector.drain()
        nc.vector.tensor_tensor(t.score[:], t.score[:], rev[:], ALU.mult)
        nc.vector.drain()
        nc.vector.reduce_max(t.best[:], t.score[:], AXIS_X)
        nc.vector.drain()
        nc.vector.tensor_tensor(hot[:], t.score[:], wide(t.best), ALU.is_equal)
        nc.vector.drain()
        if source is logits:
            nc.vector.scalar_tensor_tensor(out=t.rest[:], in0=hot[:], scalar=-3e38, in1=logits[:],
                                           op0=ALU.mult, op1=ALU.add)
            nc.vector.drain()


class TopTwo:
    def __init__(self, nc, ctx, tag, tiles, experts):
        def sb(name, shape):
            return ctx.enter_context(nc.sbuf_tensor(f"{tag}_{name}", shape, FP32))
        self.score, self.rest, self.hot1, self.hot2 = (
            sb(name, [P, tiles, experts]) for name in ("score", "rest", "hot1", "hot2"))
        self.top1, self.top2, self.best, self.gap, self.e, self.w1, self.w2, self.den = (
            sb(name, [P, tiles]) for name in ("top1", "top2", "best", "gap", "e", "w1", "w2", "den"))


def phase_moe0(nc, io, x, ident, stats):
    from contextlib import ExitStack
    gate_dram, up_dram, down_dram = io["L0_ffn_gate_proj"], io["L0_ffn_up_proj"], io["L0_ffn_down_proj"]
    NB = B
    GROUP_E = 4
    GROUP_TILES = GROUP_E * F0 // P
    GROUPS_E = E0 // GROUP_E
    HIDDEN_TILES = GROUPS_E * GROUP_TILES
    GROUP_STEPS = GROUP_TILES * NB
    SLOTS = 3
    PREP = 3

    def slot(pos):
        return pos % GROUP_TILES % SLOTS

    def pieces(pos):
        out, row = [], pos * P
        while row < (pos + 1) * P:
            e, f = row // F0, row % F0
            rows = min(F0 - f, (pos + 1) * P - row)
            out.append((e, f, row - pos * P, rows))
            row += rows
        return out

    def loaded(group, pos, per_tile):
        group, pos = group + pos // GROUP_TILES, pos % GROUP_TILES
        same = [p for p in range(GROUP_TILES) if slot(p) == slot(pos)]
        return (group * sum(per_tile(p) for p in same) + sum(per_tile(p) for p in same if p <= pos)) * DMA

    def raw_loads(pos):
        return 2 + len(pieces(pos))

    def weight_loads(pos):
        return len(pieces(pos))

    gate_rows, up_rows = (d.rearrange("e f d -> (e f) d") for d in (gate_dram, up_dram))
    weights_dram = nc.dram_tensor("expert_weights", [TILES, E0, P], FP32, kind="Internal").ap()
    with ExitStack() as ctx:
        def sb(name, shape, dt=FP32):
            return ctx.enter_context(nc.sbuf_tensor(f"m_{name}", shape, dt))

        def ps(name, shape):
            return ctx.enter_context(nc.psum_tensor(f"m_{name}", shape, FP32))

        def sem(name):
            return ctx.enter_context(nc.semaphore(f"m_{name}"))

        xnT = sb("xnT", [P, 2, DK, TOKENS], FP32R)
        gw_raw = sb("gw_raw", [E0, D])
        gwT = sb("gwT", [P, 2, DK, E0], FP32R)
        rl = sb("rl", [P, S])
        logits = sb("logits", [P, TILES, E0])
        rev = sb("rev", [P, TILES, E0])
        weight = sb("weight", [P, TILES, E0])
        weightT = sb("weightT", [TILES * E0, P])
        gate_raw = [sb(f"gate_raw{j}", [P, D]) for j in range(SLOTS)]
        up_raw = [sb(f"up_raw{j}", [P, D]) for j in range(SLOTS)]
        down_raw = [sb(f"down_raw{j}", [P, DK, P]) for j in range(SLOTS)]
        gateT = [sb(f"gateT{j}", [P, 2, DK, P], FP32R) for j in range(SLOTS)]
        upT = [sb(f"upT{j}", [P, 2, DK, P], FP32R) for j in range(SLOTS)]
        downT = [sb(f"downT{j}", [P, 2, D], FP32R) for j in range(SLOTS)]
        row_weight = [sb(f"row_weight{j}", [P, TILES, P]) for j in range(SLOTS)]
        silu = [sb(f"silu{i}", [P, S]) for i in range(2)]
        hid = [sb(f"hid{i}", [P, S]) for i in range(2)]
        hidS = [sb(f"hidS{i}", [P, 2, S], FP32R) for i in range(2)]
        n = TokenNorm(nc, ctx, "mn", stats)
        xn = row_weight[SLOTS - 1][:].rearrange("p (t a) c -> p t (a c)", t=TPB)
        t = TopTwo(nc, ctx, "mt", TILES, E0)
        g_ps = [ps(f"g{i}", [P, S]) for i in range(2)]
        u_ps = [ps(f"u{i}", [P, S]) for i in range(2)]
        y_ps = [ps(f"y{i}", [P, D]) for i in range(3)]
        prep_ps = ps("prep", [P, D])
        prep_ = Split(nc, ctx, "mp")
        xt_ = Split(nc, ctx, "mx")
        gw_in = sem("gw_in")
        raw_in = [sem(f"raw_in{j}") for j in range(SLOTS)]
        weights_in = [sem(f"weights_in{j}") for j in range(SLOTS)]
        weight_made, weight_turned, weight_copied, weight_stored, weighted = (
            sem("weight_made"), sem("weight_turned"), sem("weight_copied"), sem("weight_stored"), sem("weighted"))
        router_ready, router_copied, logits_ready, logits_done = (
            sem("router_ready"), sem("router_copied"), sem("logits_ready"), sem("logits_done"))
        gap_ready, gap_exp, rl_clear = sem("gap_ready"), sem("gap_exp"), sem("rl_clear")
        gate_ready, up_ready, silu_done, hid_done, hid_hi, hid_split = (
            sem("gate_ready"), sem("up_ready"), sem("silu_done"), sem("hid_done"), sem("hid_hi"), sem("hid_split"))
        y_ready, y_added = sem("y_ready"), sem("y_added")
        block = ctx.enter_context(nc.Block())

        def prep_views(j, part, bank=prep_ps):
            if part < 2:
                raw, to = ((gate_raw, gateT), (up_raw, upT))[part]
                return ([raw[j][:, k * P:(k + 1) * P] for k in range(DK)],
                        bank[:].rearrange("p (k c) -> p k c", k=DK), [to[j][:, h] for h in (HI, LO)])
            return [down_raw[j][:, k, :] for k in range(DK)], bank[:], [downT[j][:, h] for h in (HI, LO)]

        def first_bank(job):
            return (prep_ps, u_ps[0])[job % 2]

        @block.sync
        def _(sp):
            def load_raw(source, pos):
                j, pos = slot(pos), pos % GROUP_TILES
                rows = ds(source * (GROUP_TILES * P) + pos * P, P)
                sp.dma_start(gate_raw[j][:], gate_rows[rows, :]).then_inc(raw_in[j], DMA)
                sp.dma_start(up_raw[j][:], up_rows[rows, :]).then_inc(raw_in[j], DMA)
                for e, f, row, n_rows in pieces(pos):
                    sp.dma_start(down_raw[j][:, :, row:row + n_rows],
                                 down_dram[ds(source * GROUP_E + e, 1), :, f:f + n_rows]
                                 .rearrange("e (k p) f -> p (e k) f", p=P)).then_inc(raw_in[j], DMA)

            def load_weights(source, pos):
                j, pos = slot(pos), pos % GROUP_TILES
                for e, f, row, n_rows in pieces(pos):
                    sp.dma_start(row_weight[j][row:row + n_rows],
                                 weights_dram[:, ds(source * GROUP_E + e, 1), :].rearrange("t e p -> e t p")
                                 .to_broadcast([n_rows, TILES, P])).then_inc(weights_in[j], DMA)

            sp.dma_start(gw_raw[:], io["L0_ffn_gate_w"]).then_inc(gw_in, DMA)
            load_raw(0, 0)
            load_raw(0, 1)
            sp.wait_ge(weight_copied, 1)
            sp.dma_start(weights_dram.rearrange("t e p -> (t e) p"), weightT[:]).then_inc(weight_stored, DMA)
            sp.wait_ge(weight_stored, DMA)
            load_weights(0, 0)
            with sp.Fori(0, GROUPS_E) as g:
                for pos in range(GROUP_TILES):
                    tile = g * GROUP_TILES + pos
                    source = lambda ahead: g if pos + ahead < GROUP_TILES else g * -1 + (GROUPS_E - 1)
                    sp.wait_ge(prep_.filled, START + (tile + 1) * PREP)
                    load_raw(source(2), pos + 2)
                    sp.wait_ge(weighted, START + tile * NB)
                    load_weights(source(1), pos + 1)
            for j in range(SLOTS):
                last = max(q for q in range(HIDDEN_TILES + 2) if slot(q) == j)
                sp.wait_ge(raw_in[j], loaded(0, last, raw_loads))
                last = max(q for q in range(HIDDEN_TILES + 1) if slot(q) == j)
                sp.wait_ge(weights_in[j], loaded(0, last, weight_loads))

        @block.tensor
        def _(pe):
            start_counts(pe, xt_.filled, prep_.filled)
            def prep(job, j, part):
                pe.wait_ge(prep_.split, START + job)
                transposes(nc, prep_, prep_ps, prep_views(j, part)[0], ident)

            def tile(b, k):
                pe.wait_ge(n.xn_ready, b * TPB + k + 1)
                pe.wait_ge(xt_.split, START + b * TPB + k + 1)
                transposes(nc, xt_, y_ps[(k + 1) % 2], [xn[:, k, i * P:(i + 1) * P] for i in range(DK)], ident)

            def router(b, k):
                if k == 0:
                    pe.wait_ge(xt_.split, START + b * TPB + TPB + 2)
                    pe.wait_ge(router_copied, START + b)
                last = add_product(nc, g_ps[0][0:E0, :], [gwT[:, h, k, :] for h in (HI, LO)],
                                   [xnT[:, h, k, ds(b * S, S)] for h in (HI, LO)], start=(k == 0))
                if k == DK - 1:
                    last.then_inc(router_ready, 1)

            def turn_logits(b):
                pe.wait_ge(router_copied, START + b + 1)
                pe.wait_ge(logits_done, START + b)
                last = None
                for k in range(TPB):
                    last = nc.tensor.transpose(g_ps[1][:, k * P:(k + 1) * P], rl[:, k * P:(k + 1) * P], ident[:])
                last.then_inc(logits_ready, 1)

            pe.wait_ge(gw_in, DMA)
            transposes(nc, xt_, y_ps[0], [gw_raw[:, k * P:(k + 1) * P] for k in range(DK)], ident)
            for k in range(TPB):
                tile(0, k)
            with pe.Fori(1, NB) as b:
                for k in range(TPB - 1):
                    tile(b, k)
                    router(b - 1, k)
                router(b - 1, DK - 1)
                tile(b, TPB - 1)
                turn_logits(b - 1)
            for k in range(DK):
                router(NB - 1, k)
            turn_logits(NB - 1)
            pe.wait_ge(raw_in[0], loaded(0, 0, raw_loads))
            for part in range(PREP):
                if part >= 2:
                    pe.wait_ge(prep_.split, START + part - 1)
                transposes(nc, prep_, first_bank(part), prep_views(0, part)[0], ident)
            pe.wait_ge(weight_made, 1)
            nc.tensor.transpose(g_ps[1][:, 0:P], weight[:].rearrange("p t e -> p (t e)"), ident[:]).then_inc(weight_turned, 1)
            pe.wait_ge(weight_copied, 1)

            def down(g, local):
                step = g * GROUP_STEPS + local
                j, c = slot(local // NB), local % NB
                pe.wait_ge(hid_split, step + 1)
                for i in range(TPB):
                    pe.wait_ge(y_added, step * TPB + i + (1 if local == 0 and i < 2 else 0))
                    product(nc, y_ps[(local * TPB + i) % 3][:],
                            [([hidS[c % 2][:, h, i * P:(i + 1) * P] for h in (HI, LO)],
                              [downT[j][:, h, :] for h in (HI, LO)])]).then_inc(y_ready, 1)

            with pe.Fori(0, GROUPS_E) as g:
                for pos in range(GROUP_TILES):
                    j = slot(pos)
                    tile = g * GROUP_TILES + pos
                    pe.wait_ge(prep_.split, START + (tile + 1) * PREP)
                    for c in range(NB):
                        local = pos * NB + c
                        pe.wait_ge(hid_done, START + g * GROUP_STEPS + local)
                        for to, w, ready in ((g_ps, gateT, gate_ready), (u_ps, upT, up_ready)):
                            product(nc, to[c % 2][:], [([w[j][:, h, k, :] for h in (HI, LO)],
                                                        [xnT[:, h, k, c * S:(c + 1) * S] for h in (HI, LO)])
                                                       for k in range(DK)]).then_inc(ready, 1)
                        if local:
                            down(g, local - 1)
                        if c < PREP:
                            if c == 0:
                                pe.wait_ge(raw_in[slot(pos + 1)], loaded(g, pos + 1, raw_loads))
                            prep((tile + 1) * PREP + c, slot(pos + 1), c)
                down(g, GROUP_STEPS - 1)

        @block.scalar
        def _(act):
            start_counts(act, router_copied)
            def prep(job, j, part, bank=prep_ps):
                _, psum, (hi, lo) = prep_views(j, part, bank)
                split_hi(nc, act, prep_, job, hi, psum)

            def tile(b, k):
                split_hi(nc, act, xt_, 1 + b * TPB + k, xnT[:, HI, :, ds((b * TPB + k) * P, P)],
                         y_ps[(k + 1) % 2][:].rearrange("p (k c) -> p k c", k=DK))

            def copy_router(b):
                act.wait_ge(router_ready, b + 1)
                nc.scalar.activation(rl[0:E0, :], g_ps[0][0:E0, :], ACT.Copy).then_inc(router_copied, 1)

            token_std(nc, act, n)
            split_hi(nc, act, xt_, 0, gwT[:, HI].rearrange("p k e -> p (k e)"), y_ps[0][:, 0:DK * E0])
            act.wait_ge(rl_clear, 1)
            for k in range(TPB):
                tile(0, k)
            with act.Fori(1, NB) as b:
                for k in range(TPB - 1):
                    tile(b, k)
                copy_router(b - 1)
                tile(b, TPB - 1)
            copy_router(NB - 1)
            for part in range(2):
                prep(part, 0, part, first_bank(part))
            act.wait_ge(gap_ready, 1)
            nc.scalar.activation(t.e[:], t.gap[:], ACT.Exp).then_inc(gap_exp, 1)
            prep(2, 0, 2, first_bank(2))

            act.wait_ge(weight_turned, 1)
            nc.scalar.activation(weightT[:], g_ps[1][:, 0:P], ACT.Copy).then_inc(weight_copied, 1)

            with act.Fori(0, GROUPS_E) as g:
                for pos in range(GROUP_TILES):
                    tile = g * GROUP_TILES + pos
                    for c in range(NB):
                        step = tile * NB + c
                        act.wait_ge(gate_ready, step + 1)
                        act.wait_ge(hid_done, START + step)
                        nc.scalar.activation(silu[c % 2][:], g_ps[c % 2][:], ACT.Silu).then_inc(silu_done, 1)
                        act.wait_ge(hid_done, START + step + 2)
                        nc.scalar.activation(hidS[c % 2][:, HI, :], hid[c % 2][:], ACT.Copy).then_inc(hid_hi, 1)
                        if c < PREP:
                            prep((tile + 1) * PREP + c, slot(pos + 1), c)

        @block.gpsimd
        def _(pool):
            start_counts(pool, weighted)
            with pool.Fori(0, GROUPS_E) as g:
                for pos in range(GROUP_TILES):
                    for c in range(NB):
                        step = (g * GROUP_TILES + pos) * NB + c
                        if c == 0:
                            pool.wait_ge(weights_in[slot(pos)], loaded(g, pos, weight_loads))
                        pool.wait_ge(silu_done, step + 1)
                        nc.gpsimd.tensor_tensor(silu[c % 2][:], silu[c % 2][:],
                                                row_weight[slot(pos)][:, c * TPB:(c + 1) * TPB, :].rearrange("p t c -> p (t c)"),
                                                ALU.mult).then_inc(weighted, 1)

        @block.vector
        def _(dve):
            start_counts(dve, xt_.split, prep_.split, hid_done, logits_done)
            def prep(job, j, part, bank=prep_ps):
                _, psum, (hi, lo) = prep_views(j, part, bank)
                split_lo(nc, dve, prep_, job, lo, psum, hi)

            nc.vector.memset(rl[:], 0.0).then_inc(rl_clear, 1)
            dve.sem_inc(xt_.split, 1)
            dve.sem_inc(hid_done, 1)
            dve.sem_inc(y_added, 2)
            for i in range(E0):
                nc.vector.memset(rev[:, :, i:i + 1], float(E0 - i))

            def tiles(b, last=False):
                for k in range(TPB):
                    split_lo(nc, dve, xt_, 1 + b * TPB + k, xnT[:, LO, :, ds((b * TPB + k) * P, P)],
                             y_ps[(k + 1) % 2][:].rearrange("p (k c) -> p k c", k=DK),
                             xnT[:, HI, :, ds((b * TPB + k) * P, P)])
                    if not last:
                        normalise_tile(nc, n, x, (b + 1) * TPB + k, xn[:, k, :])

            def copy_logits(b):
                dve.wait_ge(logits_ready, b + 1)
                nc.vector.tensor_copy(logits[:, ds(b * TPB, TPB), :],
                                      g_ps[1][:].rearrange("p (k e) -> p k e", k=TPB)[:, :, 0:E0]).then_inc(logits_done, 1)

            token_var(nc, n)
            token_rstd(nc, dve, n)
            for k in range(TPB):
                normalise_tile(nc, n, x, k, xn[:, k, :])
            split_lo(nc, dve, xt_, 0, gwT[:, LO].rearrange("p k e -> p (k e)"), y_ps[0][:, 0:DK * E0],
                     gwT[:, HI].rearrange("p k e -> p (k e)"))
            tiles(0)
            with dve.Fori(1, NB - 1) as b:
                tiles(b)
                copy_logits(b - 1)
            tiles(NB - 1, last=True)
            copy_logits(NB - 2)
            copy_logits(NB - 1)
            nc.vector.drain()
            top_two(nc, dve, logits, rev, t)
            nc.vector.tensor_tensor(t.gap[:], t.top2[:], t.top1[:], ALU.subtract).then_inc(gap_ready, 1)
            dve.wait_ge(gap_exp, 1)
            nc.vector.tensor_scalar_add(t.den[:], t.e[:], 1.0)
            nc.vector.drain()
            nc.vector.reciprocal(t.w1[:], t.den[:])
            nc.vector.drain()
            nc.vector.tensor_tensor(t.w2[:], t.e[:], t.w1[:], ALU.mult)
            nc.vector.drain()
            wide = lambda a: a[:].unsqueeze(2).to_broadcast([P, TILES, E0])
            nc.vector.tensor_tensor(t.hot1[:], t.hot1[:], wide(t.w1), ALU.mult)
            nc.vector.tensor_tensor(t.hot2[:], t.hot2[:], wide(t.w2), ALU.mult)
            nc.vector.drain()
            nc.vector.tensor_tensor(weight[:], t.hot1[:], t.hot2[:], ALU.add).then_inc(weight_made, 1)
            for part in range(PREP):
                prep(part, 0, part, first_bank(part))

            def add(g, local, i):
                dve.wait_ge(y_ready, (g * GROUP_STEPS + local) * TPB + i + 1)
                at = local % NB * TPB + i
                nc.vector.tensor_tensor(x[:, at, :], y_ps[(local * TPB + i) % 3][:], x[:, at, :], ALU.add).then_inc(y_added, 1)

            def chunk_stats(c):
                for i in range(TPB):
                    tile_stats(nc, stats, x, c * TPB + i)

            with dve.Fori(0, GROUPS_E) as g:
                for pos in range(GROUP_TILES):
                    tile = g * GROUP_TILES + pos
                    for c in range(NB):
                        local = pos * NB + c
                        step = g * GROUP_STEPS + local
                        dve.wait_ge(weighted, START + step + 1)
                        dve.wait_ge(up_ready, step + 1)
                        nc.vector.tensor_tensor(hid[c % 2][:], u_ps[c % 2][:], silu[c % 2][:], ALU.mult).then_inc(hid_done, 1)
                        if local:
                            add(g, local - 1, 0)
                        dve.wait_ge(hid_hi, step + 1)
                        nc.vector.tensor_tensor(hidS[c % 2][:, LO, :], hid[c % 2][:], fp32(hidS[c % 2][:, HI, :]),
                                                ALU.subtract).then_inc(hid_split, 1)
                        if local:
                            for i in range(1, TPB):
                                add(g, local - 1, i)
                        if pos == GROUP_TILES - 1 and c >= 2:
                            dve.wait_ge(y_added, (step - 1) * TPB + 2)
                            chunk_stats(c - 2)
                        if c < PREP:
                            prep((tile + 1) * PREP + c, slot(pos + 1), c)
                for i in range(TPB):
                    add(g, GROUP_STEPS - 1, i)
                dve.wait_ge(y_added, (g + 1) * (GROUP_STEPS * TPB) + 2)
                chunk_stats(NB - 2)
                chunk_stats(NB - 1)


GROUP = 4
GROUPS = B * HEADS // GROUP
QROWS, KROWS = 3 * HD + 2, 3 * HD
PAD = 32


def scratch(nc):
    def dram(name, shape, dt):
        return nc.dram_tensor(name, shape, dt, kind="Internal").ap()
    return {"q": dram("q_stack", [B * HEADS, QROWS, S], FP32),
            "k": dram("k_stack", [B * HEADS, KROWS, S], FP32),
            "v": dram("v_pad", [GROUPS, S, GROUP * PAD], FP32)}


QK_TILES = HEADS * HD // P
STORES = 6 * QK_TILES


class OddBatch:

    def __init__(self, nc, ctx):
        self.qkT = [ctx.enter_context(nc.sbuf_tensor(f"q_qkT{i}1", [P, 2, QK_TILES, S], FP32R)) for i in range(2)]
        self.stored = ctx.enter_context(nc.semaphore("q_odd_stored"))


def store_qk(sp, scr, qkT, batch, stored, which=range(STORES)):
    for j in which:
        i, block_row, ht = j // (3 * QK_TILES), j // QK_TILES % 3, j % QK_TILES
        part = ((HI, HI, LO), (HI, LO, HI))[i][block_row]
        to = scr["qk"[i]][ds(batch * HEADS, HEADS), block_row * HD:(block_row + 1) * HD, :]
        sp.dma_start(to[ht * (P // HD):(ht + 1) * (P // HD)], fp32(qkT[i][:, part, ht, :])).then_inc(stored, DMA)


def phase_qkv1(nc, io, x, ident, stats, odd):
    from contextlib import ExitStack
    io["scratch"] = scr = scratch(nc)
    ctx_dram = io["ctx_1024"].rearrange("b (t p) c -> p (b t) c", p=P)
    pos_dram = io["fside_BxSx2_0"].rearrange("b (t p) a -> p (b t) a", p=P)
    TWO_PI = 2.0 * np.pi
    c1 = float(np.float32(np.floor(TWO_PI * 2 ** 8) / 2 ** 8))
    c2 = float(np.floor((TWO_PI - c1) * 2 ** 20) / 2 ** 20)
    c3 = float(np.float32(TWO_PI - c1 - c2))
    ROUND = 1.5 * 2 ** 23
    PI_F = float(np.nextafter(np.float32(np.pi), np.float32(0)))
    AX, HALF = 2, HD // 4
    FREQS = [float(np.float32(ROPE_BASE) ** np.float32(-j / HALF)) for j in range(HALF)]
    HT = QK_TILES
    with ExitStack() as ctx:
        def sb(name, shape, dt=FP32):
            return ctx.enter_context(nc.sbuf_tensor(f"q_{name}", shape, dt))

        def ps(name, shape):
            return ctx.enter_context(nc.psum_tensor(f"q_{name}", shape, FP32))

        def sem(name):
            return ctx.enter_context(nc.semaphore(f"q_{name}"))

        wq_raw = sb("wq_raw", [P, DK, D])
        wkv_raw = sb("wkv_raw", [P, CK, 2 * D])
        wq = sb("wq", [P, 2, DK, D], FP32R)
        wkv = sb("wkv", [P, 2, CK, 2 * D], FP32R)
        pos = sb("pos", [P, TILES, AX])
        ang, turns, red, mag, sine, cosine, nsine = (
            sb(name, [P, TILES, AX * HALF]) for name in ("ang", "turns", "red", "mag", "sine", "cosine", "nsine"))
        cos2 = sb("cos2", [P, TILES, HD])
        ctx_raw = sb("ctx_raw", [P, 2 * TPB, CTX])
        xn = [sb(f"xn{i}", [P, D]) for i in range(2)]
        xnT = [sb(f"xnT{i}", [P, 2, DK, P], FP32R) for i in range(2)]
        ctxT = [sb(f"ctxT{i}", [P, 2, CK, P], FP32R) for i in range(2)]
        by_cos = [sb(f"by_cos{i}", [P, HEADS, HD]) for i in range(2)]
        by_sin = [sb(f"by_sin{i}", [P, HEADS, HD]) for i in range(2)]
        rot = [sb(f"rot{i}", [P, HEADS * HD]) for i in range(2)]
        qkT = [[sb(f"qkT{i}0", [P, 2, HT, S], FP32R) for i in range(2)], odd.qkT]
        vpad = [sb(f"vpad{i}", [P, HEADS, PAD]) for i in range(2)]
        zeros = sb("zeros", [P, 2, S])
        n = TokenNorm(nc, ctx, "qn", stats)
        in_ps = [ps("xnt", [P, D]), ps("ctxt", [P, S])]
        turn_ps = [ps(f"turn{i}", [P, S]) for i in range(2)]
        qk_ps = [ps("qp", [P, D]), ps("kp", [P, D])]
        v_ps = [ps(f"vp{i}", [P, D]) for i in range(2)]
        in_, turn_ = Split(nc, ctx, "qi"), Split(nc, ctx, "qt")
        wq_in, wkv_in, pos_in, ctx_in = sem("wq_in"), sem("wkv_in"), sem("pos_in"), sem("ctx_in")
        wq_hi, wkv_hi, wq_split, wkv_split = sem("wq_hi"), sem("wkv_hi"), sem("wq_split"), sem("wkv_split")
        red_ready, trig_ready = sem("red_ready"), sem("trig_ready")
        qk_ready, rope_done, rot_done, v_ready, v_copied = (
            sem("qk_ready"), sem("rope_done"), sem("rot_done"), sem("v_ready"), sem("v_copied"))
        pads_set, out_zero = sem("pads_set"), sem("out_zero")
        out_q = [sem("out_q0"), odd.stored]
        out_v = [sem(f"out_v{i}") for i in range(2)]
        PAIR = 2 * TPB
        block = ctx.enter_context(nc.Block())

        @block.sync
        def _(sp):
            start_counts(sp, *out_q)
            sp.dma_start(pos[:], pos_dram).then_inc(pos_in, DMA)
            sp.dma_start(wq_raw[:], io["L1_xattn_Wq"].rearrange("(k p) n -> p k n", p=P)).then_inc(wq_in, DMA)
            sp.dma_start(wkv_raw[:], io["L1_xattn_Wkv"].rearrange("(k p) n -> p k n", p=P)).then_inc(wkv_in, DMA)

            def store(pair, e):
                sp.wait_ge(turn_.split, START + 2 * (pair * PAIR + (e + 1) * TPB) + 1)
                store_qk(sp, scr, qkT[e], 2 * pair + e, out_q[e])

            store(0, 0)
            with sp.Fori(1, B // 2) as pair:
                store(pair - 1, 1)
                store(pair, 0)
            sp.wait_ge(out_q[0], START + B // 2 * STORES * DMA)
            for i in range(2):
                sp.wait_ge(out_v[i], START + TILES // 2 * DMA)
            sp.wait_ge(out_zero, DMA)

        @block.tensor
        def _(pe):
            start_counts(pe, in_.filled, turn_.filled)
            with pe.Fori(0, B // 2) as pair:
                def inputs(t):
                    tile = pair * PAIR + t
                    pe.wait_ge(n.xn_ready, tile + 1)
                    pe.wait_ge(in_.split, START + 2 * tile)
                    transposes(nc, in_, in_ps[0], [xn[t % 2][:, k * P:(k + 1) * P] for k in range(DK)], ident)
                    pe.wait_ge(in_.split, START + 2 * tile + 1)
                    last = None
                    for k in range(CK):
                        last = nc.tensor.transpose(in_ps[1][:, k * P:(k + 1) * P],
                                                   ctx_raw[:, t, k * P:(k + 1) * P], ident[:])
                    last.then_inc(in_.filled, 1)

                def turn(t):
                    for i in range(2):
                        job = 2 * (pair * PAIR + t) + i
                        pe.wait_ge(rot_done, START + job + 1)
                        pe.wait_ge(turn_.split, START + job)
                        transposes(nc, turn_, turn_ps[i], [rot[i][:, k * P:(k + 1) * P] for k in range(HT)], ident)

                pe.wait_ge(ctx_in, DMA * (pair + 1))
                inputs(0)
                pe.wait_ge(wq_split, 1)
                for t in range(PAIR):
                    tile = pair * PAIR + t
                    if t + 1 < PAIR:
                        inputs(t + 1)
                    pe.wait_ge(in_.split, START + 2 * tile + 3)
                    pe.wait_ge(rope_done, START + 2 * tile)
                    product(nc, qk_ps[0][:], [([xnT[t % 2][:, h, k, :] for h in (HI, LO)],
                                               [wq[:, h, k, :] for h in (HI, LO)]) for k in range(DK)]).then_inc(qk_ready, 1)
                    if t == 0:
                        pe.wait_ge(wkv_split, 1)
                    product(nc, qk_ps[1][:], [([ctxT[t % 2][:, h, k, :] for h in (HI, LO)],
                                               [wkv[:, h, k, 0:D] for h in (HI, LO)]) for k in range(CK)]).then_inc(qk_ready, 1)
                    pe.wait_ge(v_copied, START + tile)
                    product(nc, v_ps[t % 2][:], [([ctxT[t % 2][:, h, k, :] for h in (HI, LO)],
                                                  [wkv[:, h, k, D:2 * D] for h in (HI, LO)]) for k in range(CK)]).then_inc(v_ready, 1)
                    if t:
                        turn(t - 1)
                turn(PAIR - 1)

        @block.scalar
        def _(act):
            start_counts(act, v_copied, *out_v)
            token_std(nc, act, n)
            act.wait_ge(red_ready, 1)
            nc.scalar.activation(sine[:], red[:], ACT.Sin).then_inc(trig_ready, 1)
            nc.scalar.activation(cosine[:], mag[:], ACT.Sin).then_inc(trig_ready, 1)
            act.wait_ge(wq_in, DMA)
            nc.scalar.activation(wq[:, HI], wq_raw[:], ACT.Copy).then_inc(wq_hi, 1)
            act.wait_ge(wkv_in, DMA)
            nc.scalar.activation(wkv[:, HI], wkv_raw[:], ACT.Copy).then_inc(wkv_hi, 1)
            act.wait_ge(pads_set, 5)
            with act.Fori(0, B // 2) as pair:
                act.wait_ge(in_.filled, START + 2 * PAIR * pair)
                act.dma_start(ctx_raw[:], ctx_dram[:, ds(pair * PAIR, PAIR), :]).then_inc(ctx_in, DMA)
                def inputs(t):
                    for i, to in enumerate((xnT, ctxT)):
                        blocks = (DK, CK)[i]
                        split_hi(nc, act, in_, 2 * (pair * PAIR + t) + i, to[t % 2][:, HI],
                                 in_ps[i][:, 0:blocks * P].rearrange("p (k c) -> p k c", k=blocks))

                def turn(t):
                    e, cols = t // TPB, slice(t % TPB * P, (t % TPB + 1) * P)
                    if t % TPB == 0:
                        act.wait_ge(out_q[e], START + pair * (STORES * DMA))
                    for i in range(2):
                        split_hi(nc, act, turn_, 2 * (pair * PAIR + t) + i, qkT[e][i][:, HI, :, cols],
                                 turn_ps[i][:].rearrange("p (k c) -> p k c", k=HT))

                inputs(0)
                for t in range(PAIR):
                    tile = pair * PAIR + t
                    if t + 1 < PAIR:
                        inputs(t + 1)
                    act.wait_ge(v_ready, tile + 1)
                    act.wait_ge(out_v[t % 2], START + (pair * (PAIR // 2) + t // 2) * DMA)
                    nc.scalar.activation(vpad[t % 2][:, :, 0:HD], v_ps[t % 2][:].rearrange("p (h c) -> p h c", h=HEADS),
                                         ACT.Copy).then_inc(v_copied, 1)
                    if t:
                        turn(t - 1)
                    act.wait_ge(v_copied, START + tile + 1)
                    groups = HEADS // GROUP
                    act.dma_start(scr["v"][ds((2 * pair + t // TPB) * groups, groups), t % TPB * P:(t % TPB + 1) * P, :]
                                  .rearrange("g p c -> p g c"),
                                  vpad[t % 2][:].rearrange("p (g h) c -> p g (h c)", h=GROUP)).then_inc(out_v[t % 2], DMA)
                turn(PAIR - 1)

        @block.gpsimd
        def _(pool):
            start_counts(pool, rot_done)
            for i in range(2):
                nc.gpsimd.memset(vpad[i][:], 0.0).then_inc(pads_set, 1)
            nc.gpsimd.memset(zeros[:], 0.0).then_inc(pads_set, 1)
            pool.wait_ge(pads_set, 3)
            for i in range(2):
                nc.gpsimd.memset(vpad[i][:, :, HD:HD + 1], 1.0).then_inc(pads_set, 1)
            pool.dma_start(scr["q"][:, 3 * HD:QROWS, :], zeros[:]).then_inc(out_zero, DMA)
            pool.wait_ge(wkv_hi, 1)
            nc.gpsimd.tensor_tensor(wkv[:, LO], wkv_raw[:], fp32(wkv[:, HI]), ALU.subtract).then_inc(wkv_split, 1)
            with pool.Fori(0, B // 2) as pair:
                for t in range(PAIR):
                    tile = pair * PAIR + t
                    for i in range(2):
                        pool.wait_ge(rope_done, START + 2 * tile + i + 1)
                        pool.wait_ge(turn_.filled, START + (2 * (tile - 1) + i + 1 if t else 2 * tile))
                        nc.gpsimd.tensor_tensor(rot[i][:], by_cos[i][:].rearrange("p h c -> p (h c)"),
                                                by_sin[i][:].rearrange("p h c -> p (h c)"), ALU.add).then_inc(rot_done, 1)

        @block.vector
        def _(dve):
            start_counts(dve, in_.split, turn_.split, rope_done)
            dve.sem_inc(in_.split, 1)
            dve.sem_inc(turn_.split, 1)
            token_var(nc, n)
            token_rstd(nc, dve, n)
            dve.wait_ge(pos_in, DMA)
            ang4 = ang[:].rearrange("p t (a j) -> p t a j", a=AX)
            for j in range(HALF):
                nc.vector.tensor_scalar(ang4[:, :, :, j], pos[:], FREQS[j], None, ALU.mult)
            nc.vector.drain()
            nc.vector.tensor_scalar(turns[:], ang[:], float(1.0 / TWO_PI), ROUND, ALU.mult, ALU.add)
            nc.vector.drain()
            nc.vector.tensor_scalar(turns[:], turns[:], -ROUND, None, ALU.add)
            nc.vector.drain()
            source = ang
            for part in (c1, c2, c3):
                nc.vector.scalar_tensor_tensor(out=red[:], in0=turns[:], scalar=-part, in1=source[:], op0=ALU.mult, op1=ALU.add)
                nc.vector.drain()
                source = red
            nc.vector.tensor_scalar(red[:], red[:], PI_F, -PI_F, ALU.min, ALU.max)
            nc.vector.drain()
            nc.vector.tensor_scalar(mag[:], red[:], -1.0, None, ALU.mult)
            nc.vector.drain()
            nc.vector.tensor_tensor(mag[:], mag[:], red[:], ALU.max)
            nc.vector.drain()
            nc.vector.tensor_scalar(mag[:], mag[:], -1.0, float(np.pi / 2), ALU.mult, ALU.add).then_inc(red_ready, 1)
            dve.wait_ge(trig_ready, 2)
            nc.vector.tensor_scalar(nsine[:], sine[:], -1.0, None, ALU.mult)
            for r in range(2):
                nc.vector.tensor_copy(cos2[:].rearrange("p t (f r) -> p t f r", r=2)[:, :, :, r], cosine[:])
            dve.wait_ge(wq_hi, 1)
            nc.vector.tensor_tensor(wq[:, LO], wq_raw[:], fp32(wq[:, HI]), ALU.subtract).then_inc(wq_split, 1)
            with dve.Fori(0, B // 2) as pair:
                def inputs(t):
                    for i, to in enumerate((xnT, ctxT)):
                        blocks = (DK, CK)[i]
                        split_lo(nc, dve, in_, 2 * (pair * PAIR + t) + i, to[t % 2][:, LO],
                                 in_ps[i][:, 0:blocks * P].rearrange("p (k c) -> p k c", k=blocks), to[t % 2][:, HI])

                def turn(t):
                    e, cols = t // TPB, slice(t % TPB * P, (t % TPB + 1) * P)
                    for i in range(2):
                        split_lo(nc, dve, turn_, 2 * (pair * PAIR + t) + i, qkT[e][i][:, LO, :, cols],
                                 turn_ps[i][:].rearrange("p (k c) -> p k c", k=HT), qkT[e][i][:, HI, :, cols])

                for t in range(2):
                    normalise_tile(nc, n, x, pair * PAIR + t, xn[t][:])
                inputs(0)
                for t in range(PAIR):
                    tile = pair * PAIR + t
                    if t + 1 < PAIR:
                        inputs(t + 1)
                    for i in range(2):
                        dve.wait_ge(qk_ready, 2 * tile + i + 1)
                        dve.wait_ge(rot_done, START + (2 * (tile - 1) + i + 1 if t else 2 * tile))
                        src = qk_ps[i][:].rearrange("p (h c) -> p h c", h=HEADS)
                        nc.vector.tensor_tensor(by_cos[i][:], src, cos2[:, ds(tile, 1), :].to_broadcast([P, HEADS, HD]), ALU.mult)
                        pairs = qk_ps[i][:].rearrange("p (h f r) -> p h f r", h=HEADS, r=2)
                        swapped = by_sin[i][:].rearrange("p h (f r) -> p h f r", r=2)
                        for r, table in ((0, nsine), (1, sine)):
                            last = nc.vector.tensor_tensor(swapped[:, :, :, r], pairs[:, :, :, 1 - r],
                                                           table[:, ds(tile, 1), :].to_broadcast([P, HEADS, HD // 2]), ALU.mult)
                        last.then_inc(rope_done, 1)
                    if t + 2 < PAIR:
                        dve.wait_ge(in_.filled, START + 2 * tile + 1)
                        normalise_tile(nc, n, x, tile + 2, xn[t % 2][:])
                    if t:
                        turn(t - 1)
                turn(PAIR - 1)


RING = 4


def phase_rope_attention1(nc, io, x, ident, odd, attn, wout):
    from contextlib import ExitStack
    scr = io["scratch"]
    KT = S // P
    SCALE = 1.0 / float(np.sqrt(HD))
    with ExitStack() as ctx:
        def sb(name, shape, dt=FP32):
            return ctx.enter_context(nc.sbuf_tensor(f"r_{name}", shape, dt))

        def ps(name, shape):
            return ctx.enter_context(nc.psum_tensor(f"r_{name}", shape, FP32))

        def sem(name):
            return ctx.enter_context(nc.semaphore(f"r_{name}"))

        kM = [sb(f"kM{s}", [P, GROUP, S], FP32R) for s in range(RING)]
        qS = [sb(f"qS{s}", [P, GROUP // 2, S], FP32R) for s in range(RING)]
        v = [sb(f"v{s}", [P, KT, GROUP * PAD]) for s in range(RING)]
        probs = [sb(f"probs{k}", [P, GROUP, S]) for k in range(KT)]
        top = [sb(f"top{i}", [P, KT, GROUP]) for i in range(2)]
        shift = [sb(f"shift{i}", [P, KT, GROUP, 2], FP32R) for i in range(2)]
        shiftT = [sb(f"shiftT{i}", [2 * GROUP, S], FP32R) for i in range(2)]
        outT = sb("outT", [P, S])
        rinv = sb("rinv", [P, KT * GROUP])
        bout = sb("bout", [P, D])
        st_ps = [ps(f"st{i}", [P, 2, S]) for i in range(2)]
        out_ps = ps("out", [P, S])
        ring_ps = [ps(f"ring{i}", [P, S]) for i in range(3)]
        PLACES = KT * GROUP + 2
        SHIFT_PLACE, OUT_PLACE = GROUP, 2 * GROUP + 1

        def place(q, h):
            return q * GROUP + h + min(q, 2)

        def ring(at):
            return ring_ps[at % 3]

        slot_set_pool = sem("slot_set_pool")
        slot_set = [sem(f"slot_set{s}") for s in range(RING)]
        kqv_in = [sem(f"kqv_in{s}") for s in range(RING)]
        shift_in = [sem(f"shift_in{s}") for s in range(RING)]
        bout_in = sem("bout_in")
        max_ready, max_read, shift_made = sem("max_ready"), sem("max_read"), sem("shift_made")
        shift_turned, shift_copied = sem("shift_turned"), sem("shift_copied")
        scores_ready, exp_done = sem("scores_ready"), sem("exp_done")
        out_ready, out_copied, out_turned, out_done = sem("out_ready"), sem("out_copied"), sem("out_turned"), sem("out_done")
        LOADS, SHIFTS = 5, 4
        block = ctx.enter_context(nc.Block())

        def steps(engine, step):
            rings = GROUPS // RING
            for s in range(RING):
                step(s, 0, s, s == 0, RING)
            with engine.Fori(1, rings - 1) as i:
                for s in range(RING):
                    step(i * RING + s, i, s, False, RING)
            for s in range(RING):
                step((rings - 1) * RING + s, rings - 1, s, False, RING - 1 - s)

        CONST_ROWS = 6

        def set_slot(memset, s, halves=(0, 1), each=lambda done: None):
            done = 0
            for half in halves:
                tail = slice(64 * half + 32, 64 * half + 64)
                other = slice(64 * (1 - half), 64 * (1 - half) + 64)
                for rows, value in ((qS[s][tail, :, :], 0.0), (kM[s][tail, half:GROUP:2, :], 1.0),
                                    (kM[s][other, half:GROUP:2, :], 0.0)):
                    memset(fp32(rows), value).then_inc(slot_set_pool if halves == (1,) else slot_set[s], 1)
                    done += 1
                    each(done)

        @block.gpsimd
        def _(pool):
            set_slot(nc.gpsimd.memset, 0, (1,), lambda done: pool.wait_ge(slot_set_pool, done))
            for s in range(1, RING):
                set_slot(nc.gpsimd.memset, s, (0, 1), lambda done: pool.wait_ge(slot_set[s], done))
            pool.wait_ge(bout_in, DMA)
            with pool.Fori(0, TILES) as tile:
                nc.gpsimd.tensor_tensor(x[:, ds(tile, 1), :], x[:, ds(tile, 1), :],
                                        bout[:].rearrange("p (a c) -> p a c", a=1), ALU.add)

        @block.sync
        def _(sp):
            def load(g, s):
                for half in range(2):
                    rows = 64 * half
                    heads = slice(half, GROUP, 2)
                    sp.dma_start(fp32(kM[s][rows:rows + KROWS, heads, :]),
                                 scr["k"][ds(g * GROUP, GROUP), :, :][heads].rearrange("h r n -> r h n")).then_inc(kqv_in[s], DMA)
                    sp.dma_start(fp32(qS[s][rows:rows + QROWS, :, :]),
                                 scr["q"][ds(g * GROUP, GROUP), :, :][heads].rearrange("h r n -> r h n")).then_inc(kqv_in[s], DMA)
                sp.dma_start(v[s][:], scr["v"][ds(g, 1), :, :].rearrange("g (k p) c -> p (g k) c", p=P)).then_inc(kqv_in[s], DMA)

            def shifts(g, s):
                sp.wait_ge(shift_copied, g + 1)
                for h in range(GROUP):
                    row = 64 * (h % 2) + 3 * HD
                    sp.dma_start(fp32(qS[s][row:row + 2, h // 2, :]), fp32(shiftT[s % 2][2 * h:2 * h + 2, :])).then_inc(shift_in[s], DMA)

            sp.wait_ge(slot_set[0], CONST_ROWS // 2)
            sp.wait_ge(slot_set_pool, CONST_ROWS // 2)
            load(0, 0)
            sp.wait_ge(slot_set[1], CONST_ROWS)
            load(1, 1)
            sp.dma_start(wout.raw[:], io["L1_xattn_Wout"].rearrange("(k p) n -> p k n", p=P)).then_inc(wout.loaded, DMA)
            sp.dma_start(bout[:], io["L1_xattn_bout"].rearrange("(a n) -> a n", a=1).to_broadcast([P, D])).then_inc(bout_in, DMA)
            shifts(0, 0)
            sp.wait_ge(slot_set[2], CONST_ROWS)
            load(2, 2)
            sp.wait_ge(slot_set[3], CONST_ROWS)

            def step(g, i, s, first, left):
                if isinstance(g, int) and g < RING:
                    store_qk(sp, scr, odd.qkT, B - 1, odd.stored, range(g * STORES // RING, (g + 1) * STORES // RING))
                    if g == RING - 1:
                        sp.wait_ge(odd.stored, START + B // 2 * STORES * DMA)
                if left >= RING - 1:
                    sp.wait_ge(out_ready, g)
                    load(g + RING - 1, (s + RING - 1) % RING)
                if left >= 1:
                    shifts(g + 1, (s + 1) % RING)

            steps(sp, step)

        @block.tensor
        def _(pe):
            def bank_free(g, at):
                exists = lambda n, low, high: not isinstance(n, int) or low <= n <= high
                while True:
                    at -= 3
                    if at < 0:
                        at, g = at + PLACES, g - 1
                    if isinstance(g, int) and g < 0:
                        return
                    if at == SHIFT_PLACE:
                        if exists(g, 1, GROUPS):
                            pe.wait_ge(shift_copied, g)
                            return
                    elif at == OUT_PLACE:
                        if exists(g, 3, GROUPS + 2):
                            pe.wait_ge(out_done, g - 2)
                            return
                    elif exists(g, 0, GROUPS - 1):
                        before = at - (at > SHIFT_PLACE) - (at > OUT_PLACE)
                        pe.wait_ge(max_read, g * (KT * GROUP) + before + 1)
                        return

            def scores(g, i, s, k, pair):
                if k == 0 and pair == 0:
                    pe.wait_ge(shift_in[s], (i + 1) * SHIFTS * DMA)
                pe.wait_ge(exp_done, (g * KT + k) * 2 + pair)
                last = None
                for j in range(2):
                    last = nc.tensor.matmul(st_ps[pair][:, j, :], kM[s][:, 2 * pair + j, k * P:(k + 1) * P],
                                            qS[s][:, pair, :], start=True, stop=True)
                last.then_inc(scores_ready, 1)

            def maxima(g, i, s, q, heads):
                for h in heads:
                    if q == 0 and h == 0:
                        pe.wait_ge(kqv_in[s], (i + 1) * LOADS * DMA)
                    bank_free(g, place(q, h))
                    nc.tensor.matmul(ring(place(q, h))[:], qS[s][:, h // 2, q * P:(q + 1) * P], kM[s][:, h, :],
                                     start=True, stop=True).then_inc(max_ready, 1)

            def turn_shifts(g, s):
                pe.wait_ge(shift_made, g + 1)
                bank_free(g + 1, SHIFT_PLACE)
                last = None
                for q in range(KT):
                    last = nc.tensor.transpose(ring(SHIFT_PLACE)[0:2 * GROUP, q * P:(q + 1) * P],
                                               fp32(shift[s % 2][:, q].rearrange("p h a -> p (h a)")), ident[:])
                last.then_inc(shift_turned, 1)

            def values(g, s, k):
                pe.wait_ge(exp_done, (g * KT + k) * 2 + 3)
                if k == 0:
                    pe.wait_ge(out_copied, g)
                last = None
                for h in range(GROUP):
                    last = nc.tensor.matmul(out_ps[h * PAD:(h + 1) * PAD, :], v[s][:, k, h * PAD:(h + 1) * PAD],
                                            probs[k][:, h, :], start=(k == 0), stop=(k == KT - 1))
                if k == KT - 1:
                    last.then_inc(out_ready, 1)

            def turn_out(g):
                pe.wait_ge(out_copied, g + 1)
                bank_free(g + 3, OUT_PLACE)
                last = None
                for q in range(KT):
                    last = nc.tensor.transpose(ring(OUT_PLACE)[:, q * P:(q + 1) * P], outT[:, q * P:(q + 1) * P], ident[:])
                last.then_inc(out_turned, 1)

            for g in range(2):
                for q in range(KT):
                    maxima(g, 0, g, q, range(GROUP))
                    if (g, q) == (1, 0):
                        turn_shifts(0, 0)

            def step(g, i, s, first, left):
                for k in range(KT):
                    def maxima_of(*heads):
                        if left >= 2:
                            maxima(g + 2, i + (s + 2) // RING, (s + 2) % RING, k, heads)

                    maxima_of(0)
                    scores(g, i, s, k, 0)
                    maxima_of(1)
                    scores(g, i, s, k, 1)
                    maxima_of(2, 3)
                    if k == 0:
                        if not first:
                            values(g - 1, (s - 1) % RING, KT - 1)
                        if left >= 1:
                            turn_shifts(g + 1, (s + 1) % RING)
                    else:
                        values(g, s, k - 1)
                        if k == 1 and not first:
                            turn_out(g - 1)

            steps(pe, step)
            values(GROUPS - 1, RING - 1, KT - 1)
            turn_out(GROUPS - 1)

        @block.scalar
        def _(act):
            def copy_shifts(g, s):
                act.wait_ge(shift_turned, g + 1)
                nc.scalar.activation(shiftT[s % 2][:], ring(SHIFT_PLACE)[0:2 * GROUP, :], ACT.Copy).then_inc(shift_copied, 1)

            def copy_out(g):
                act.wait_ge(out_ready, g + 1)
                nc.scalar.activation(outT[:], out_ps[:], ACT.Copy).then_inc(out_copied, 1)

            copy_shifts(0, 0)

            def step(g, i, s, first, left):
                for k in range(KT):
                    for pair in range(2):
                        act.wait_ge(scores_ready, (g * KT + k) * 2 + pair + 1)
                        nc.scalar.activation(probs[k][:, 2 * pair:2 * pair + 2, :], st_ps[pair][:], ACT.Exp,
                                             scale=SCALE).then_inc(exp_done, 1)
                    if k == 0:
                        if not first:
                            copy_out(g - 1)
                        if left >= 1:
                            copy_shifts(g + 1, (s + 1) % RING)

            steps(act, step)
            copy_out(GROUPS - 1)

        @block.vector
        def _(dve):
            def read_maxima(g, s, q):
                for h in range(GROUP):
                    dve.wait_ge(max_ready, (g * KT + q) * GROUP + h + 1)
                    nc.vector.reduce_max(top[s % 2][:, q, h:h + 1], ring(place(q, h))[:], AXIS_X).then_inc(max_read, 1)

            def make_shifts(s):
                nc.vector.drain()
                nc.vector.tensor_scalar(shift[s % 2][:, :, :, 0], top[s % 2][:], -1.0, None, ALU.mult)
                nc.vector.drain()
                nc.vector.scalar_tensor_tensor(out=shift[s % 2][:, :, :, 1], in0=top[s % 2][:], scalar=-1.0,
                                               in1=fp32(shift[s % 2][:, :, :, 0]), op0=ALU.mult,
                                               op1=ALU.subtract).then_inc(shift_made, 1)

            def normalise(g):
                dve.wait_ge(out_turned, g + 1)
                turned = ring(OUT_PLACE)[:].rearrange("p (a c) -> p a c", c=PAD)
                nc.vector.reciprocal(rinv[:], turned[:, :, HD])
                nc.vector.drain()
                nc.vector.tensor_tensor(attn[:, ds(g, 1), :, :].rearrange("p g a c -> p (g a) c"), turned[:, :, 0:HD],
                                        rinv[:].unsqueeze(2).to_broadcast([P, KT * GROUP, HD]), ALU.mult).then_inc(out_done, 1)

            set_slot(nc.vector.memset, 0, (0,))
            dve.sem_inc(exp_done, 1)
            for g in range(2):
                for q in range(KT):
                    read_maxima(g, g, q)
                make_shifts(g)

            def step(g, i, s, first, left):
                for q in range(KT):
                    if left >= 2:
                        read_maxima(g + 2, s, q)
                    if q == 1 and not first:
                        normalise(g - 1)
                if left >= 2:
                    make_shifts((s + 2) % RING)

            steps(dve, step)
            normalise(GROUPS - 1)


class OutWeights:

    def __init__(self, nc, ctx):
        self.raw = ctx.enter_context(nc.sbuf_tensor("wout_raw", [P, DK, D], FP32))
        self.loaded = ctx.enter_context(nc.semaphore("wout_in"))


def phase_out1(nc, io, x, ident, stats, attn, wout):
    from contextlib import ExitStack
    with ExitStack() as ctx:
        def sb(name, shape, dt=FP32):
            return ctx.enter_context(nc.sbuf_tensor(f"o_{name}", shape, dt))

        def ps(name, shape):
            return ctx.enter_context(nc.psum_tensor(f"o_{name}", shape, FP32))

        def sem(name):
            return ctx.enter_context(nc.semaphore(f"o_{name}"))

        w = sb("w", [P, 2, DK, D], FP32R)
        rows = [sb(f"rows{i}", [P, D]) for i in range(2)]
        aT = [sb(f"aT{i}", [P, 2, DK, P], FP32R) for i in range(2)]
        tp = [ps(f"tp{i}", [P, D]) for i in range(2)]
        y_ps = [ps(f"y{i}", [P, D]) for i in range(2)]
        t_ = Split(nc, ctx, "ot")
        w_hi, w_split, rows_ready, y_ready, y_added = (
            sem("w_hi"), sem("w_split"), sem("rows_ready"), sem("y_ready"), sem("y_added"))
        block = ctx.enter_context(nc.Block())

        @block.tensor
        def _(pe):
            start_counts(pe, t_.filled)
            def out_product(tile, t):
                pe.wait_ge(t_.split, START + tile + 2)
                pe.wait_ge(y_added, START + tile)
                product(nc, y_ps[t % 2][:], [([aT[t % 2][:, h, k, :] for h in (HI, LO)],
                                              [w[:, h, k, :] for h in (HI, LO)]) for k in range(DK)]).then_inc(y_ready, 1)

            with pe.Fori(0, B) as b:
                for t in range(TPB):
                    tile = b * TPB + t
                    pe.wait_ge(rows_ready, tile + 1)
                    pe.wait_ge(t_.split, START + tile)
                    transposes(nc, t_, tp[t % 2], [rows[t % 2][:, k * P:(k + 1) * P] for k in range(DK)], ident)
                    if t == 0:
                        pe.wait_ge(w_split, DK)
                    if t:
                        out_product(tile - 1, t - 1)
                out_product(b * TPB + TPB - 1, TPB - 1)

        @block.scalar
        def _(act):
            act.wait_ge(wout.loaded, DMA)
            for k in range(DK):
                nc.scalar.activation(w[:, HI, k, :], wout.raw[:, k, :], ACT.Copy).then_inc(w_hi, 1)
            with act.Fori(0, B) as b:
                for t in range(TPB):
                    tile = b * TPB + t
                    act.wait_ge(t_.filled, START + (tile - 1 if t else b * TPB))
                    nc.scalar.activation(rows[t % 2][:].rearrange("p (g c) -> p g c", g=HEADS // GROUP),
                                         attn[:, ds(b * (HEADS // GROUP), HEADS // GROUP), t * GROUP:(t + 1) * GROUP, :]
                                         .rearrange("p g a c -> p g (a c)"), ACT.Copy).then_inc(rows_ready, 1)
                    split_hi(nc, act, t_, tile, aT[t % 2][:, HI], tp[t % 2][:].rearrange("p (k c) -> p k c", k=DK))

        @block.vector
        def _(dve):
            start_counts(dve, t_.split, y_added)
            dve.sem_inc(t_.split, 1)
            dve.sem_inc(y_added, 1)
            for k in range(DK):
                dve.wait_ge(w_hi, k + 1)
                nc.vector.tensor_tensor(w[:, LO, k, :], wout.raw[:, k, :], fp32(w[:, HI, k, :]), ALU.subtract).then_inc(w_split, 1)

            def add(tile, t):
                dve.wait_ge(y_ready, tile + 1)
                nc.vector.tensor_tensor(x[:, ds(tile, 1), :], y_ps[t % 2][:].rearrange("p (a c) -> p a c", a=1),
                                        x[:, ds(tile, 1), :], ALU.add).then_inc(y_added, 1)

            def out_stats(tile):
                dve.wait_ge(y_added, START + tile + 2)
                tile_stats(nc, stats, x, tile)

            with dve.Fori(0, B) as b:
                for t in range(TPB):
                    tile = b * TPB + t
                    split_lo(nc, dve, t_, tile, aT[t % 2][:, LO], tp[t % 2][:].rearrange("p (k c) -> p k c", k=DK), aT[t % 2][:, HI])
                    if t >= 2:
                        out_stats(tile - 2)
                    if t:
                        add(tile - 1, t - 1)
                out_stats(b * TPB + TPB - 2)
                add(b * TPB + TPB - 1, TPB - 1)
                out_stats(b * TPB + TPB - 1)


def phase_rope1(nc, io, x, ident, stats):
    from contextlib import ExitStack
    with ExitStack() as ctx:
        odd = OddBatch(nc, ctx)
        phase_qkv1(nc, io, x, ident, stats, odd)
        attn = ctx.enter_context(nc.sbuf_tensor("attn", [P, GROUPS, TPB * GROUP, HD], FP32))
        wout = OutWeights(nc, ctx)
        phase_rope_attention1(nc, io, x, ident, odd, attn, wout)
        phase_out1(nc, io, x, ident, stats, attn, wout)


def phase_ffn1(nc, io, x, ident, stats):
    from contextlib import ExitStack
    ER = E1 * R1
    NF = DFF // P
    HALVES = 2
    CH = B // HALVES
    HT, HTOK = CH * TPB, CH * S
    STEPS = NF * CH
    PREP = 4
    USES = TPB + 2
    gate_dram, up_dram, down_dram = io["L1_ffn_Wg"], io["L1_ffn_Wu"], io["L1_ffn_Wd"]
    out_dram = io["out"].rearrange("b (t p) d -> p (b t) d", p=P)
    with ExitStack() as ctx:
        def sb(name, shape, dt=FP32):
            return ctx.enter_context(nc.sbuf_tensor(f"f_{name}", shape, dt))

        def ps(name, shape):
            return ctx.enter_context(nc.psum_tensor(f"f_{name}", shape, FP32))

        def sem(name):
            return ctx.enter_context(nc.semaphore(f"f_{name}"))

        xnT = sb("xnT", [P, 2, DK, HTOK], FP32R)
        agT, auT = sb("agT", [P, 2, DK, ER], FP32R), sb("auT", [P, 2, DK, ER], FP32R)
        wrT = sb("wrT", [P, 2, DK, E1], FP32R)
        bdT = sb("bdT", [ER, 2, D], FP32R)
        wr_raw = sb("wr_raw", [E1, D])
        gate_raw, up_raw, down_raw = sb("gate_raw", [P, D]), sb("up_raw", [P, D]), sb("down_raw", [P, DK, P])
        lora_raw = sb("lora_raw", [P, 3, P])
        gateT = [sb(f"gateT{s}", [P, 2, DK, P], FP32R) for s in range(2)]
        upT = [sb(f"upT{s}", [P, 2, DK, P], FP32R) for s in range(2)]
        downT = [sb(f"downT{s}", [P, 2, D], FP32R) for s in range(2)]
        loraT = [sb(f"loraT{s}", [P, 2, 3, P], FP32R) for s in range(2)]
        rl = sb("rl", [P, S])
        logits = sb("logits", [P, HT, E1])
        shifted = sb("shifted", [P, HT, E1])
        rev = sb("rev", [P, HT, E1])
        hots = sb("hots", [P, HT, 4, E1])
        am = sb("am", [P, 2, 2, 2, HTOK], FP32R)
        down_acc = sb("down_acc", [P, 2, HTOK])
        hidS = [sb(f"hidS{c}", [P, 3, 2, S], FP32R) for c in range(2)]
        work = sb("work", [P, 10, S])

        def hid(c, var):
            return work[:, 4 + 3 * c + var, :]

        mk = [work[:, 4, :], work[:, 9, :]]
        maskT = work[:, 5:9, :].rearrange("p (k c) n -> p k (c n)", k=2)
        xn = work[:, 0:4, :]
        n = TokenNorm(nc, ctx, "fn", stats)
        t = TopTwo(nc, ctx, "ft", HT, E1)
        g_ps = [ps(f"g{c}", [P, S]) for c in range(CH)]
        u_ps = [ps(f"u{c}", [P, S]) for c in range(CH)]
        prep_ps = ps("prep", [P, S])
        y_ps = [ps(f"y{i}", [P, S]) for i in range(3)]
        c_, xt_, prep_ = Split(nc, ctx, "fc"), Split(nc, ctx, "fx"), Split(nc, ctx, "fp")
        am_ = Split(nc, ctx, "fa")
        const_in, raw_in = sem("const_in"), sem("raw_in")
        router_ready, router_copied, logits_ready, logits_done = (
            sem("router_ready"), sem("router_copied"), sem("logits_ready"), sem("logits_done"))
        gap_ready, gap_exp, rl_clear = sem("gap_ready"), sem("gap_exp"), sem("rl_clear")
        mk_made, mk_turned, mask_copied, a_ready, a_used, acc_clear = (
            sem("mk_made"), sem("mk_turned"), sem("mask_copied"), sem("a_ready"), sem("a_used"), sem("acc_clear"))
        gate_ready, up_ready = sem("gate_ready"), sem("up_ready")
        silu_done, hid_done, hid_hi, hid_split = sem("silu_done"), sem("hid_done"), sem("hid_hi"), sem("hid_split")
        y_ready, y_added = sem("y_ready"), sem("y_added")
        z_ready, z_hi, z_split, z_out, z_added, stored = (
            sem("z_ready"), sem("z_hi"), sem("z_split"), sem("z_out"), sem("z_added"), sem("stored"))
        am_split2 = sem("am_split2")
        CONST_JOBS = 4
        a_ps = [[g_ps[c], u_ps[c]] for c in range(CH)]
        block = ctx.enter_context(nc.Block())

        def first_bank(job):
            return (prep_ps, y_ps[2])[job % 2]

        def const_views(job):
            bank = first_bank(job)
            if job < 2:
                raw, to = ((gate_raw, agT), (up_raw, auT))[job]
                return ([raw[:, k * P:(k + 1) * P] for k in range(DK)],
                        bank[:].rearrange("p (k c) -> p k c", k=DK), [to[:, h] for h in (HI, LO)])
            if job == 2:
                return ([wr_raw[:, k * P:(k + 1) * P] for k in range(DK)],
                        bank[:, 0:DK * E1].rearrange("p (k c) -> p k c", k=DK), [wrT[:, h] for h in (HI, LO)])
            return ([down_raw[:, k, :] for k in range(DK)], bank[:], [bdT[:, h] for h in (HI, LO)])

        def prep_views(s, part, bank=prep_ps):
            if part < 2:
                raw, to = ((gate_raw, gateT), (up_raw, upT))[part]
                return ([raw[:, k * P:(k + 1) * P] for k in range(DK)],
                        bank[:].rearrange("p (k c) -> p k c", k=DK), [to[s][:, h] for h in (HI, LO)])
            if part == 2:
                return ([down_raw[:, k, :] for k in range(DK)], bank[:], [downT[s][:, h] for h in (HI, LO)])
            return ([lora_raw[:, k, :] for k in range(3)], bank[:, 0:3 * P].rearrange("p (k c) -> p k c", k=3),
                    [loraT[s][:, h] for h in (HI, LO)])

        def tiles(engine, half, tile):
            tile(0, 0, True, False)
            tile(1, 1, False, False)
            with engine.Fori(1, (NF - 1) // 2) as i:
                for s in range(2):
                    tile(2 * i + s, s, False, False)
            tile(NF - 1, 0, False, True)

        def ring(c, use):
            return y_ps[(c * USES + use) % 3]

        @block.sync
        def _(sp):
            sp.dma_start(wr_raw[:], io["L1_ffn_Wr"]).then_inc(const_in, DMA)
            sp.dma_start(gate_raw[:], io["L1_ffn_Ag"].rearrange("e r d -> (e r) d")).then_inc(const_in, DMA)
            sp.dma_start(up_raw[:], io["L1_ffn_Au"].rearrange("e r d -> (e r) d")).then_inc(const_in, DMA)
            for k in range(DK):
                sp.dma_start(down_raw[:, k, :].rearrange("p (e r) -> p e r", e=E1),
                             io["L1_ffn_Bd"][:, k * P:(k + 1) * P, :].rearrange("e p r -> p e r")).then_inc(const_in, DMA)
            sp.wait_ge(c_.filled, START + CONST_JOBS)

            def load(h, f):
                sp.wait_ge(prep_.filled, START + (h * NF + f) * PREP)
                sp.dma_start(gate_raw[:], gate_dram[ds(f * P, P), :]).then_inc(raw_in, DMA)
                sp.dma_start(up_raw[:], up_dram[ds(f * P, P), :]).then_inc(raw_in, DMA)
                sp.dma_start(down_raw[:], down_dram[:, ds(f * P, P)].rearrange("(k p) f -> p k f", p=P)).then_inc(raw_in, DMA)
                for i, name in enumerate(("L1_ffn_Bg", "L1_ffn_Bu")):
                    sp.dma_start(lora_raw[:, i, :].rearrange("p (e r) -> p e r", e=E1),
                                 io[name][:, ds(f * P, P), :].rearrange("e f r -> f e r")).then_inc(raw_in, DMA)
                sp.dma_start(lora_raw[:, 2, :], io["L1_ffn_Ad"].rearrange("e r f -> (e r) f")[:, ds(f * P, P)]).then_inc(raw_in, DMA)

            with sp.Fori(0, HALVES) as h:
                with sp.Fori(0, NF) as f:
                    load(h, f)
                for c in range(CH):
                    sp.wait_ge(z_added, START + h * HT + (c + 1) * TPB)
                    sp.dma_start(out_dram[:, ds(h * HT + c * TPB, TPB), :], x[:, ds(h * HT + c * TPB, TPB), :]).then_inc(stored, DMA)
            sp.wait_ge(stored, HALVES * CH * DMA)

        LOADS = 6

        @block.tensor
        def _(pe):
            start_counts(pe, xt_.filled, c_.filled, prep_.filled)
            def prep(h, f, s, part):
                job = (h * NF + f) * PREP + part
                if part == 0:
                    pe.wait_ge(raw_in, (h * NF + f + 1) * LOADS * DMA)
                pe.wait_ge(prep_.split, START + job)
                transposes(nc, prep_, prep_ps, prep_views(s, part)[0], ident)

            pe.wait_ge(const_in, (3 + DK) * DMA)
            for job in range(CONST_JOBS):
                if job >= 2:
                    pe.wait_ge(c_.split, START + job - 1)
                transposes(nc, c_, first_bank(job), const_views(job)[0], ident)
            pe.wait_ge(c_.split, START + CONST_JOBS)
            with pe.Fori(0, HALVES) as h:
                def token_tile(c, k):
                    job = (h * CH + c) * TPB + k
                    pe.wait_ge(n.xn_ready, job + 1)
                    pe.wait_ge(xt_.split, START + job)
                    transposes(nc, xt_, (g_ps, u_ps)[k % 2][0], [xn[:, k, i * P:(i + 1) * P] for i in range(DK)], ident)

                def router(c, k):
                    if k == 0:
                        pe.wait_ge(xt_.split, START + (h * CH + c + 1) * TPB + 1)
                        pe.wait_ge(router_copied, START + h * CH + c)
                    last = add_product(nc, g_ps[1][0:E1, :], [wrT[:, i, k, :] for i in (HI, LO)],
                                       [xnT[:, i, k, c * S:(c + 1) * S] for i in (HI, LO)], start=(k == 0))
                    if k == DK - 1:
                        last.then_inc(router_ready, 1)

                def turn_logits(c):
                    pe.wait_ge(router_copied, START + h * CH + c + 1)
                    pe.wait_ge(logits_done, START + h * CH + c)
                    last = None
                    for k in range(TPB):
                        last = nc.tensor.transpose(u_ps[1][:, k * P:(k + 1) * P], rl[:, k * P:(k + 1) * P], ident[:])
                    last.then_inc(logits_ready, 1)

                for c in range(CH):
                    for k in range(TPB):
                        token_tile(c, k)
                        if c:
                            router(c - 1, k)
                    if c:
                        turn_logits(c - 1)
                for k in range(DK):
                    router(CH - 1, k)
                pe.wait_ge(raw_in, (h * NF + 1) * LOADS * DMA)
                for part in range(PREP):
                    pe.wait_ge(prep_.split, START + h * NF * PREP + max(part - 1, 0))
                    transposes(nc, prep_, first_bank(part), prep_views(0, part, first_bank(part))[0], ident)
                turn_logits(CH - 1)

                def turn_masks(base):
                    for i in range(HT):
                        pe.wait_ge(mk_made, base + i + 1)
                        pe.wait_ge(mask_copied, START + base + i)
                        for k in range(4):
                            last = nc.tensor.transpose(y_ps[i % 2][:, k * P:(k + 1) * P], mk[i % 2][:, k * P:(k + 1) * P], ident[:])
                        last.then_inc(mk_turned, 1)

                pe.wait_ge(logits_done, START + h * CH + CH)
                for c in range(CH):
                    for i, a in enumerate((agT, auT)):
                        if (c, i) == (CH - 1, 1):
                            turn_masks(h * 2 * HT)
                        product(nc, a_ps[c][i][:], [([a[:, j, k, :] for j in (HI, LO)],
                                                     [xnT[:, j, k, c * S:(c + 1) * S] for j in (HI, LO)])
                                                    for k in range(DK)]).then_inc(a_ready, 1)

                def ring_wait(step, use):
                    pe.wait_ge(y_added, START + step * USES + use)

                def down(step, s, c):
                    pe.wait_ge(hid_split, START + 3 * step + 3 + 1)
                    for i in range(TPB):
                        ring_wait(step, i)
                        product(nc, ring(c, i)[:], [([hidS[c][:, 0, j, i * P:(i + 1) * P] for j in (HI, LO)],
                                                     [downT[s][:, j, :] for j in (HI, LO)])]).then_inc(y_ready, 1)

                def down_lora(step, s, c):
                    for k in range(2):
                        pe.wait_ge(hid_split, START + 3 * step + 3 + 2 + k)
                        ring_wait(step, TPB + k)
                        product(nc, ring(c, TPB + k)[:], [([loraT[s][:, j, 2, :] for j in (HI, LO)],
                                                          [hidS[c][:, 1 + k, j, :] for j in (HI, LO)])]).then_inc(y_ready, 1)

                def lora(step, s, c, var):
                    pe.wait_ge(hid_done, START + 3 * step + var + 3)
                    if var == 1:
                        pe.wait_ge(am_.split, START + (h + 1) * CH * 2)
                        pe.wait_ge(am_split2, START + (h + 1) * CH * 2)
                    for i, (to, ready) in enumerate(((g_ps[c], gate_ready), (u_ps[c], up_ready))):
                        add_product(nc, to[:], [loraT[s][:, j, i, :] for j in (HI, LO)],
                                    [am[:, i, var - 1, j, c * S:(c + 1) * S] for j in (HI, LO)]).then_inc(ready, 1)

                def tile(f, s, first, last):
                    pe.wait_ge(prep_.split, START + (h * NF + f + 1) * PREP)
                    for c in range(CH):
                        step = h * STEPS + f * CH + c
                        before = (step - 1, s if c else 1 - s, 1 - c)
                        has_before = not (first and c == 0)
                        if first:
                            pe.wait_ge(a_used, (h * CH + c + 1) * 4)
                        pe.wait_ge(hid_done, START + 3 * step)
                        product(nc, g_ps[c][:], [([gateT[s][:, j, k, :] for j in (HI, LO)],
                                                  [xnT[:, j, k, c * S:(c + 1) * S] for j in (HI, LO)])
                                                 for k in range(DK)]).then_inc(gate_ready, 1)
                        if not last:
                            prep(h, f + 1, 1 - s, 2 * c)
                        product(nc, u_ps[c][:], [([upT[s][:, j, k, :] for j in (HI, LO)],
                                                  [xnT[:, j, k, c * S:(c + 1) * S] for j in (HI, LO)])
                                                 for k in range(DK)]).then_inc(up_ready, 1)
                        if has_before:
                            down(*before)
                        lora(step, s, c, 1)
                        if not last:
                            prep(h, f + 1, 1 - s, 2 * c + 1)
                        if has_before:
                            down_lora(*before)
                        lora(step, s, c, 2)

                tiles(pe, h, tile)
                end = (h * STEPS + STEPS - 1, 0, CH - 1)
                down(*end)
                down_lora(*end)
                pe.wait_ge(y_added, START + (h + 1) * STEPS * USES + 2)
                turn_masks(h * 2 * HT + HT)
                pe.wait_ge(z_split, h + 1)
                for i in range(HT):
                    pe.wait_ge(z_added, START + (h * HT + i - 1 if i else h * HT))
                    product(nc, y_ps[i % 2][:], [([am[:, 0, 0, j, i * P:(i + 1) * P] for j in (HI, LO)],
                                                 [bdT[:, j, :] for j in (HI, LO)])]).then_inc(z_out, 1)

        @block.scalar
        def _(act):
            start_counts(act, router_copied, mask_copied)
            def prep(h, f, s, part, bank=prep_ps):
                _, psum, (hi, lo) = prep_views(s, part, bank)
                split_hi(nc, act, prep_, (h * NF + f) * PREP + part, hi, psum)

            token_std(nc, act, n)
            for job in range(CONST_JOBS):
                _, psum, (hi, lo) = const_views(job)
                split_hi(nc, act, c_, job, hi, psum)
            act.wait_ge(rl_clear, 1)
            with act.Fori(0, HALVES) as h:
                def copy_router(c):
                    act.wait_ge(router_ready, h * CH + c + 1)
                    nc.scalar.activation(rl[0:E1, :], g_ps[1][0:E1, :], ACT.Copy).then_inc(router_copied, 1)

                for c in range(CH):
                    for k in range(TPB):
                        at = (c * TPB + k) * P
                        split_hi(nc, act, xt_, (h * CH + c) * TPB + k, xnT[:, HI, :, at:at + P],
                                 (g_ps, u_ps)[k % 2][0][:].rearrange("p (k c) -> p k c", k=DK))
                    if c:
                        copy_router(c - 1)
                copy_router(CH - 1)
                for part in range(PREP):
                    prep(h, 0, 0, part, first_bank(part))
                act.wait_ge(gap_ready, h + 1)
                nc.scalar.activation(shifted[:], shifted[:], ACT.Exp).then_inc(gap_exp, 1)
                nc.scalar.activation(t.e[:], t.gap[:], ACT.Exp).then_inc(gap_exp, 1)

                def copy_masks(base, part):
                    for i in range(HT):
                        act.wait_ge(mk_turned, base + i + 1)
                        nc.scalar.activation(maskT[:, :, i * P:(i + 1) * P],
                                             y_ps[i % 2][:, part * 2 * P:(part + 1) * 2 * P].rearrange("p (k c) -> p k c", k=2),
                                             ACT.Copy).then_inc(mask_copied, 1)

                copy_masks(h * 2 * HT, 0)
                for c in range(CH):
                    for i in range(2):
                        for k in range(2):
                            job = 4 * (h * CH + c) + 2 * i + k
                            act.wait_ge(a_used, job + 1)
                            nc.scalar.activation(am[:, i, k, HI, c * S:(c + 1) * S], work[:, 2 * i + k, :], ACT.Copy).then_inc(am_.hi_done, 1)

                def tile(f, s, first, last):
                    for c in range(CH):
                        step = h * STEPS + f * CH + c

                        def silu(var):
                            act.wait_ge(gate_ready, 3 * step + var + 1)
                            nc.scalar.activation(hid(c, var), g_ps[c][:], ACT.Silu).then_inc(silu_done, 1)

                        def hi(var):
                            act.wait_ge(hid_done, START + 3 * step + var + 1 + 3)
                            nc.scalar.activation(hidS[c][:, var, HI, :], hid(c, var), ACT.Copy).then_inc(hid_hi, 1)

                        act.wait_ge(hid_split, START + 3 * step)
                        silu(0)
                        if not last:
                            prep(h, f + 1, 1 - s, 2 * c)
                        hi(0)
                        silu(1)
                        if not last:
                            prep(h, f + 1, 1 - s, 2 * c + 1)
                        hi(1)
                        silu(2)
                        hi(2)

                tiles(act, h, tile)
                copy_masks(h * 2 * HT + HT, 1)
                act.wait_ge(z_ready, h + 1)
                nc.scalar.activation(am[:, 0, 0, HI, :], down_acc[:, 0, :], ACT.Copy).then_inc(z_hi, 1)

        @block.gpsimd
        def _(pool):
            start_counts(pool, hid_split, am_split2)
            pool.sem_inc(hid_split, 3)
            with pool.Fori(0, HALVES) as h:
                for c in range(CH):
                    for i in range(2):
                        pool.wait_ge(am_.hi_done, 4 * (h * CH + c) + 2 * i + 2)
                        nc.gpsimd.tensor_tensor(am[:, i, 1, LO, c * S:(c + 1) * S], work[:, 2 * i + 1, :],
                                                fp32(am[:, i, 1, HI, c * S:(c + 1) * S]), ALU.subtract).then_inc(am_split2, 1)
                nc.gpsimd.memset(down_acc[:], 0.0).then_inc(acc_clear, 1)

                def tile(f, s, first, last):
                    for c in range(CH):
                        step = h * STEPS + f * CH + c
                        for var in range(3):
                            pool.wait_ge(hid_hi, 3 * step + var + 1)
                            nc.gpsimd.tensor_tensor(hidS[c][:, var, LO, :], hid(c, var), fp32(hidS[c][:, var, HI, :]),
                                                    ALU.subtract).then_inc(hid_split, 1)

                tiles(pool, h, tile)

        @block.vector
        def _(dve):
            start_counts(dve, xt_.split, c_.split, prep_.split, am_.split, logits_done, y_added, hid_done, z_added)
            def prep(h, f, s, part, bank=prep_ps):
                _, psum, (hi, lo) = prep_views(s, part, bank)
                split_lo(nc, dve, prep_, (h * NF + f) * PREP + part, lo, psum, hi)

            nc.vector.memset(rl[:], 0.0).then_inc(rl_clear, 1)
            dve.sem_inc(xt_.split, 1)
            dve.sem_inc(mask_copied, 1)
            dve.sem_inc(hid_done, 3)
            dve.sem_inc(y_added, 2)
            for i in range(E1):
                nc.vector.memset(rev[:, :, i:i + 1], float(E1 - i))
            token_var(nc, n)
            token_rstd(nc, dve, n)
            for job in range(CONST_JOBS):
                _, psum, (hi, lo) = const_views(job)
                split_lo(nc, dve, c_, job, lo, psum, hi)
            with dve.Fori(0, HALVES) as h:
                def copy_logits(c):
                    dve.wait_ge(logits_ready, h * CH + c + 1)
                    nc.vector.tensor_copy(logits[:, c * TPB:(c + 1) * TPB, :],
                                          u_ps[1][:].rearrange("p (k e) -> p k e", k=TPB)[:, :, 0:E1]).then_inc(logits_done, 1)

                for k in range(TPB):
                    normalise_tile(nc, n, x, h * HT + k, xn[:, k, :])
                for c in range(CH):
                    for k in range(TPB):
                        at = (c * TPB + k) * P
                        split_lo(nc, dve, xt_, (h * CH + c) * TPB + k, xnT[:, LO, :, at:at + P],
                                 (g_ps, u_ps)[k % 2][0][:].rearrange("p (k c) -> p k c", k=DK), xnT[:, HI, :, at:at + P])
                        if c + 1 < CH:
                            normalise_tile(nc, n, x, h * HT + (c + 1) * TPB + k, xn[:, k, :])
                    if c:
                        copy_logits(c - 1)
                for part in range(PREP):
                    prep(h, 0, 0, part, first_bank(part))
                copy_logits(CH - 1)
                nc.vector.drain()
                top_two(nc, dve, logits, rev, t)
                wide = lambda a: a[:].unsqueeze(2).to_broadcast([P, HT, E1])
                nc.vector.tensor_tensor(shifted[:], logits[:], wide(t.top1), ALU.subtract)
                nc.vector.tensor_tensor(t.gap[:], t.top2[:], t.top1[:], ALU.subtract)
                nc.vector.drain().then_inc(gap_ready, 1)
                dve.wait_ge(gap_exp, 2 * h + 2)
                nc.vector.reduce_sum(t.den[:], shifted[:], AXIS_X)
                nc.vector.drain()
                nc.vector.reciprocal(t.w1[:], t.den[:])
                nc.vector.drain()
                nc.vector.tensor_tensor(t.w2[:], t.e[:], t.w1[:], ALU.mult)
                nc.vector.tensor_copy(hots[:, :, 0, :], t.hot1[:])
                nc.vector.tensor_tensor(hots[:, :, 1, :], t.hot2[:], t.hot1[:], ALU.subtract)
                nc.vector.drain()
                nc.vector.tensor_tensor(hots[:, :, 2, :], t.hot1[:], wide(t.w1), ALU.mult)
                nc.vector.tensor_tensor(hots[:, :, 3, :], t.hot2[:], wide(t.w2), ALU.mult)
                nc.vector.drain()

                def make_masks(base):
                    for i in range(HT):
                        if i >= 2:
                            dve.wait_ge(mk_turned, base + i - 1)
                        nc.vector.tensor_copy(mk[i % 2].rearrange("p (e r) -> p e r", r=R1),
                                              hots[:, i].rearrange("p k e -> p (k e)").unsqueeze(2)
                                              .to_broadcast([P, 4 * E1, R1])).then_inc(mk_made, 1)

                make_masks(h * 2 * HT)
                for c in range(CH):
                    dve.wait_ge(mask_copied, START + h * 2 * HT + (c + 1) * TPB + 1)
                    dve.wait_ge(am_split2, START + 2 * (h * CH + c))
                    for i, src in enumerate(a_ps[c]):
                        dve.wait_ge(a_ready, 2 * (h * CH + c) + i + 1)
                        for k in range(2):
                            nc.vector.scalar_tensor_tensor(out=work[:, 2 * i + k, :], in0=src[:], scalar=SCALING1,
                                                           in1=maskT[:, k, c * S:(c + 1) * S], op0=ALU.mult,
                                                           op1=ALU.mult).then_inc(a_used, 1)
                    for i in range(2):
                        dve.wait_ge(am_.hi_done, 4 * (h * CH + c) + 2 * i + 1)
                        nc.vector.tensor_tensor(am[:, i, 0, LO, c * S:(c + 1) * S], work[:, 2 * i, :],
                                                fp32(am[:, i, 0, HI, c * S:(c + 1) * S]), ALU.subtract).then_inc(am_.split, 1)
                    dve.wait_ge(am_.split, START + 2 * (h * CH + c) + 2)
                dve.wait_ge(acc_clear, h + 1)

                def add_down(step, c, i):
                    dve.wait_ge(y_ready, step * USES + i + 1)
                    at = ds(h * HT + c * TPB + i, 1)
                    nc.vector.tensor_tensor(x[:, at, :], ring(c, i)[:].rearrange("p (a c) -> p a c", a=1), x[:, at, :],
                                            ALU.add).then_inc(y_added, 1)

                def add_down_lora(step, c, k):
                    dve.wait_ge(y_ready, step * USES + TPB + k + 1)
                    acc = down_acc[:, k, c * S:(c + 1) * S]
                    nc.vector.tensor_tensor(acc, ring(c, TPB + k)[:], acc, ALU.add).then_inc(y_added, 1)

                def tile(f, s, first, last):
                    for c in range(CH):
                        step = h * STEPS + f * CH + c
                        before = (step - 1, 1 - c)
                        has_before = not (first and c == 0)

                        def hidden(var):
                            dve.wait_ge(silu_done, 3 * step + var + 1)
                            dve.wait_ge(up_ready, 3 * step + var + 1)
                            nc.vector.tensor_tensor(hid(c, var), hid(c, var), u_ps[c][:], ALU.mult).then_inc(hid_done, 1)

                        if not last:
                            prep(h, f + 1, 1 - s, 2 * c)
                        hidden(0)
                        if has_before:
                            for i in range(TPB):
                                add_down(*before, i)
                        hidden(1)
                        if not last:
                            prep(h, f + 1, 1 - s, 2 * c + 1)
                        if has_before:
                            for k in range(2):
                                add_down_lora(*before, k)
                        hidden(2)

                tiles(dve, h, tile)
                end = (h * STEPS + STEPS - 1, CH - 1)
                for i in range(TPB):
                    add_down(*end, i)
                for k in range(2):
                    add_down_lora(*end, k)
                dve.wait_ge(hid_split, START + 3 * (h + 1) * STEPS + 3)
                make_masks(h * 2 * HT + HT)
                dve.wait_ge(mask_copied, START + h * 2 * HT + 2 * HT + 1)
                dve.wait_ge(y_added, START + (h + 1) * STEPS * USES + 2)
                nc.vector.tensor_tensor(down_acc[:, 0, :], down_acc[:, 0, :], maskT[:, 0, :], ALU.mult)
                nc.vector.tensor_tensor(down_acc[:, 1, :], down_acc[:, 1, :], maskT[:, 1, :], ALU.mult)
                nc.vector.drain()
                nc.vector.tensor_tensor(down_acc[:, 0, :], down_acc[:, 0, :], down_acc[:, 1, :], ALU.add).then_inc(z_ready, 1)
                dve.wait_ge(z_hi, h + 1)
                nc.vector.tensor_tensor(am[:, 0, 0, LO, :], down_acc[:, 0, :], fp32(am[:, 0, 0, HI, :]), ALU.subtract).then_inc(z_split, 1)
                for i in range(HT):
                    dve.wait_ge(z_out, h * HT + i + 1)
                    at = h * HT + i
                    nc.vector.scalar_tensor_tensor(out=x[:, ds(at, 1), :], in0=y_ps[i % 2][:].rearrange("p (a c) -> p a c", a=1),
                                                   scalar=SCALING1, in1=x[:, ds(at, 1), :], op0=ALU.mult, op1=ALU.add).then_inc(z_added, 1)
                dve.wait_ge(z_added, START + (h + 1) * HT)


def program(nc, io):
    with nc.sbuf_tensor("x_tokens", [P, TILES, D], FP32) as x, nc.sbuf_tensor("identity", [P, P], FP32) as ident, \
            nc.sbuf_tensor("token_stats", [P, TILES, 6], FP32) as stats:
        phase_attention0(nc, io, x, ident, stats)
        phase_moe0(nc, io, x, ident, stats)
        phase_rope1(nc, io, x, ident, stats)
        phase_ffn1(nc, io, x, ident, stats)


_INS = ["x", "ctx_1024", "fside_BxSx2_0", "L0_xattn_Wq", "L0_xattn_bq", "L0_xattn_Wk", "L0_xattn_bk",
        "L0_ffn_gate_w", "L0_ffn_gate_proj", "L0_ffn_up_proj", "L0_ffn_down_proj",
        "L1_xattn_Wq", "L1_xattn_Wkv", "L1_xattn_Wout", "L1_xattn_bout",
        "L1_ffn_Wg", "L1_ffn_Wu", "L1_ffn_Wd", "L1_ffn_Wr", "L1_ffn_Ag", "L1_ffn_Bg", "L1_ffn_Au", "L1_ffn_Bu",
        "L1_ffn_Ad", "L1_ffn_Bd"]
_OUT = ((4, 512, 512), "float32")


def kernel(**inputs):
    import numpy as _np
    import concourse.bacc as _bacc
    from concourse import mybir as _mybir
    from concourse.bass_utils import run_bass_kernel_spmd as _run

    nc = _bacc.Bacc("TRN2", target_bir_lowering=False, num_devices=1)
    arrays, io = {}, {}
    for name in _INS:
        a = _np.ascontiguousarray(inputs[name])
        arrays[f"in_{name}"] = a
        io[name] = nc.dram_tensor(f"in_{name}", a.shape, _mybir.dt.from_np(a.dtype), kind="ExternalInput").ap()
    shape, dtype = _OUT
    io["out"] = nc.dram_tensor("out_0", shape, _mybir.dt.from_np(_np.dtype(dtype)), kind="ExternalOutput").ap()
    program(nc, io)
    r = _run(nc, [arrays], core_ids=[0])
    return r.results[0]["out_0"]
```
